# Optimizing a Trainium2 kernel written in Bass

```python
import numpy as np
import jax
import jax.numpy as jnp

def _softmax(x, axis=-1):
    return jax.nn.softmax(x, axis=axis)

def _gelu(x):
    return jax.nn.gelu(x, approximate=True)

def _silu(x):
    return jax.nn.silu(x)

def _sigmoid(x):
    return jax.nn.sigmoid(x)

def _layernorm(x, axis=-1, eps=1e-05):
    m = jnp.mean(x, axis=axis, keepdims=True)
    v = jnp.var(x, axis=axis, keepdims=True)
    return (x - m) / jnp.sqrt(v + eps)

def _scatter_add(tgt, idx, src, axis=0):
    return tgt.at[idx].add(src)

def _segment_sum(src, seg, n):
    return jax.ops.segment_sum(src, seg, n)
kernel_name = 'mk_gps_d2_gnn_r8_136137'

def setup_inputs(seed: int=0):
    np.random.seed(seed)
    _w = jnp.asarray

    def _rec_inputs():
        import jax
        import jax.numpy as jnp
        _gk = jax.random.key(seed)
        x = -0.0003713 + 1 * jax.random.normal(jax.random.fold_in(_gk, 1), (6250, 256), jnp.float32)
        src = jax.random.randint(jax.random.fold_in(_gk, 2), (200000,), 0, 6250, jnp.int32)
        dst = jnp.minimum((6250 * jax.random.uniform(jax.random.fold_in(_gk, 3), (200000,)) ** 2.0).astype(jnp.int32), 49999)
        _o = jnp.argsort(dst, stable=True)
        src = src[_o]
        dst = dst[_o]
        edge_attr_128 = 9.41057e-06 + 1 * jax.random.normal(jax.random.fold_in(_gk, 11), (200000, 128), jnp.float32)
        node_vec1 = jax.random.uniform(jax.random.fold_in(_gk, 13), (6250, 1), jnp.float32, 0.0, 0.999973)
        node_vec1_n2 = jax.random.uniform(jax.random.fold_in(_gk, 14), (6250, 1), jnp.float32, 0.0, 0.999973)
        return (x, src, dst, edge_attr_128, node_vec1, node_vec1_n2)
    x, src, dst, edge_attr_128, node_vec1, node_vec1_n2 = _rec_inputs()

    def _L0_gnn_setup():
        import jax, jax.numpy as jnp
        import numpy as np
        NUM_NODES = 6250
        NUM_EDGES = 200000
        NODE_DIM = 256
        EDGE_DIM = 128
        MAX_IN_DEGREE = 512
        MAX_OUT_DEGREE = 512
        key = jax.random.key(seed)
        ks = jax.random.split(key, 12)
        x = jax.random.normal(ks[0], (NUM_NODES, NODE_DIM), dtype=jnp.float32)
        edge_index = jax.random.randint(ks[1], (2, NUM_EDGES), 0, NUM_NODES, dtype=jnp.int64 if jax.config.read('jax_enable_x64') else jnp.int32)
        edge_attr = jax.random.normal(ks[2], (NUM_EDGES, EDGE_DIM), dtype=jnp.float32)
        voronoi_values = jax.random.uniform(ks[3], (NUM_NODES, 1), dtype=jnp.float32)
        centralities = jax.random.uniform(ks[4], (NUM_NODES, 1), dtype=jnp.float32)
        z_in = jax.random.normal(ks[5], (MAX_IN_DEGREE, NODE_DIM), dtype=jnp.float32)
        z_out = jax.random.normal(ks[6], (MAX_OUT_DEGREE, NODE_DIM), dtype=jnp.float32)
        W_cent = jax.random.normal(ks[7], (1, NODE_DIM), dtype=jnp.float32) * 0.5
        b_cent = jnp.zeros((NODE_DIM,), dtype=jnp.float32)
        W_vor = jax.random.normal(ks[8], (1, NODE_DIM), dtype=jnp.float32) * 0.5
        b_vor = jnp.zeros((NODE_DIM,), dtype=jnp.float32)
        W_sum = jax.random.normal(ks[9], (EDGE_DIM, NODE_DIM), dtype=jnp.float32) * (1.0 / np.sqrt(EDGE_DIM))
        b_sum = jnp.zeros((NODE_DIM,), dtype=jnp.float32)
        return {'x': x, 'edge_index': edge_index, 'edge_attr': edge_attr, 'voronoi_values': voronoi_values, 'centralities': centralities, 'z_in': z_in, 'z_out': z_out, 'W_cent': W_cent, 'b_cent': b_cent, 'W_vor': W_vor, 'b_vor': b_vor, 'W_sum': W_sum, 'b_sum': b_sum}
    _L0_gnn_all = _L0_gnn_setup()
    _L0_gnn_in = {k: v for k, v in _L0_gnn_all.items() if k in ('z_in', 'z_out', 'W_cent', 'b_cent', 'W_vor', 'b_vor', 'W_sum', 'b_sum')}
    del _L0_gnn_all

    def _L0_mix_setup():
        import jax, jax.numpy as jnp
        import numpy as np
        HEADS = 8
        DIM_HEAD = 32
        SCALE = DIM_HEAD ** (-0.5)
        EPS = 1e-05

        def _layernorm_gamma(x, gamma):
            mu = jnp.mean(x, axis=-1, keepdims=True)
            var = jnp.var(x, axis=-1, keepdims=True)
            return (x - mu) * jax.lax.rsqrt(var + EPS) * gamma
        key = jax.random.key(seed)
        k1, k2, k3 = jax.random.split(key, 3)
        B, N, D = (8, 2048, 256)
        hidden = HEADS * DIM_HEAD
        x = jax.random.normal(k1, (B, N, D), dtype=jnp.float32)
        Wqkv = jax.random.normal(k2, (D, 3 * hidden), dtype=jnp.float32) * D ** (-0.5)
        Wout = jax.random.normal(k3, (hidden, D), dtype=jnp.float32) * hidden ** (-0.5)
        gamma = jnp.ones((D,), dtype=jnp.float32)
        return {'x': x, 'Wqkv': Wqkv, 'Wout': Wout, 'gamma': gamma}
    _L0_mix_all = _L0_mix_setup()
    _L0_mix_in = {k: v for k, v in _L0_mix_all.items() if k in ('Wqkv', 'Wout', 'gamma')}
    del _L0_mix_all

    def _L0_ffn_setup():
        import jax, jax.numpy as jnp
        import numpy as np
        B, S, D = (8, 512, 256)
        H = 4 * D
        CAPACITY = 0.5
        key = jax.random.key(seed)
        ks = jax.random.split(key, 6)
        x = jax.random.normal(ks[0], (B, S, D), dtype=jnp.float32)
        attention_mask = jnp.zeros((B, 1, 1, S), dtype=jnp.float32)
        wr = jax.random.normal(ks[1], (D, 1), dtype=jnp.float32) * 0.02
        br = jnp.zeros((1,), dtype=jnp.float32)
        w1 = jax.random.normal(ks[2], (D, H), dtype=jnp.float32) * 0.02
        b1 = jnp.zeros((H,), dtype=jnp.float32)
        w2 = jax.random.normal(ks[3], (H, D), dtype=jnp.float32) * 0.02
        b2 = jnp.zeros((D,), dtype=jnp.float32)
        return {'x': x, 'attention_mask': attention_mask, 'wr': wr, 'br': br, 'w1': w1, 'b1': b1, 'w2': w2, 'b2': b2}
    _L0_ffn_all = _L0_ffn_setup()
    _L0_ffn_in = {k: v for k, v in _L0_ffn_all.items() if k in ('attention_mask', 'wr', 'br', 'w1', 'b1', 'w2', 'b2')}
    del _L0_ffn_all

    def _L1_gnn_setup():
        import jax, jax.numpy as jnp
        import numpy as np
        N_NODES = 6250
        N_EDGES = 100000
        D_IN = 256
        D_OUT = 256
        BN_EPS = 1e-05
        L2_EPS = 1e-12
        key = jax.random.key(seed)
        ks = jax.random.split(key, 8)
        x = jax.random.normal(ks[0], (N_NODES, D_IN), dtype=jnp.float32)
        edge_index = jax.random.randint(ks[1], (2, N_EDGES), 0, N_NODES, dtype=jnp.int64)
        s = 1.0 / np.sqrt(D_IN)
        W_l = jax.random.uniform(ks[2], (D_OUT, D_IN), jnp.float32, -s, s)
        b_l = jax.random.uniform(ks[3], (D_OUT,), jnp.float32, -s, s)
        W_r = jax.random.uniform(ks[4], (D_OUT, D_IN), jnp.float32, -s, s)
        gamma = jnp.ones((D_OUT,), jnp.float32)
        beta = jnp.zeros((D_OUT,), jnp.float32)
        return {'x': x, 'edge_index': edge_index, 'W_l': W_l, 'b_l': b_l, 'W_r': W_r, 'gamma': gamma, 'beta': beta}
    _L1_gnn_all = _L1_gnn_setup()
    _L1_gnn_in = {k: v for k, v in _L1_gnn_all.items() if k in ('W_l', 'b_l', 'W_r', 'gamma', 'beta')}
    del _L1_gnn_all

    def _L1_mix_setup():
        import jax, jax.numpy as jnp
        import numpy as np
        MIDC = 256
        HEADS = 8
        HEADC = MIDC // HEADS
        EPS = 1e-05

        def _ln(x, gamma, beta):
            mu = jnp.mean(x, axis=-1, keepdims=True)
            var = jnp.var(x, axis=-1, keepdims=True)
            return (x - mu) * jax.lax.rsqrt(var + EPS) * gamma + beta
        key = jax.random.key(seed)
        ks = jax.random.split(key, 8)
        B, HW, C = (8, 512, MIDC)
        s = 1.0 / np.sqrt(C)
        return {'x': jax.random.normal(ks[0], (B, HW, C), jnp.float32), 'w_qkv': jax.random.normal(ks[1], (C, 3 * C), jnp.float32) * s, 'b_qkv': jnp.zeros((3 * C,), jnp.float32), 'kln_g': jnp.ones((HEADC,), jnp.float32), 'kln_b': jnp.zeros((HEADC,), jnp.float32), 'vln_g': jnp.ones((HEADC,), jnp.float32), 'vln_b': jnp.zeros((HEADC,), jnp.float32), 'w1': jax.random.normal(ks[2], (C, C), jnp.float32) * s, 'b1': jnp.zeros((C,), jnp.float32), 'w2': jax.random.normal(ks[3], (C, C), jnp.float32) * s, 'b2': jnp.zeros((C,), jnp.float32)}
    _L1_mix_all = _L1_mix_setup()
    _L1_mix_in = {k: v for k, v in _L1_mix_all.items() if k in ('w_qkv', 'b_qkv', 'kln_g', 'kln_b', 'vln_g', 'vln_b', 'w1', 'b1', 'w2', 'b2')}
    del _L1_mix_all

    def _L1_ffn_setup():
        import jax, jax.numpy as jnp
        import numpy as np
        E = 8
        K = 2
        D = 256
        H = 512
        DOUT = 256
        EPS = 1e-05
        key = jax.random.key(seed)
        ks = jax.random.split(key, 9)
        s = 0.02
        return {'x': jax.random.normal(ks[0], (4, 1024, D), jnp.float32), 'gamma': 1.0 + 0.05 * jax.random.normal(ks[1], (D,), jnp.float32), 'beta': 0.05 * jax.random.normal(ks[2], (D,), jnp.float32), 'Wr': 0.01 * jax.random.normal(ks[3], (D, E), jnp.float32), 'br': jnp.zeros((E,), jnp.float32), 'W1': s * jax.random.normal(ks[4], (E, D, H), jnp.float32), 'b1': s * jax.random.normal(ks[5], (E, H), jnp.float32), 'W2': s * jax.random.normal(ks[6], (E, H, DOUT), jnp.float32), 'b2': s * jax.random.normal(ks[7], (E, DOUT), jnp.float32)}
    _L1_ffn_all = _L1_ffn_setup()
    _L1_ffn_in = {k: v for k, v in _L1_ffn_all.items() if k in ('gamma', 'beta', 'Wr', 'br', 'W1', 'b1', 'W2', 'b2')}
    del _L1_ffn_all
    return {'x': x, 'src': src, 'dst': dst, 'edge_attr_128': edge_attr_128, 'node_vec1': node_vec1, 'node_vec1_n2': node_vec1_n2, 'L0_gnn_z_in': _L0_gnn_in['z_in'], 'L0_gnn_z_out': _L0_gnn_in['z_out'], 'L0_gnn_W_cent': _L0_gnn_in['W_cent'], 'L0_gnn_b_cent': _L0_gnn_in['b_cent'], 'L0_gnn_W_vor': _L0_gnn_in['W_vor'], 'L0_gnn_b_vor': _L0_gnn_in['b_vor'], 'L0_gnn_W_sum': _L0_gnn_in['W_sum'], 'L0_gnn_b_sum': _L0_gnn_in['b_sum'], 'L0_mix_Wqkv': _L0_mix_in['Wqkv'], 'L0_mix_Wout': _L0_mix_in['Wout'], 'L0_mix_gamma': _L0_mix_in['gamma'], 'L0_ffn_attention_mask': _L0_ffn_in['attention_mask'], 'L0_ffn_wr': _L0_ffn_in['wr'], 'L0_ffn_br': _L0_ffn_in['br'], 'L0_ffn_w1': _L0_ffn_in['w1'], 'L0_ffn_b1': _L0_ffn_in['b1'], 'L0_ffn_w2': _L0_ffn_in['w2'], 'L0_ffn_b2': _L0_ffn_in['b2'], 'L1_gnn_W_l': _L1_gnn_in['W_l'], 'L1_gnn_b_l': _L1_gnn_in['b_l'], 'L1_gnn_W_r': _L1_gnn_in['W_r'], 'L1_gnn_gamma': _L1_gnn_in['gamma'], 'L1_gnn_beta': _L1_gnn_in['beta'], 'L1_mix_w_qkv': _L1_mix_in['w_qkv'], 'L1_mix_b_qkv': _L1_mix_in['b_qkv'], 'L1_mix_kln_g': _L1_mix_in['kln_g'], 'L1_mix_kln_b': _L1_mix_in['kln_b'], 'L1_mix_vln_g': _L1_mix_in['vln_g'], 'L1_mix_vln_b': _L1_mix_in['vln_b'], 'L1_mix_w1': _L1_mix_in['w1'], 'L1_mix_b1': _L1_mix_in['b1'], 'L1_mix_w2': _L1_mix_in['w2'], 'L1_mix_b2': _L1_mix_in['b2'], 'L1_ffn_gamma': _L1_ffn_in['gamma'], 'L1_ffn_beta': _L1_ffn_in['beta'], 'L1_ffn_Wr': _L1_ffn_in['Wr'], 'L1_ffn_br': _L1_ffn_in['br'], 'L1_ffn_W1': _L1_ffn_in['W1'], 'L1_ffn_b1': _L1_ffn_in['b1'], 'L1_ffn_W2': _L1_ffn_in['W2'], 'L1_ffn_b2': _L1_ffn_in['b2']}

def reference(x, src, dst, edge_attr_128, node_vec1, node_vec1_n2, L0_gnn_z_in, L0_gnn_z_out, L0_gnn_W_cent, L0_gnn_b_cent, L0_gnn_W_vor, L0_gnn_b_vor, L0_gnn_W_sum, L0_gnn_b_sum, L0_mix_Wqkv, L0_mix_Wout, L0_mix_gamma, L0_ffn_attention_mask, L0_ffn_wr, L0_ffn_br, L0_ffn_w1, L0_ffn_b1, L0_ffn_w2, L0_ffn_b2, L1_gnn_W_l, L1_gnn_b_l, L1_gnn_W_r, L1_gnn_gamma, L1_gnn_beta, L1_mix_w_qkv, L1_mix_b_qkv, L1_mix_kln_g, L1_mix_kln_b, L1_mix_vln_g, L1_mix_vln_b, L1_mix_w1, L1_mix_b1, L1_mix_w2, L1_mix_b2, L1_ffn_gamma, L1_ffn_beta, L1_ffn_Wr, L1_ffn_br, L1_ffn_W1, L1_ffn_b1, L1_ffn_W2, L1_ffn_b2):
    import jax
    import jax.numpy as jnp

    def _L0_gnn_ref(x, edge_index, edge_attr, voronoi_values, centralities, z_in, z_out, W_cent, b_cent, W_vor, b_vor, W_sum, b_sum):
        import jax, jax.numpy as jnp
        import numpy as np
        NUM_NODES = 6250
        NUM_EDGES = 200000
        NODE_DIM = 256
        EDGE_DIM = 128
        MAX_IN_DEGREE = 512
        MAX_OUT_DEGREE = 512
        num_nodes = x.shape[0]
        src = edge_index[0]
        dst = edge_index[1]
        ones = jnp.ones_like(src, dtype=jnp.int32)
        in_deg = jnp.minimum(jax.ops.segment_sum(ones, dst, num_segments=num_nodes), MAX_IN_DEGREE - 1)
        out_deg = jnp.minimum(jax.ops.segment_sum(ones, src, num_segments=num_nodes), MAX_OUT_DEGREE - 1)
        edge_proj = edge_attr @ W_sum + b_sum
        sum3d = jax.ops.segment_sum(edge_proj, src, num_segments=num_nodes)
        cent_term = jax.nn.sigmoid(centralities @ W_cent + b_cent)
        vor_term = jax.nn.sigmoid(voronoi_values @ W_vor + b_vor)
        return x + z_in[in_deg] + z_out[out_deg] + cent_term + vor_term + sum3d

    def _L0_mix_ref(x, Wqkv, Wout, gamma):
        import jax, jax.numpy as jnp
        import numpy as np
        HEADS = 8
        DIM_HEAD = 32
        SCALE = DIM_HEAD ** (-0.5)
        EPS = 1e-05

        def _layernorm_gamma(x, gamma):
            mu = jnp.mean(x, axis=-1, keepdims=True)
            var = jnp.var(x, axis=-1, keepdims=True)
            return (x - mu) * jax.lax.rsqrt(var + EPS) * gamma
        B, N, D = x.shape
        qkv = x @ Wqkv
        q, k, v = jnp.split(qkv, 3, axis=-1)

        def to_heads(t):
            return t.reshape(B, N, HEADS, DIM_HEAD).transpose(0, 2, 1, 3)
        q, k, v = map(to_heads, (q, k, v))
        q = jax.nn.softmax(q, axis=-1) * SCALE
        k = jax.nn.softmax(k, axis=2)
        context = jnp.einsum('bhnd,bhne->bhde', k, v)
        out = jnp.einsum('bhde,bhnd->bhne', context, q)
        out = out.transpose(0, 2, 1, 3).reshape(B, N, HEADS * DIM_HEAD)
        out = out @ Wout
        return _layernorm_gamma(out, gamma)

    def _L0_ffn_ref(x, attention_mask, wr, br, w1, b1, w2, b2):
        import jax, jax.numpy as jnp
        import numpy as np
        B, S, D = (8, 512, 256)
        H = 4 * D
        CAPACITY = 0.5
        b, s, d = x.shape
        weights = (jnp.einsum('bsd,do->bso', x, wr) + br)[..., 0]
        k = max(1, int(CAPACITY * s))
        kk = k - 1 if k > 1 else 1
        _, idx = jax.lax.top_k(weights, k)
        sel_idx = idx[:, :kk]
        sel = jnp.take_along_axis(x, sel_idx[:, :, None], axis=1)
        h = jax.nn.gelu(jnp.einsum('bkd,dh->bkh', sel, w1) + b1)
        y = jnp.einsum('bkh,hd->bkd', h, w2) + b2
        w_sel = jnp.take_along_axis(weights, sel_idx, axis=1)
        y = y * w_sel[..., None]
        batch_idx = jnp.arange(b)[:, None]
        processed = jnp.zeros_like(x).at[batch_idx, sel_idx].set(y)
        return processed + x

    def _L1_gnn_ref(x, edge_index, W_l, b_l, W_r, gamma, beta):
        import jax, jax.numpy as jnp
        import numpy as np
        N_NODES = 6250
        N_EDGES = 100000
        D_IN = 256
        D_OUT = 256
        BN_EPS = 1e-05
        L2_EPS = 1e-12
        N = x.shape[0]
        src = edge_index[0]
        dst = edge_index[1]
        agg = jax.ops.segment_sum(x[src], dst, num_segments=N)
        deg = jax.ops.segment_sum(jnp.ones_like(src, dtype=x.dtype), dst, num_segments=N)
        mean = agg / jnp.maximum(deg, 1.0)[:, None]
        out = mean @ W_l.T + b_l + x @ W_r.T
        nrm = jnp.sqrt(jnp.sum(out * out, axis=-1, keepdims=True))
        out = out / jnp.maximum(nrm, L2_EPS)
        mu = jnp.mean(out, axis=0)
        var = jnp.mean((out - mu) ** 2, axis=0)
        out = (out - mu) / jnp.sqrt(var + BN_EPS) * gamma + beta
        return jax.nn.relu(out)

    def _L1_mix_ref(x, w_qkv, b_qkv, kln_g, kln_b, vln_g, vln_b, w1, b1, w2, b2):
        import jax, jax.numpy as jnp
        import numpy as np
        MIDC = 256
        HEADS = 8
        HEADC = MIDC // HEADS
        EPS = 1e-05

        def _ln(x, gamma, beta):
            mu = jnp.mean(x, axis=-1, keepdims=True)
            var = jnp.var(x, axis=-1, keepdims=True)
            return (x - mu) * jax.lax.rsqrt(var + EPS) * gamma + beta
        B, HW, C = x.shape
        bias = x
        qkv = (x @ w_qkv + b_qkv).reshape(B, HW, HEADS, 3 * HEADC)
        qkv = qkv.transpose(0, 2, 1, 3)
        q, k, v = jnp.split(qkv, 3, axis=-1)
        k = _ln(k, kln_g, kln_b)
        v = _ln(v, vln_g, vln_b)
        kv = jnp.einsum('bhnd,bhne->bhde', k, v) / HW
        out = jnp.einsum('bhnd,bhde->bhne', q, kv)
        out = out.transpose(0, 2, 1, 3).reshape(B, HW, C)
        ret = out + bias
        h = jax.nn.gelu(ret @ w1 + b1, approximate=False)
        return h @ w2 + b2 + bias

    def _L1_ffn_ref(x, gamma, beta, Wr, br, W1, b1, W2, b2):
        import jax, jax.numpy as jnp
        import numpy as np
        E = 8
        K = 2
        D = 256
        H = 512
        DOUT = 256
        EPS = 1e-05
        mu = jnp.mean(x, axis=-1, keepdims=True)
        var = jnp.mean(jnp.square(x - mu), axis=-1, keepdims=True)
        xn = (x - mu) * jax.lax.rsqrt(var + EPS) * gamma + beta
        logits = jnp.einsum('bsd,de->bse', xn, Wr) + br
        top_vals, top_idx = jax.lax.top_k(logits, K)
        w = jax.nn.softmax(top_vals, axis=-1)
        w_full = jnp.einsum('bsk,bske->bse', w, jax.nn.one_hot(top_idx, E, dtype=w.dtype))
        y = jnp.zeros(x.shape[:-1] + (DOUT,), x.dtype)
        for e in range(E):
            h = jax.nn.gelu(jnp.einsum('bsd,dh->bsh', xn, W1[e]) + b1[e], approximate=False)
            y_e = jnp.einsum('bsh,hd->bsd', h, W2[e]) + b2[e]
            y = y + y_e * w_full[..., e, None]
        return y
    edge_index = jnp.stack([src, dst])
    xn = _layernorm(x, axis=-1)
    x = x + _L0_gnn_ref(xn, edge_index, edge_attr_128, node_vec1, node_vec1_n2, L0_gnn_z_in, L0_gnn_z_out, L0_gnn_W_cent, L0_gnn_b_cent, L0_gnn_W_vor, L0_gnn_b_vor, L0_gnn_W_sum, L0_gnn_b_sum) + _L0_mix_ref(xn[None], L0_mix_Wqkv, L0_mix_Wout, L0_mix_gamma)[0]
    x = x + _L0_ffn_ref(_layernorm(x, axis=-1)[None], L0_ffn_attention_mask, L0_ffn_wr, L0_ffn_br, L0_ffn_w1, L0_ffn_b1, L0_ffn_w2, L0_ffn_b2)[0]
    xn = _layernorm(x, axis=-1)
    x = x + _L1_gnn_ref(xn, edge_index, L1_gnn_W_l, L1_gnn_b_l, L1_gnn_W_r, L1_gnn_gamma, L1_gnn_beta) + _L1_mix_ref(xn[None], L1_mix_w_qkv, L1_mix_b_qkv, L1_mix_kln_g, L1_mix_kln_b, L1_mix_vln_g, L1_mix_vln_b, L1_mix_w1, L1_mix_b1, L1_mix_w2, L1_mix_b2)[0]
    x = x + _L1_ffn_ref(_layernorm(x, axis=-1)[None], L1_ffn_gamma, L1_ffn_beta, L1_ffn_Wr, L1_ffn_br, L1_ffn_W1, L1_ffn_b1, L1_ffn_W2, L1_ffn_b2)[0]
    return x

_drawn_inputs = setup_inputs


def setup_inputs(seed=0):
    import zlib

    import numpy as np

    out = dict(_drawn_inputs(seed))
    spreads = {'L0_gnn_b_cent': (0.0, 0.8),
     'L0_gnn_b_vor': (0.0, 0.8),
     'L0_gnn_b_sum': (0.0, 0.1),
     'L0_mix_gamma': (1.0, 0.6),
     'L0_ffn_b1': (0.0, 0.8),
     'L0_ffn_b2': (0.0, 0.8),
     'L1_gnn_gamma': (1.0, 0.6),
     'L1_gnn_beta': (0.0, 0.8),
     'L1_mix_b_qkv': (0.0, 0.1),
     'L1_mix_kln_g': (1.0, 0.6),
     'L1_mix_kln_b': (0.0, 0.478),
     'L1_mix_vln_g': (1.0, 0.6),
     'L1_mix_vln_b': (0.0, 0.353),
     'L1_mix_b1': (0.0, 0.8),
     'L1_mix_b2': (0.0, 0.737),
     'L1_ffn_br': (0.0, 0.8)}
    factors = {'node_vec1': 8.0,
     'node_vec1_n2': 8.0,
     'L0_gnn_W_cent': 5.395,
     'L0_gnn_W_vor': 5.729,
     'L0_ffn_wr': 8.0,
     'L0_ffn_w1': 8.0,
     'L0_ffn_w2': 8.0,
     'L1_gnn_W_l': 3.515,
     'L1_gnn_b_l': 200.0,
     'L1_ffn_gamma': 8.0,
     'L1_ffn_beta': 8.0,
     'L1_ffn_Wr': 8.0,
     'L1_ffn_W1': 8.0,
     'L1_ffn_b1': 64.0,
     'L1_ffn_W2': 8.0,
     'L1_ffn_b2': 173.673}
    for name, (base, spread) in spreads.items():
        noise = np.random.default_rng([zlib.crc32(name.encode()), seed]).standard_normal(out[name].shape)
        drawn = base * np.exp(spread * noise) if base else spread * noise
        out[name] = jnp.asarray(drawn.astype(out[name].dtype))
    for name, factor in factors.items():
        out[name] = (out[name] * factor).astype(out[name].dtype)
    return out
```

```python
from contextlib import ExitStack

import concourse.bass as bass
from concourse import mybir

F32 = mybir.dt.float32
BF16 = mybir.dt.bfloat16
I32 = mybir.dt.int32
U32 = mybir.dt.uint32
I16 = mybir.dt.int16
U16 = mybir.dt.uint16
ALU = mybir.AluOpType
ACT = mybir.ActivationFunctionType
AX = mybir.AxisListType.X

N, D, E, ED = 6250, 256, 200000, 128
P = 125
NT = N // P
EC = E // P
TS = 256
PAD_KEY = 99999
W1 = 512
W2 = 256
NW1 = (E + NT * (W1 - 1)) // W1
NW2 = -(-((E + NT * (W2 - 1)) // W2) // 4) * 4
MAGIC = 12582912.0
EPS = 1e-5
MAX_DEGREE = 512
TOPK = N // 2 - 1
HEADS, HD = 8, 32
FFN_H = 1024
EXPERTS, EXP_H = 8, 512


def at(eng, sem, value, passed):
    eng.wait_ge(sem, value)
    eng.sem_inc(passed)


class Chain:

    def __init__(self, eng, sem, passed):
        self.eng, self.sem, self.passed = eng, sem, passed
        self.base, self.k, self.i, self.per = 0, 0, None, 0

    def enter(self, i, per):
        self.i, self.per, self.k = i, per, 0

    def leave(self, times):
        assert self.k == self.per, (self.k, self.per)
        self.base += times * self.per
        self.i, self.k = None, 0

    def step(self, ins):
        ins.then_inc(self.sem, 1)
        self.k += 1
        if self.i is None:
            self.base += 1
            self.k = 0
            self.eng.wait_ge(self.sem, self.base)
        else:
            at(self.eng, self.sem, self.i * self.per + (self.base + self.k), self.passed)


def bcast_rows(ap, rows):
    return ap.rearrange("(a d) -> a d", a=1).to_broadcast([rows, ap.shape[0]])


def program(nc, a, out):
    top = ExitStack()
    uid, section = [0], []

    def sem(name):
        uid[0] += 1
        section.append(nc.alloc_semaphore(f"{name}_{uid[0]}"))
        return section[-1]

    def end_section():
        nc.clear_and_free_semaphores(section)
        nc.all_engine_barrier()
        section.clear()

    def sbuf(ctx, name, shape, dt=F32):
        return ctx.enter_context(nc.sbuf_tensor(name, shape, dt))

    def psum(ctx, name, banks):
        return ctx.enter_context(nc.psum_tensor(name, [128, banks, 512], F32))

    passed = {e: sem("passed_" + e) for e in ("dve", "act", "pe", "sp", "pool")}
    steps = {e: sem("steps_" + e) for e in ("dve", "act", "pool")}
    chains = {}

    def chain(kind, eng):
        if kind not in chains:
            chains[kind] = Chain(eng, steps[kind], passed[kind])
        chains[kind].eng = eng
        return chains[kind]

    rows_d = nc.dram_tensor("rows_by_src", (E + W1, ED + 1), F32, kind="Internal").ap()
    pairs_d = nc.dram_tensor("pairs_by_dst", (E + W2, 2), I32, kind="Internal").ap()
    xn2_d = nc.dram_tensor("xn2_rows", (N, D), F32, kind="Internal").ap()

    R = sbuf(top, "R", [P, NT * TS])
    XT = sbuf(top, "XT", [128, NT * TS])
    ident = sbuf(top, "ident", [128, 128])
    ones = sbuf(top, "ones", [128, 128])
    lower = sbuf(top, "lower", [128, 128])
    blockdiag = sbuf(top, "blockdiag", [128, 128])
    iota_f = sbuf(top, "iota_f", [128, 128])
    win1_b = sbuf(top, "win1_b", [1, NW1], I32)
    win1_s = sbuf(top, "win1_s", [1, NW1], I32)
    win2_b = sbuf(top, "win2_b", [1, NW2], I32)
    win2_s = sbuf(top, "win2_s", [1, NW2], I32)
    unsorted = sbuf(top, "unsorted", [1, 1], I32)
    deg_in = sbuf(top, "deg_in", [P, NT])
    mean = sbuf(top, "mean", [P, NT])
    rstd = sbuf(top, "rstd", [P, NT])
    stats = sbuf(top, "stats", [P, NT * 6])

    def Rt(t):
        return R[:, bass.ds(t * TS, D)]

    def row_stats_loop(dve, ch, read):
        with dve.Fori(0, NT // 2) as i:
            for u in range(2):
                ins = dve.bn_stats(stats[:, bass.ds((i * 2 + u) * 6, 6)], read(i * 2 + u))
            ins.then_inc(stats_done, 1)
        dve.wait_ge(stats_done, stats_target[0])

    stats_done = sem("stats_done")
    stats_target = [0]
    var_ready, sd_ready = sem("var_ready"), sem("sd_ready")
    ln_count = [0, 0]

    def finish_stats_dve(dve, ch):
        s6 = stats[:].rearrange("p (t s) -> p t s", s=6)
        ln_count[0] += 1
        ch.step(dve.tensor_tensor(mean[:], s6[:, :, 1], s6[:, :, 4], ALU.add))
        ch.step(dve.tensor_scalar(mean[:], mean[:], 0.5, None, ALU.mult))
        ch.step(dve.tensor_tensor(rstd[:], s6[:, :, 1], mean[:], ALU.subtract))
        ch.step(dve.tensor_tensor(rstd[:], rstd[:], rstd[:], ALU.mult))
        ch.step(dve.tensor_tensor(s6[:, :, 2], s6[:, :, 2], s6[:, :, 5], ALU.add))
        ch.step(dve.tensor_scalar(s6[:, :, 2], s6[:, :, 2], 1.0 / D, None, ALU.mult))
        ch.step(dve.tensor_tensor(rstd[:], rstd[:], s6[:, :, 2], ALU.add))
        dve.tensor_scalar(rstd[:], rstd[:], EPS, None, ALU.add).then_inc(var_ready, 1)
        dve.wait_ge(sd_ready, ln_count[0])
        ch.step(dve.reciprocal(rstd[:], rstd[:]))

    def finish_stats_act(act):
        ln_count[1] += 1
        act.wait_ge(var_ready, ln_count[1])
        act.activation(rstd[:], rstd[:], ACT.Sqrt).then_inc(sd_ready, 1)

    def layer_stats(dve, ch, read):
        stats_target[0] += NT // 2
        row_stats_loop(dve, ch, read)
        finish_stats_dve(dve, ch)

    def rank_edges(dve, ch, hi, before, mask, rank, pos_f, pos):
        with dve.Fori(0, NT // 2) as i:
            ch.enter(i, 6)
            for u in range(2):
                b = i * 2 + u
                m = mask[:, u * EC:(u + 1) * EC]
                ch.step(dve.tensor_scalar(m, hi[:], iota_f[0:P, bass.ds(b, 1)], None, ALU.is_equal))
                ch.step(dve.tensor_tensor_scan(rank[:], m, m, before[:, bass.ds(b, 1)], ALU.add, ALU.bypass))
                ch.step(dve.copy_predicated(pos_f[:], m.bitcast(U16), rank[:]))
            ch.leave(NT // 2)
        ch.step(dve.tensor_copy(pos[:], pos_f[:]))

    section.clear()

    s01 = ExitStack()
    pair = sbuf(s01, "pair", [P, EC * 2], I32)
    pos_src = sbuf(s01, "pos_src", [P, EC], I32)
    first_dst = sbuf(s01, "first_dst", [P, NT])
    hi_src = sbuf(s01, "hi_src", [P, EC], BF16)
    lo_src = sbuf(s01, "lo_src", [P, EC], BF16)
    hi_dst = sbuf(s01, "hi_dst", [P, EC], BF16)
    lo_dst = sbuf(s01, "lo_dst", [P, EC], BF16)
    iota_b = sbuf(s01, "iota_b", [128, 128], BF16)

    with ExitStack() as ctx:
        src_i = sbuf(ctx, "src_i", [P, EC], I32)
        dst_i = sbuf(ctx, "dst_i", [P, EC], I32)
        src_f = XT[0:P, 0 * EC:1 * EC]
        dst_f = XT[0:P, 1 * EC:2 * EC]
        pos_f = XT[0:P, 2 * EC:3 * EC]
        rank = XT[0:P, 3 * EC:4 * EC]
        mask = sbuf(ctx, "mask", [P, 2 * EC], BF16)
        free_i = sbuf(ctx, "free_i", [128, 128], I32)
        part_i = sbuf(ctx, "part_i", [128, 1], I32)
        fblk_i = sbuf(ctx, "fblk_i", [128, 128], I32)
        pblk_i = sbuf(ctx, "pblk_i", [128, 1], I32)
        fblk_f = sbuf(ctx, "fblk_f", [128, 128])
        small = sbuf(ctx, "small", [128, 8])
        win_i = sbuf(ctx, "win_i", [128, NW2], I32)
        win_f = sbuf(ctx, "win_f", [128, NW2])
        cum = sbuf(ctx, "cum", [128, NW2])
        row = sbuf(ctx, "row", [1, NW2])
        cnt = sbuf(ctx, "cnt", [P, NT])
        tot = sbuf(ctx, "tot", [P, NT])
        first = sbuf(ctx, "first", [P, NT])
        first_src = sbuf(ctx, "first_src", [P, NT])
        col = sbuf(ctx, "col", [64, 8])
        col_i = sbuf(ctx, "col_i", [64, 2], I32)
        pad = sbuf(ctx, "pad", [128, 4 * (ED + 1)])
        pad_i = sbuf(ctx, "pad_i", [128, 2 * W2 // 128], I32)
        next_i = sbuf(ctx, "next_i", [P, 1], I32)
        next_f = sbuf(ctx, "next_f", [P, 1])
        falls = sbuf(ctx, "falls", [P, 2])
        ps = psum(ctx, "ps_sort", 4)

        ids_in, x_in, iotas, pads, consts = (sem(s) for s in ("ids_in", "x_in", "iotas", "pads", "consts"))
        falls_ready, falls_summed = sem("falls_ready"), sem("falls_summed")
        counted, summed, pads_set = sem("counted"), sem("summed"), sem("pads_set")
        block = ctx.enter_context(nc.Block())

        @block.sync
        def _(sp):
            sp.dma_start(src_i[:], a["src"].rearrange("(p c) -> p c", c=EC)).then_inc(ids_in, 16)
            sp.dma_start(dst_i[:], a["dst"].rearrange("(p c) -> p c", c=EC)).then_inc(ids_in, 16)
            dst2 = a["dst"].rearrange("(p c) -> p c", c=EC)
            sp.wait_ge(pads_set, 5)
            with nc.allow_non_contiguous_dma(reason="one number a partition"):
                sp.dma_start(next_i[0:P - 1, :], dst2[1:P, 0:1]).then_inc(ids_in, 16)
            sp.dma_start(R[:].rearrange("p (t d) -> p t d", d=TS),
                         a["x"].rearrange("(t p) d -> p t d", p=P)).then_inc(x_in, 16)
            sp.dma_start(rows_d[E:E + W1, :].rearrange("(p r) c -> p (r c)", p=128), pad[:]).then_inc(pads, 16)
            sp.dma_start(pairs_d[E:E + W2, :].rearrange("(p r) c -> p (r c)", p=128), pad_i[:]).then_inc(pads, 16)
            sp.wait_ge(pads, 32)
            sp.wait_ge(x_in, 16)

        @block.gpsimd
        def _(pool):
            pool.iota(free_i[:], pattern=[[1, 128]], base=0, channel_multiplier=0).then_inc(iotas, 1)
            pool.iota(part_i[:], pattern=[[0, 1]], base=0, channel_multiplier=1).then_inc(iotas, 1)
            pool.iota(fblk_i[:], pattern=[[1, 4], [0, 32]], base=0, channel_multiplier=0).then_inc(iotas, 1)
            pool.iota(win_i[:], pattern=[[1, NW2]], base=0, channel_multiplier=0).then_inc(iotas, 1)
            pool.memset(pad[:], 0.0).then_inc(pads_set, 1)
            pool.memset(pad_i[:], 0).then_inc(pads_set, 1)
            pool.memset(next_i[:], PAD_KEY).then_inc(pads_set, 1)
            pool.wait_ge(pads_set, 3)
            pool.memset(pad[:].rearrange("p (r c) -> p r c", c=ED + 1)[:, :, ED:], float(PAD_KEY)).then_inc(pads_set, 1)
            pool.memset(pad_i[:].rearrange("p (r c) -> p r c", c=2)[:, :, 1:], PAD_KEY).then_inc(pads_set, 1)
            pool.memset(ones[:], 1.0).then_inc(iotas, 1)

        def sort_dve(dve, ch, hi, pos, width, tab_b, tab_s, which, first2, rank_now):
            shift = width.bit_length() - 1
            nw = tab_b.shape[1]
            with dve.Fori(0, NT // 2) as i:
                ch.enter(i, 2)
                for u in range(2):
                    b = i * 2 + u
                    ch.step(dve.tensor_scalar(mask[:, u * EC:(u + 1) * EC], hi[:], iota_f[0:P, bass.ds(b, 1)], 0.0,
                                              ALU.is_equal, ALU.add, accum_out=cnt[:, bass.ds(b, 1)]))
                ch.leave(NT // 2)
            ch.step(dve.tensor_copy(tot[:], cnt[:]))
            dve.sem_inc(counted)
            dve.wait_ge(summed, 1 + 3 * which)
            ch.step(dve.tensor_copy(tot[:], ps[0:P, 0, 64:64 + NT]))
            ch.step(dve.tensor_tensor_scan(first[:], tot[:], tot[:], 0.0, ALU.add, ALU.bypass))
            ch.step(dve.tensor_tensor(first2[:], first[:], tot[:], ALU.subtract))
            ch.step(dve.tensor_tensor(first[:], first2[:], ps[0:P, 0, 0:NT], ALU.add))
            ch.step(dve.tensor_scalar(first2[:], first[:], -1.0, None, ALU.add))
            ch.step(dve.tensor_copy(col[0:NT, 0:1], ps[0:NT, 0, 128:129]))
            ch.step(dve.tensor_scalar(col_i[0:NT, 0:1], col[0:NT, 0:1], float(width - 1), None, ALU.add))
            ch.step(dve.tensor_scalar(col_i[0:NT, 1:2], col_i[0:NT, 0:1], shift, None, ALU.arith_shift_right))
            ch.step(dve.tensor_copy(col[0:NT, 1:2], col_i[0:NT, 1:2]))
            ch.step(dve.scalar_tensor_tensor(out=col[0:NT, 2:3], in0=col[0:NT, 1:2], scalar=-float(width),
                                             in1=col[0:NT, 0:1], op0=ALU.mult, op1=ALU.add))
            dve.sem_inc(counted)
            dve.wait_ge(summed, 2 + 3 * which)
            ch.step(dve.tensor_copy(col[0:NT, 3:4], ps[0:NT, 0, 129:130]))
            ch.step(dve.tensor_scalar(cum[0:NT, 0:nw], win_f[0:NT, 0:nw], col[0:NT, 3:4], None, ALU.is_ge))
            dve.sem_inc(counted)
            dve.wait_ge(summed, 3 + 3 * which)
            h = nw // 2
            for q in range(2):
                ch.step(dve.tensor_copy(tab_b[:, q * h:(q + 1) * h], ps[0:1, 1, 0:h] if q == 0 else ps[0:1, 2, 0:h]))
            for q, bank in ((0, 3), (1, 0)):
                ch.step(dve.scalar_tensor_tensor(out=row[:, q * h:(q + 1) * h], in0=win_f[0:1, q * h:(q + 1) * h],
                                                 scalar=float(width), in1=ps[0:1, bank, 0:h], op0=ALU.mult, op1=ALU.add))
            ch.step(dve.tensor_scalar(tab_s[:], row[:, 0:nw], float(E), None, ALU.min))
            if rank_now:
                rank_edges(dve, ch, hi, first2, mask, rank, pos_f, pos)

        @block.vector
        def _(dve):
            ch = chain("dve", dve)
            dve.wait_ge(iotas, 5)
            ch.step(dve.tensor_copy(iota_f[:], free_i[:]))
            ch.step(dve.tensor_copy(iota_b[:], free_i[:]))
            ch.step(dve.tensor_copy(small[:, 0:1], part_i[:]))
            ch.step(dve.tensor_scalar(ident[:], iota_f[:], small[:, 0:1], None, ALU.is_equal))
            ch.step(dve.tensor_scalar(lower[:], iota_f[:], small[:, 0:1], None, ALU.is_gt))
            ch.step(dve.tensor_scalar(pblk_i[:], part_i[:], 5, None, ALU.arith_shift_right))
            ch.step(dve.tensor_copy(small[:, 1:2], pblk_i[:]))
            ch.step(dve.tensor_copy(fblk_f[:], fblk_i[:]))
            ch.step(dve.tensor_scalar(blockdiag[:], fblk_f[:], small[:, 1:2], None, ALU.is_equal))
            ch.step(dve.tensor_copy(win_f[:], win_i[:]))
            ch.step(dve.memset(pos_f[:], 0.0))
            dve.wait_ge(ids_in, 48)
            for ids, keys, hi, lo, word in ((src_i, src_f, hi_src, lo_src, 0), (dst_i, dst_f, hi_dst, lo_dst, 1)):
                ch.step(dve.tensor_copy(keys[:], ids[:]))
                ch.step(dve.tensor_copy(pair[:].rearrange("p (c w) -> p c w", w=2)[:, :, word], ids[:]))
                ch.step(dve.tensor_scalar(rank[:], keys[:], -float(P // 2), 1.0 / P, ALU.add, ALU.mult))
                ch.step(dve.tensor_scalar(hi[:], rank[:], MAGIC, -MAGIC, ALU.add, ALU.add))
                ch.step(dve.scalar_tensor_tensor(out=lo[:], in0=hi[:], scalar=-float(P), in1=keys[:],
                                                 op0=ALU.mult, op1=ALU.add))
            ch.step(dve.tensor_tensor(rank[:, 0:EC - 1], dst_f[:, 0:EC - 1], dst_f[:, 1:EC], ALU.is_gt))
            ch.step(dve.tensor_reduce(falls[:, 0:1], rank[:, 0:EC - 1], AX.X, ALU.add))
            ch.step(dve.tensor_copy(next_f[:], next_i[:]))
            ch.step(dve.tensor_tensor(falls[:, 1:2], dst_f[:, EC - 1:EC], next_f[:], ALU.is_gt))
            ch.step(dve.tensor_tensor(falls[:, 0:1], falls[:, 0:1], falls[:, 1:2], ALU.add))
            dve.sem_inc(falls_ready)
            dve.wait_ge(falls_summed, 1)
            ch.step(dve.tensor_copy(unsorted[:], ps[0:1, 3, 0:1]))
            sort_dve(dve, ch, hi_src, pos_src, W1, win1_b, win1_s, 0, first_src, True)
            sort_dve(dve, ch, hi_dst, None, W2, win2_b, win2_s, 1, first_dst, False)

        @block.tensor
        def _(pe):
            pe.wait_ge(falls_ready, 1)
            pe.matmul(ps[0:1, 3, 0:1], falls[:, 0:1], ones[0:P, 0:1], start=True, stop=True).then_inc(falls_summed, 1)
            for which, nw in ((0, NW1), (1, NW2)):
                h = nw // 2
                pe.wait_ge(counted, 1 + 3 * which)
                pe.matmul(ps[0:P, 0, 0:NT], lower[0:P, 0:P], cnt[:], start=True, stop=True)
                pe.matmul(ps[0:P, 0, 64:64 + NT], ones[0:P, 0:P], cnt[:], start=True, stop=True)
                pe.matmul(ps[0:NT, 0, 128:129], cnt[:], ones[0:P, 0:1], start=True, stop=True).then_inc(summed, 1)
                pe.wait_ge(counted, 2 + 3 * which)
                pe.matmul(ps[0:NT, 0, 129:130], lower[0:NT, 0:NT], col[0:NT, 1:2], start=True, stop=False)
                pe.matmul(ps[0:NT, 0, 129:130], ident[0:NT, 0:NT], col[0:NT, 1:2], start=False, stop=True).then_inc(summed, 1)
                pe.wait_ge(counted, 3 + 3 * which)
                for q, bank in ((0, 1), (1, 2)):
                    pe.matmul(ps[0:1, bank, 0:h], ones[0:NT, 0:1], cum[0:NT, q * h:(q + 1) * h], start=True, stop=True)
                for q, bank in ((0, 3), (1, 0)):
                    mm = pe.matmul(ps[0:1, bank, 0:h], col[0:NT, 2:3], cum[0:NT, q * h:(q + 1) * h], start=True, stop=True)
                mm.then_inc(summed, 1)

    def tiles(eng, body, ch=None, per=0, n=NT):
        body(0, 0, 0)
        body(1, 1, 0)
        with eng.Fori(1, n // 2) as i:
            if ch:
                ch.base -= per
                ch.enter(i, per)
            body(2 * i, 0, i)
            body(2 * i + 1, 1, i)
        if ch:
            ch.base += per
            ch.leave(n // 2 - 1)

    def later(t):
        return not isinstance(t, int) or t >= 2

    def XTt(t, k):
        return XT[:, bass.ds(t * TS + k * P, P)]

    with ExitStack() as ctx:
        ring = sbuf(ctx, "ring", [P, 2 * 8 * (ED + 1)])
        stage = sbuf(ctx, "stage", [P, 2 * 8], I32)
        w_qkv = sbuf(ctx, "w_qkv", [128, 2 * 768])
        w_out = sbuf(ctx, "w_out", [128, 2 * D])
        w_mix = sbuf(ctx, "w_mix", [128, 2 * D])
        wcv = sbuf(ctx, "wcv", [P, 4 * D])
        nvec = sbuf(ctx, "nvec", [P, 2 * NT])
        b_sum = sbuf(ctx, "b_sum", [P, D])
        gamma = sbuf(ctx, "gamma", [P, D])
        lo1 = sbuf(ctx, "lo1", [P, 2 * 8 * P], BF16)
        hi1 = sbuf(ctx, "hi1", [P, 2 * 8 * NT], BF16)
        deg_out = sbuf(ctx, "deg_out", [P, NT])
        z_idx = sbuf(ctx, "z_idx", [P, NT * 2], I32)
        z_stage = sbuf(ctx, "z_stage", [P, 4], I32)
        z_rows = sbuf(ctx, "z_rows", [P, 2 * 2 * D])
        xn = sbuf(ctx, "xn", [P, 2 * D])
        xs = sbuf(ctx, "xs", [128, 2 * TS])
        cv = sbuf(ctx, "cv", [P, 2 * 2 * D])
        kmax_t = sbuf(ctx, "kmax_t", [128, NT * 2])
        kmax = sbuf(ctx, "kmax", [128, 2])
        neg_kmax = sbuf(ctx, "neg_kmax", [1, D])
        k_exp = sbuf(ctx, "k_exp", [P, 2 * D])
        v_one = sbuf(ctx, "v_one", [P, 2 * 2 * 129])
        q_sb = sbuf(ctx, "q_sb", [P, 2 * D])
        q_m = sbuf(ctx, "q_m", [P, 2 * HEADS])
        q_s = sbuf(ctx, "q_s", [P, 2 * HEADS])
        rsum = sbuf(ctx, "rsum", [128, 2])
        ctxn = sbuf(ctx, "ctxn", [128, 2 * 128])
        ctxt = sbuf(ctx, "ctxt", [128, 2 * 128])
        mixed = sbuf(ctx, "mixed", [P, 2 * D])
        pq = psum(ctx, "pq", 2)
        pkv = psum(ctx, "pkv", 2)
        ptr = psum(ctx, "ptr", 2)
        pctx = psum(ctx, "pctx", 1)
        phist = psum(ctx, "phist", 1)

        weights_in, mix_w_in, v_ones = sem("weights_in"), sem("mix_w_in"), sem("v_ones")
        ring_in = [sem("ring_in0"), sem("ring_in1")]
        ring_out = [sem("ring_out0"), sem("ring_out1")]
        onehot_ready, counted_to, degrees_ready = sem("onehot_ready"), sem("counted_to"), sem("degrees_ready")
        xn_ready, xt_ready, xt_stored = sem("xn_ready"), sem("xt_ready"), sem("xt_stored")
        cv_ready, sg_ready = sem("cv_ready"), sem("sg_ready")
        kt_ready, kt_read, kmax_ready, kmax_row, kmax_row_in = (sem(s) for s in ("kt_ready", "kt_read", "kmax_ready", "kmax_row", "kmax_row_in"))
        qkv_ready, kv_stored, qs_ready, qexp_ready, qn_ready, qt_ready, qt_stored, ctx_done = (
            sem(s) for s in ("qkv_ready", "kv_stored", "qs_ready", "qexp_ready", "qn_ready", "qt_ready", "qt_stored", "ctx_done"))
        xs_ready, qs2_ready = sem("xs_ready"), sem("qs2_ready")
        ctxn_ready, ctxt_ready, ctxt_in, wmix_ready, wmix_in = (sem(s) for s in ("ctxn_ready", "ctxt_ready", "ctxt_in", "wmix_ready", "wmix_in"))
        o_ready, o_read, o_stats = sem("o_ready"), sem("o_read"), sem("o_stats")
        z_in_ = [sem("z_in0"), sem("z_in1")]
        z_used = sem("z_used")
        block = ctx.enter_context(nc.Block())
        attr = a["edge_attr_128"].rearrange("(p c) d -> p c d", c=EC)
        ring4 = ring[:].rearrange("p (h c w) -> p h c w", h=2, c=8)
        pair_w = pair[:].rearrange("p (c w) -> p c w", w=2)

        @block.sync
        def _(sp):
            sp.dma_start(w_qkv[:].rearrange("p (k n) -> p k n", k=2), a["L0_mix_Wqkv"].rearrange("(k p) n -> p k n", p=128)).then_inc(mix_w_in, 16)
            sp.dma_start(w_out[:].rearrange("p (k n) -> p k n", k=2), a["L0_mix_Wout"].rearrange("(k p) n -> p k n", p=128)).then_inc(mix_w_in, 16)
            for j, name in enumerate(("W_cent", "b_cent", "W_vor", "b_vor")):
                v = a["L0_gnn_" + name]
                v = v.rearrange("a d -> (a d)") if len(v.shape) == 2 else v
                sp.dma_start(wcv[:, j * D:(j + 1) * D], bcast_rows(v, P)).then_inc(weights_in, 16)
            sp.dma_start(b_sum[:], bcast_rows(a["L0_gnn_b_sum"], P)).then_inc(weights_in, 16)
            sp.dma_start(gamma[:], bcast_rows(a["L0_mix_gamma"], P)).then_inc(weights_in, 16)
            with nc.allow_non_contiguous_dma(reason="one number a node"):
                for j, name in enumerate(("node_vec1_n2", "node_vec1")):
                    sp.dma_start(nvec[:, j * NT:(j + 1) * NT], a[name].rearrange("(t p) a -> p (t a)", p=P)).then_inc(weights_in, 16)

            def load(i):
                for h in range(2):
                    if not isinstance(i, int):
                        at(sp, ring_out[h], i * 128, passed["sp"])
                    sp.dma_start(ring4[:, h, :, 0:ED], attr[:, bass.ds(i * 16 + h * 8, 8), :]).then_inc(ring_in[h], 16)

            load(0)
            with sp.Fori(1, EC // 16) as i:
                load(i)

        @block.gpsimd
        def _(pool):
            ch = chain("pool", pool)
            pool.memset(v_one[:], 1.0).then_inc(v_ones, 1)

            def scatter_rows(i):
                for h in range(2):
                    c = i * 16 + h * 8
                    at(pool, ring_in[h], i * 16 + 16, passed["pool"])
                    ch.step(pool.tensor_copy(ring4[:, h, :, ED], pair_w[:, bass.ds(c, 8), 0]))
                    ch.step(pool.tensor_copy(stage[:, h * 8:h * 8 + 8], pos_src[:, bass.ds(c, 8)]))
                    for j in range(8):
                        pool.indirect_dma_start(rows_d, bass.IndirectOffsetOnAxis(ap=stage[:, h * 8 + j:h * 8 + j + 1].bitcast(U32), axis=0),
                                                ring4[:, h, j, :], None).then_inc(ring_out[h], 16)

            with pool.Fori(0, EC // 16) as i:
                ch.enter(i, 4)
                scatter_rows(i)
                ch.leave(EC // 16)
            for h in range(2):
                pool.wait_ge(ring_out[h], 128 * (EC // 16))

            pool.wait_ge(degrees_ready, 1)

            def gather_z(t, u, i):
                if later(t):
                    at(pool, z_used, t - 1, passed["pool"])
                ch.step(pool.tensor_copy(z_stage[:, 2 * u:2 * u + 2], z_idx[:, bass.ds(t * 2, 2)]))
                for k, name in enumerate(("L0_gnn_z_in", "L0_gnn_z_out")):
                    pool.indirect_dma_start(z_rows[:, (2 * u + k) * D:(2 * u + k + 1) * D], None, a[name],
                                            bass.IndirectOffsetOnAxis(ap=z_stage[:, 2 * u + k:2 * u + k + 1].bitcast(U32), axis=0)
                                            ).then_inc(z_in_[u], 16)

            tiles(pool, gather_z, ch, 2)

        @block.vector
        def _(dve):
            ch = chain("dve", dve)

            def onehots(lo, hi, which):
                def body(t, u, i):
                    if later(t) or which:
                        at(dve, counted_to, t - 1 + which * (EC // 8), passed["dve"])
                    dve.tensor_tensor(lo1[:, u * 8 * P:(u + 1) * 8 * P].rearrange("p (c n) -> p c n", c=8),
                                      iota_b[0:P, 0:P].unsqueeze(1).to_broadcast([P, 8, P]),
                                      lo[:, bass.ds(t * 8, 8)].unsqueeze(2).to_broadcast([P, 8, P]), ALU.is_equal)
                    dve.tensor_tensor(hi1[:, u * 8 * NT:(u + 1) * 8 * NT].rearrange("p (c n) -> p c n", c=8),
                                      iota_b[0:P, 0:NT].unsqueeze(1).to_broadcast([P, 8, NT]),
                                      hi[:, bass.ds(t * 8, 8)].unsqueeze(2).to_broadcast([P, 8, NT]), ALU.is_equal).then_inc(onehot_ready, 1)
                tiles(dve, body, n=EC // 8)

            onehots(lo_src, hi_src, 0)
            onehots(lo_dst, hi_dst, 1)
            dve.wait_ge(counted_to, 2 * (EC // 8))
            ch.step(dve.tensor_copy(deg_out[:], phist[0:P, 0, 0:NT]))
            ch.step(dve.tensor_copy(deg_in[:], phist[0:P, 0, 64:64 + NT]))
            z3 = z_idx[:].rearrange("p (t k) -> p t k", k=2)
            ch.step(dve.tensor_scalar(z3[:, :, 0], deg_in[:], float(MAX_DEGREE - 1), None, ALU.min))
            ch.step(dve.tensor_scalar(z3[:, :, 1], deg_out[:], float(MAX_DEGREE - 1), None, ALU.min))
            dve.sem_inc(degrees_ready)

            layer_stats(dve, ch, Rt)
            dve.wait_ge(weights_in, 128)

            def add_terms(t, u):
                at(dve, sg_ready, t + 1, passed["dve"])
                for k in range(2):
                    ch.step(dve.tensor_tensor(Rt(t), Rt(t), cv[:, (2 * u + k) * D:(2 * u + k + 1) * D], ALU.add))

            def norm(t, u, i):
                if later(t):
                    at(dve, xt_ready, t - 1, passed["dve"])
                    add_terms(t - 2, u)
                x_u = xn[:, u * D:(u + 1) * D]
                dve.tensor_scalar(x_u, Rt(t), mean[:, bass.ds(t, 1)], rstd[:, bass.ds(t, 1)], ALU.subtract, ALU.mult).then_inc(xn_ready, 1)
                at(dve, xn_ready, t + 1, passed["dve"])
                ch.step(dve.tensor_tensor(Rt(t), Rt(t), x_u, ALU.add))
                for k in range(2):
                    ins = dve.scalar_tensor_tensor(out=cv[:, (2 * u + k) * D:(2 * u + k + 1) * D], in0=wcv[:, 2 * k * D:(2 * k + 1) * D],
                                                   scalar=nvec[:, bass.ds(t + k * NT, 1)], in1=wcv[:, (2 * k + 1) * D:(2 * k + 2) * D],
                                                   op0=ALU.mult, op1=ALU.add)
                ins.then_inc(cv_ready, 1)

            tiles(dve, norm, ch, 6)
            add_terms(NT - 2, 0)
            add_terms(NT - 1, 1)

            def max_k(t, u, i):
                at(dve, kt_ready, t + 1, passed["dve"])
                dve.tensor_reduce(kmax_t[:, bass.ds(t * 2, 2)], pkv[:, u, 0:2 * P].rearrange("p (k n) -> p k n", k=2), AX.X, ALU.max).then_inc(kt_read, 1)

            tiles(dve, max_k)
            dve.wait_ge(kt_read, NT)
            dve.tensor_reduce(kmax[:], kmax_t[:].rearrange("p (t k) -> p k t", k=2), AX.X, ALU.max).then_inc(kmax_ready, 1)
            dve.wait_ge(kmax_row, 1)
            dve.tensor_scalar(neg_kmax[:], pctx[0:1, 0, 0:D], -1.0, None, ALU.mult).then_inc(kmax_row_in, 1)

            def q_softmax(t, u, i):
                at(dve, qkv_ready, t + 1, passed["dve"])
                q3 = pq[0:P, u, 0:D].rearrange("p (h d) -> p h d", h=HEADS)
                s3 = q_sb[:, u * D:(u + 1) * D].rearrange("p (h d) -> p h d", h=HEADS)
                qm, qs = q_m[:, u * HEADS:(u + 1) * HEADS], q_s[:, u * HEADS:(u + 1) * HEADS]
                ch.step(dve.tensor_reduce(qm, q3, AX.X, ALU.max))
                if later(t):
                    at(dve, qt_ready, t - 1, passed["dve"])
                dve.tensor_tensor(s3, q3, qm.unsqueeze(2).to_broadcast([P, HEADS, HD]), ALU.subtract).then_inc(qs_ready, 1)
                at(dve, qexp_ready, t + 1, passed["dve"])
                ch.step(dve.tensor_reduce(qs, s3, AX.X, ALU.add))
                ch.step(dve.reciprocal(qs, qs))
                dve.tensor_tensor(s3, s3, qs.unsqueeze(2).to_broadcast([P, HEADS, HD]), ALU.mult).then_inc(qn_ready, 1)

            tiles(dve, q_softmax, ch, 6)
            dve.wait_ge(ctx_done, NT)
            for m in range(2):
                ch.step(dve.reciprocal(rsum[:, m:m + 1], pctx[:, 0, 129 * m + 128:129 * m + 129]))
                ch.step(dve.tensor_scalar(ctxn[:, m * 128:(m + 1) * 128], pctx[:, 0, 129 * m:129 * m + 128], rsum[:, m:m + 1], None, ALU.mult))
                dve.tensor_tensor(ctxn[:, m * 128:(m + 1) * 128], ctxn[:, m * 128:(m + 1) * 128], blockdiag[:], ALU.mult).then_inc(ctxn_ready, 1)
            dve.wait_ge(ctxt_ready, 2)
            for m in range(2):
                dve.tensor_copy(ctxt[:, m * 128:(m + 1) * 128], ptr[:, m, 0:128]).then_inc(ctxt_in, 1)
            dve.wait_ge(wmix_ready, 2)
            for m in range(2):
                dve.tensor_scalar(w_mix[:, m * D:(m + 1) * D], pq[:, m, 0:D], float(HD) ** -0.5, None, ALU.mult).then_inc(wmix_in, 1)

            stats_target[0] += NT

            def out_stats(t, u, i):
                at(dve, o_read, t + 1, passed["dve"])
                dve.bn_stats(stats[:, bass.ds(t * 6, 6)], XT[0:P, bass.ds(t * TS, D)]).then_inc(stats_done, 1)

            tiles(dve, out_stats)
            dve.wait_ge(stats_done, stats_target[0])
            finish_stats_dve(dve, ch)

            def add_mix(t, u, i):
                m_u = mixed[:, u * D:(u + 1) * D]
                ch.step(dve.tensor_scalar(m_u, XT[0:P, bass.ds(t * TS, D)], mean[:, bass.ds(t, 1)], rstd[:, bass.ds(t, 1)], ALU.subtract, ALU.mult))
                ch.step(dve.tensor_tensor(m_u, m_u, gamma[:], ALU.mult))
                ch.step(dve.tensor_tensor(Rt(t), Rt(t), m_u, ALU.add))
                ch.step(dve.scalar_tensor_tensor(out=Rt(t), in0=b_sum[:], scalar=deg_out[:, bass.ds(t, 1)], in1=Rt(t), op0=ALU.mult, op1=ALU.add))
                at(dve, z_in_[u], i * 32 + 32, passed["dve"])
                for k in range(2):
                    ch.step(dve.tensor_tensor(Rt(t), Rt(t), z_rows[:, (2 * u + k) * D:(2 * u + k + 1) * D], ALU.add))
                dve.sem_inc(z_used)

            tiles(dve, add_mix, ch, 12)

        @block.scalar
        def _(act):
            finish_stats_act(act)

            def store_xt(t, u, i):
                at(act, cv_ready, t + 1, passed["act"])
                act.activation(cv[:, u * 2 * D:(u + 1) * 2 * D], cv[:, u * 2 * D:(u + 1) * 2 * D], ACT.Sigmoid).then_inc(sg_ready, 1)
                at(act, xt_ready, t + 1, passed["act"])
                act.copy(XT[:, bass.ds(t * TS, 2 * P)], ptr[:, u, 0:2 * P]).then_inc(xt_stored, 1)

            tiles(act, store_xt)
            act.wait_ge(v_ones, 1)

            def store_qt(t, u):
                at(act, qt_ready, t + 1, passed["act"])
                act.copy(XT[:, bass.ds(t * TS, 2 * P)], ptr[:, u, 0:2 * P]).then_inc(qt_stored, 1)

            def exps(t, u, i):
                if later(t):
                    at(act, qkv_ready, t - 1, passed["act"])
                act.copy(xs[:, u * TS:u * TS + 2 * P], XT[:, bass.ds(t * TS, 2 * P)]).then_inc(xs_ready, 1)
                at(act, qkv_ready, t + 1, passed["act"])
                if later(t):
                    at(act, ctx_done, t - 1, passed["act"])
                act.activation(k_exp[:, u * D:(u + 1) * D], pkv[0:P, u, 0:D], ACT.Exp).then_inc(kv_stored, 1)
                act.copy(v_one[:, u * 258:(u + 1) * 258].rearrange("p (m c) -> p m c", m=2)[:, :, 0:128],
                         pkv[0:P, u, D:2 * D].rearrange("p (m c) -> p m c", m=2)).then_inc(kv_stored, 1)
                at(act, qs_ready, t + 1, passed["act"])
                act.activation(q_sb[:, u * D:(u + 1) * D], q_sb[:, u * D:(u + 1) * D], ACT.Exp).then_inc(qexp_ready, 1)
                if not isinstance(t, int) or t >= 1:
                    store_qt(t - 1, 1 - u)

            tiles(act, exps)
            store_qt(NT - 1, 1)

            def store_out(t, u, i):
                if later(t):
                    at(act, o_ready, t - 1, passed["act"])
                act.copy(xs[:, u * TS:u * TS + 2 * P], XT[:, bass.ds(t * TS, 2 * P)]).then_inc(qs2_ready, 1)
                at(act, o_ready, t + 1, passed["act"])
                act.copy(XT[0:P, bass.ds(t * TS, D)], pq[0:P, u, 0:D]).then_inc(o_read, 1)

            tiles(act, store_out)
            finish_stats_act(act)

        @block.tensor
        def _(pe):
            def count(which):
                def body(t, u, i):
                    at(pe, onehot_ready, t + 1 + which * (EC // 8), passed["pe"])
                    for j in range(8):
                        mm = pe.matmul(phist[0:P, 0, which * 64:which * 64 + NT], lo1[:, (u * 8 + j) * P:(u * 8 + j + 1) * P],
                                       hi1[:, (u * 8 + j) * NT:(u * 8 + j + 1) * NT],
                                       start=(isinstance(t, int) and t == 0 and j == 0), stop=True, skip_group_check=True)
                    mm.then_inc(counted_to, 1)
                tiles(pe, body, n=EC // 8)

            count(0)
            count(1)

            def transpose_x(t, u, i):
                at(pe, xn_ready, t + 1, passed["pe"])
                if later(t):
                    at(pe, xt_stored, t - 1, passed["pe"])
                for k in range(2):
                    mm = pe.transpose(ptr[:, u, k * P:(k + 1) * P], xn[:, u * D + k * 128:u * D + (k + 1) * 128], ident[0:P, 0:P])
                mm.then_inc(xt_ready, 1)

            tiles(pe, transpose_x)
            pe.wait_ge(mix_w_in, 32)
            pe.wait_ge(xt_stored, NT)

            def k_transposed(t, u, i):
                if later(t):
                    at(pe, kt_read, t - 1, passed["pe"])
                for m in range(2):
                    for k in range(2):
                        mm = pe.matmul(pkv[:, u, m * P:(m + 1) * P], w_qkv[:, k * 768 + D + m * 128:k * 768 + D + (m + 1) * 128],
                                       XTt(t, k), start=(k == 0), stop=(k == 1))
                mm.then_inc(kt_ready, 1)

            tiles(pe, k_transposed)
            pe.wait_ge(kmax_ready, 1)
            for m in range(2):
                mm = pe.matmul(pctx[0:1, 0, m * 128:(m + 1) * 128], kmax[:, m:m + 1], ident[:], start=True, stop=True)
            mm.then_inc(kmax_row, 1)
            pe.wait_ge(kmax_row_in, 1)

            def context(t, u):
                at(pe, kv_stored, 2 * t + 2, passed["pe"])
                first = isinstance(t, int) and t == 0
                for m in range(2):
                    mm = pe.matmul(pctx[:, 0, m * 129:(m + 1) * 129], k_exp[:, u * D + m * 128:u * D + (m + 1) * 128],
                                   v_one[:, u * 258 + m * 129:u * 258 + (m + 1) * 129], start=first and m == 0, stop=True, skip_group_check=True)
                mm.then_inc(ctx_done, 1)
                at(pe, qn_ready, t + 1, passed["pe"])
                if later(t):
                    at(pe, qt_stored, t - 1, passed["pe"])
                for k in range(2):
                    mm = pe.transpose(ptr[:, u, k * P:(k + 1) * P], q_sb[:, u * D + k * 128:u * D + (k + 1) * 128], ident[0:P, 0:P])
                mm.then_inc(qt_ready, 1)

            def qkv(t, u, i):
                at(pe, xs_ready, t + 1, passed["pe"])
                if later(t):
                    at(pe, kv_stored, 2 * t - 2, passed["pe"])
                    at(pe, qs_ready, t - 1, passed["pe"])
                for k in range(2):
                    pe.matmul(pq[0:P, u, 0:D], xs[:, u * TS + k * P:u * TS + (k + 1) * P], w_qkv[:, k * 768:k * 768 + D], start=(k == 0), stop=(k == 1))
                for k in range(2):
                    pe.matmul(pkv[0:P, u, 0:D], xs[:, u * TS + k * P:u * TS + (k + 1) * P], w_qkv[:, k * 768 + D:k * 768 + 2 * D], start=(k == 0), stop=False)
                pe.matmul(pkv[0:P, u, 0:D], ones[0:1, 0:P], neg_kmax[:], start=False, stop=True)
                for k in range(2):
                    mm = pe.matmul(pkv[0:P, u, D:2 * D], xs[:, u * TS + k * P:u * TS + (k + 1) * P], w_qkv[:, k * 768 + 2 * D:k * 768 + 3 * D], start=(k == 0), stop=(k == 1))
                mm.then_inc(qkv_ready, 1)
                if not isinstance(t, int) or t >= 1:
                    context(t - 1, 1 - u)

            tiles(pe, qkv)
            context(NT - 1, 1)
            pe.wait_ge(ctxn_ready, 2)
            pe.wait_ge(qt_stored, NT)
            for m in range(2):
                pe.transpose(ptr[:, m, 0:128], ctxn[:, m * 128:(m + 1) * 128], ident[:]).then_inc(ctxt_ready, 1)
            pe.wait_ge(ctxt_in, 2)
            for m in range(2):
                pe.matmul(pq[:, m, 0:D], ctxt[:, m * 128:(m + 1) * 128], w_out[:, m * D:(m + 1) * D], start=True, stop=True).then_inc(wmix_ready, 1)
            pe.wait_ge(wmix_in, 2)

            def attend(t, u, i):
                at(pe, qs2_ready, t + 1, passed["pe"])
                if later(t):
                    at(pe, o_read, t - 1, passed["pe"])
                for k in range(2):
                    mm = pe.matmul(pq[0:P, u, 0:D], xs[:, u * TS + k * P:u * TS + (k + 1) * P], w_mix[:, k * D:(k + 1) * D], start=(k == 0), stop=(k == 1))
                mm.then_inc(o_ready, 1)

            tiles(pe, attend)

    with s01, ExitStack() as ctx:
        pos_dst = sbuf(ctx, "pos_dst", [P, EC], I32)
        mask = sbuf(ctx, "mask2", [P, 2 * EC], BF16)
        rank, pos_f = XT[0:P, 0:EC], XT[0:P, EC:2 * EC]
        stage = sbuf(ctx, "stage2", [P, 2 * 8], I32)
        pstage = sbuf(ctx, "pstage", [P, 2 * 16], I32)
        pair_out = [sem("pair_out0"), sem("pair_out1")]
        pairs_out, dst_ranked, rank_steps, stage_steps = (sem(s) for s in ("pairs_out", "dst_ranked", "rank_steps", "stage_steps"))
        block = ctx.enter_context(nc.Block())

        @block.sync
        def _(sp):
            falls = sp.value_load(unsorted[0:1, 0:1], min_val=0, max_val=E)
            with sp.If(falls == 0):
                sp.dma_start(pairs_d[0:E, :].rearrange("(p c) w -> p (c w)", p=P), pair[:]).then_inc(pairs_out, 16)
                sp.wait_ge(pairs_out, 16)

        @block.vector
        def _(dve):
            falls = dve.value_load(unsorted[0:1, 0:1], min_val=0, max_val=E)
            with dve.If(falls != 0):
                ch = Chain(dve, rank_steps, passed["dve"])
                ch.step(dve.memset(pos_f, 0.0))
                rank_edges(dve, ch, hi_dst, first_dst, mask, rank, pos_f, pos_dst)
                dve.sem_inc(dst_ranked)

        @block.gpsimd
        def _(pool):
            falls = pool.value_load(unsorted[0:1, 0:1], min_val=0, max_val=E)
            with pool.If(falls != 0):
                ch = Chain(pool, stage_steps, passed["pool"])
                pool.wait_ge(dst_ranked, 1)

                def scatter_pairs(i):
                    for h in range(2):
                        c = i * 16 + h * 8
                        if not isinstance(i, int):
                            at(pool, pair_out[h], i * 128, passed["pool"])
                        pool.tensor_copy(pstage[:, h * 16:h * 16 + 16], pair[:, bass.ds(c * 2, 16)])
                        ch.step(pool.tensor_copy(stage[:, h * 8:h * 8 + 8], pos_dst[:, bass.ds(c, 8)]))
                        for j in range(8):
                            pool.indirect_dma_start(pairs_d, bass.IndirectOffsetOnAxis(ap=stage[:, h * 8 + j:h * 8 + j + 1].bitcast(U32), axis=0),
                                                    pstage[:, h * 16 + 2 * j:h * 16 + 2 * j + 2], None).then_inc(pair_out[h], 16)

                scatter_pairs(0)
                with pool.Fori(1, EC // 16) as i:
                    ch.base -= 2
                    ch.enter(i, 2)
                    scatter_pairs(i)
                    ch.base += 2
                    ch.leave(EC // 16 - 1)
                for h in range(2):
                    pool.wait_ge(pair_out[h], 128 * (EC // 16))

    end_section()

    def fill_iota(pool, ids):
        return pool.iota(ids[:], pattern=[[1, (NT + 1) * P]], base=0, channel_multiplier=0, allow_small_or_imprecise_dtypes=True)

    with ExitStack() as ctx:
        U = 8
        ids = sbuf(ctx, "ids", [128, (NT + 1) * P], I16)
        acc = sbuf(ctx, "acc", [128, (NT + 1) * P])
        win = sbuf(ctx, "win", [128, U * 4 * (ED + 1)])
        hot = sbuf(ctx, "hot", [128, 2 * 4 * P])
        w_sum = sbuf(ctx, "w_sum", [128, D])
        acc_s = sbuf(ctx, "acc_s", [128, 2 * P])
        pw = psum(ctx, "pw", 4)
        py = psum(ctx, "py", 2)
        win_in = [sem(f"win_in{s}") for s in range(U)]
        accs_ready = sem("accs_ready")
        wsum_in, init2, hot_ready, win_summed, acc_done, y_ready, y_added = (
            sem(s) for s in ("wsum_in", "init2", "hot_ready", "win_summed", "acc_done", "y_ready", "y_added"))
        block = ctx.enter_context(nc.Block())

        @block.sync
        def _(sp):
            sp.dma_start(w_sum[:], a["L0_gnn_W_sum"]).then_inc(wsum_in, 16)

            def load(i):
                for s in range(U):
                    if not isinstance(i, int):
                        at(sp, win_summed, i * U + s + 1 - U, passed["sp"])
                    start = sp.value_load(win1_s[0:1, bass.ds(i * U + s, 1)], min_val=0, max_val=E)
                    sp.dma_start(win[:, s * 4 * (ED + 1):(s + 1) * 4 * (ED + 1)],
                                 rows_d[bass.ds(start, W1), :].rearrange("(p r) c -> p (r c)", p=128)).then_inc(win_in[s], 16)

            load(0)
            with sp.Fori(1, NW1 // U) as i:
                load(i)

        @block.gpsimd
        def _(pool):
            fill_iota(pool, ids).then_inc(init2, 1)
            pool.memset(acc[:], 0.0).then_inc(init2, 1)

        @block.vector
        def _(dve):
            ch = chain("dve", dve)
            dve.wait_ge(init2, 2)

            def windows(i):
                b = [dve.value_load(win1_b[0:1, bass.ds(i * U + s, 1)], min_val=0, max_val=NT) for s in range(U)]

                def add(s):
                    g = i * U + s
                    at(dve, win_summed, g + 1, passed["dve"])
                    if not isinstance(g, int) or g:
                        at(dve, acc_done, g, passed["dve"])
                    tile = acc[:, bass.ds(b[s] * P, P)]
                    dve.tensor_tensor(tile, tile, pw[:, s % 4, 0:P], ALU.add).then_inc(acc_done, 1)

                for s in range(U):
                    at(dve, win_in[s], i * 16 + 16, passed["dve"])
                    keys = win[:, s * 4 * (ED + 1):(s + 1) * 4 * (ED + 1)].rearrange("p (r c) -> p r c", r=4)[:, :, ED]
                    dve.tensor_tensor(hot[:, (s % 2) * 4 * P:(s % 2 + 1) * 4 * P].rearrange("p (r n) -> p r n", r=4),
                                      ids[:, bass.ds(b[s] * P, P)].unsqueeze(1).to_broadcast([128, 4, P]),
                                      keys.unsqueeze(2).to_broadcast([128, 4, P]), ALU.is_equal).then_inc(hot_ready, 1)
                    if s:
                        add(s - 1)
                add(U - 1)

            windows(0)
            with dve.Fori(1, NW1 // U) as i:
                windows(i)

            def add_sum(t, u, i):
                at(dve, y_ready, t + 1, passed["dve"])
                dve.tensor_tensor(Rt(t), Rt(t), py[0:P, u, 0:D], ALU.add).then_inc(y_added, 1)

            tiles(dve, add_sum)

        @block.scalar
        def _(act):
            act.wait_ge(acc_done, NW1)

            def stage_acc(t, u, i):
                if later(t):
                    at(act, y_ready, t - 1, passed["act"])
                act.copy(acc_s[:, u * P:(u + 1) * P], acc[:, bass.ds(t * P, P)]).then_inc(accs_ready, 1)

            tiles(act, stage_acc)

        @block.tensor
        def _(pe):
            def windows(i):
                for s in range(U):
                    g = i * U + s
                    at(pe, hot_ready, g + 1, passed["pe"])
                    at(pe, win_in[s], i * 16 + 16, passed["pe"])
                    if not isinstance(i, int) or s >= 4:
                        at(pe, acc_done, g - 3, passed["pe"])
                    for r in range(4):
                        mm = pe.matmul(pw[:, s % 4, 0:P], win[:, (s * 4 + r) * (ED + 1):(s * 4 + r) * (ED + 1) + ED],
                                       hot[:, ((s % 2) * 4 + r) * P:((s % 2) * 4 + r + 1) * P], start=(r == 0), stop=(r == 3))
                    mm.then_inc(win_summed, 1)

            windows(0)
            with pe.Fori(1, NW1 // U) as i:
                windows(i)
            pe.wait_ge(wsum_in, 16)

            def project(t, u, i):
                at(pe, accs_ready, t + 1, passed["pe"])
                if later(t):
                    at(pe, y_added, t - 1, passed["pe"])
                pe.matmul(py[0:P, u, 0:D], acc_s[:, u * P:(u + 1) * P], w_sum[:], start=True, stop=True).then_inc(y_ready, 1)

            tiles(pe, project)

    G, GC = NT // 2, 2 * P

    def groups(eng, body, ch=None, per=0):
        for g in range(3):
            body(g, g % 2)
        with eng.Fori(1, G // 2) as i:
            if ch:
                ch.base -= per
                ch.enter(i, per)
            body(2 * i + 1, 1)
            body(2 * i + 2, 0)
        if ch:
            ch.base += per
            ch.leave(G // 2 - 1)

    def XTg(g, k):
        return XT[:, bass.ds(g * 2 * TS, 2 * TS)].rearrange("p (t c) -> p t c", t=2)[:, :, k * P:(k + 1) * P]

    class Ffn:

        def __init__(self, ctx, name, nm):
            self.nm, self.uses = nm, {"pe": 0, "act": 0, "dve": 0}
            self.hT = sbuf(ctx, name + "_hT", [128, 2 * nm * GC])
            self.ph = psum(ctx, name + "_ph", 4)
            self.py = psum(ctx, name + "_py", 2)
            self.h_ready, self.h_stored, self.y_ready, self.y_added = (sem(name + s) for s in ("_h_ready", "_h_stored", "_y_ready", "_y_added"))

        def hidden(self, u, m):
            return self.hT[:, (u * self.nm + m) * GC:(u * self.nm + m + 1) * GC]

        def pe(self, pe, w1, w2):
            r, nm = self.uses["pe"], self.nm
            self.uses["pe"] += 1

            def second(g, u):
                at(pe, self.h_stored, (g + 1 + r * G) * nm, passed["pe"])
                for v in range(2):
                    if not isinstance(g, int) or g or r:
                        at(pe, self.y_added, 2 * (g + r * G) + v - 1, passed["pe"])
                    for m in range(nm):
                        mm = pe.matmul(self.py[0:P, v, 0:D], self.hidden(u, m)[:, v * P:(v + 1) * P], w2(m), start=(m == 0), stop=(m == nm - 1))
                    mm.then_inc(self.y_ready, 1)

            def body(g, u):
                for m in range(nm):
                    bank = m % 4 if nm >= 4 else 2 * u + m
                    if not isinstance(g, int) or r or g * nm + m >= 4:
                        at(pe, self.h_stored, (g + r * G) * nm + m - 3, passed["pe"])
                    for k in range(2):
                        mm = pe.matmul(self.ph[:, bank, 0:GC].rearrange("p (t c) -> p t c", t=2), w1(k, m), XTg(g, k), start=(k == 0), stop=(k == 1))
                    mm.then_inc(self.h_ready, 1)
                if not isinstance(g, int) or g:
                    second(g - 1, 1 - u)

            groups(pe, body)
            second(G - 1, 0)

        def act(self, act, func, bias):
            r, nm = self.uses["act"], self.nm
            self.uses["act"] += 1

            def body(g, u):
                if not isinstance(g, int) or g >= 2 or r:
                    at(act, self.y_ready, 2 * (g - 1 + r * G), passed["act"])
                for m in range(nm):
                    bank = m % 4 if nm >= 4 else 2 * u + m
                    at(act, self.h_ready, (g + r * G) * nm + m + 1, passed["act"])
                    act.activation(self.hidden(u, m), self.ph[:, bank, 0:GC], func, bias=bias(m)).then_inc(self.h_stored, 1)

            groups(act, body)

        def dve(self, dve, ch, per, body):
            r = self.uses["dve"]
            self.uses["dve"] += 1

            def both(g, u):
                for v in range(2):
                    at(dve, self.y_ready, 2 * (g + r * G) + v + 1, passed["dve"])
                    body(2 * g + v, self.py[0:P, v, 0:D])
                    dve.sem_inc(self.y_added)

            groups(dve, both, ch, per * 4)

    def load_cols(sp, dst, vec, n):
        with nc.allow_non_contiguous_dma(reason="a bias per partition"):
            return sp.dma_start(dst, vec.rearrange("(m p) -> p m", p=128))

    def load_rows(sp, dst, w):
        return sp.dma_start(dst.rearrange("p (k n) -> p k n", n=w.shape[1]), w.rearrange("(k p) n -> p k n", p=128))

    with ExitStack() as ctx:
        w1 = sbuf(ctx, "f_w1", [128, 2 * FFN_H])
        w2 = sbuf(ctx, "f_w2", [128, 8 * D])
        b1 = sbuf(ctx, "f_b1", [128, 8])
        b2 = sbuf(ctx, "f_b2", [P, D])
        wr = sbuf(ctx, "f_wr", [P, D])
        br = sbuf(ctx, "f_br", [P, 1])
        xn = sbuf(ctx, "f_xn", [P, 2 * D])
        prod = sbuf(ctx, "f_prod", [P, 2 * D])
        wt = sbuf(ctx, "f_wt", [P, NT])
        key_i = sbuf(ctx, "key_i", [P, 3 * NT], I32)
        key = sbuf(ctx, "key", [P, 3 * NT])
        hit = sbuf(ctx, "hit", [P, 3 * NT])
        sel = sbuf(ctx, "sel", [P, NT])
        cur = sbuf(ctx, "cur", [P, 8])
        pow2 = sbuf(ctx, "pow2", [P, 16])
        ptr = psum(ctx, "f_ptr", 2)
        ffn = Ffn(ctx, "f", FFN_H // 128)
        f_in, pows, xn_ready, xt_ready, xt_stored, sum_asked, sum_given = (
            sem(s) for s in ("f_in", "pows", "f_xn_ready", "f_xt_ready", "f_xt_stored", "sum_asked", "sum_given"))
        block = ctx.enter_context(nc.Block())

        @block.sync
        def _(sp):
            sp.dma_start(wr[:], bcast_rows(a["L0_ffn_wr"].rearrange("d a -> (d a)"), P)).then_inc(f_in, 16)
            sp.dma_start(br[:], bcast_rows(a["L0_ffn_br"], P)).then_inc(f_in, 16)
            load_rows(sp, w1[:], a["L0_ffn_w1"]).then_inc(f_in, 16)
            load_rows(sp, w2[:], a["L0_ffn_w2"]).then_inc(f_in, 16)
            load_cols(sp, b1[:], a["L0_ffn_b1"], 8).then_inc(f_in, 16)
            sp.dma_start(b2[:], bcast_rows(a["L0_ffn_b2"], P)).then_inc(f_in, 16)

        @block.gpsimd
        def _(pool):
            for j in range(16):
                pool.memset(pow2[:, j:j + 1], float(2 ** (15 - j))).then_inc(pows, 1)
            pool.iota(key_i[:, 2 * NT:3 * NT], pattern=[[-P, NT]], base=8191, channel_multiplier=-1).then_inc(pows, 1)

        @block.vector
        def _(dve):
            ch = chain("dve", dve)
            layer_stats(dve, ch, Rt)
            dve.wait_ge(f_in, 96)

            def norm(t, u, i):
                x_u = xn[:, u * D:(u + 1) * D]
                if later(t):
                    at(dve, xt_ready, t - 1, passed["dve"])
                dve.tensor_scalar(x_u, Rt(t), mean[:, bass.ds(t, 1)], rstd[:, bass.ds(t, 1)], ALU.subtract, ALU.mult).then_inc(xn_ready, 1)
                at(dve, xn_ready, t + 1, passed["dve"])
                ch.step(dve.tensor_tensor(Rt(t), Rt(t), x_u, ALU.add))
                ch.step(dve.tensor_tensor(prod[:, u * D:(u + 1) * D], x_u, wr[:], ALU.mult))
                ch.step(dve.tensor_reduce(wt[:, bass.ds(t, 1)], prod[:, u * D:(u + 1) * D], AX.X, ALU.add))

            tiles(dve, norm, ch, 6)
            ch.step(dve.tensor_scalar(wt[:], wt[:], br[:, 0:1], 0.0, ALU.add, ALU.add))
            ki = [key_i[:, k * NT:(k + 1) * NT] for k in range(3)]
            dve.wait_ge(pows, 17)
            ch.step(dve.tensor_scalar(ki[0], wt[:].bitcast(I32), 31, -2147483648, ALU.arith_shift_right, ALU.bitwise_or))
            ch.step(dve.tensor_tensor(ki[1], ki[0], wt[:].bitcast(I32), ALU.bitwise_xor))
            ch.step(dve.tensor_scalar(ki[0], ki[1], 16, None, ALU.logical_shift_right))
            ch.step(dve.tensor_scalar(ki[1], ki[1], 65535, None, ALU.bitwise_and))
            ch.step(dve.tensor_copy(key[:], key_i[:]))
            need, low, cand, part, gain = (cur[:, j:j + 1] for j in range(5))
            ch.step(dve.memset(need, float(TOPK)))
            ch.step(dve.memset(sel[:], 1.0))
            asked = [0]

            def count(v, threshold, op):
                ch.step(dve.tensor_scalar(hit[:, 0:NT], v, threshold, 0.0, op, ALU.add, accum_out=part))
                dve.sem_inc(sum_asked)

            for level in range(3):
                v, bits = key[:, level * NT:(level + 1) * NT], (16, 16, 13)[level]
                if level:
                    ch.step(dve.tensor_scalar(v, v, 1.0, None, ALU.add))
                    ch.step(dve.tensor_tensor(v, v, sel[:], ALU.mult))
                    ch.step(dve.tensor_scalar(v, v, -1.0, None, ALU.add))
                ch.step(dve.memset(low, 0.0))
                with dve.Fori(0, bits) as j:
                    ch.enter(j, 4)
                    step = pow2[:, bass.ds(j + (16 - bits), 1)]
                    ch.step(dve.tensor_tensor(cand, low, step, ALU.add))
                    count(v, cand, ALU.is_ge)
                    at(dve, sum_given, j + (asked[0] + 1), passed["dve"])
                    ch.step(dve.tensor_scalar(gain, ptr[0:P, 0, 0:1], need, step, ALU.is_ge, ALU.mult))
                    ch.step(dve.tensor_tensor(low, low, gain, ALU.add))
                    ch.leave(bits)
                asked[0] += bits
                if level < 2:
                    count(v, low, ALU.is_gt)
                    asked[0] += 1
                    dve.wait_ge(sum_given, asked[0])
                    ch.step(dve.tensor_copy(gain, ptr[0:P, 0, 0:1]))
                    ch.step(dve.tensor_tensor(need, need, gain, ALU.subtract))
                    ch.step(dve.tensor_scalar(hit[:, (level + 1) * NT:(level + 2) * NT], v, low, None, ALU.is_gt))
                    ch.step(dve.tensor_scalar(sel[:], v, low, None, ALU.is_equal))
                else:
                    ch.step(dve.tensor_scalar(sel[:], v, low, None, ALU.is_ge))
            for k in (1, 2):
                ch.step(dve.tensor_tensor(sel[:], sel[:], hit[:, k * NT:(k + 1) * NT], ALU.max))
            ch.step(dve.tensor_tensor(wt[:], wt[:], sel[:], ALU.mult))

            def add_y(t, y):
                tmp = prod[:, 0:D]
                ch.step(dve.tensor_tensor(tmp, y, b2[:], ALU.add))
                ch.step(dve.scalar_tensor_tensor(out=Rt(t), in0=tmp, scalar=wt[:, bass.ds(t, 1)], in1=Rt(t), op0=ALU.mult, op1=ALU.add))

            ffn.dve(dve, ch, 2, add_y)

        @block.scalar
        def _(act):
            finish_stats_act(act)

            def store_xt(t, u, i):
                at(act, xt_ready, t + 1, passed["act"])
                act.copy(XT[:, bass.ds(t * TS, 2 * P)], ptr[:, u, 0:2 * P]).then_inc(xt_stored, 1)

            tiles(act, store_xt)
            act.wait_ge(f_in, 96)
            ffn.act(act, ACT.Gelu_apprx_tanh, lambda m: b1[:, m:m + 1])

        @block.tensor
        def _(pe):
            def transpose_x(t, u, i):
                at(pe, xn_ready, t + 1, passed["pe"])
                if later(t):
                    at(pe, xt_stored, t - 1, passed["pe"])
                for k in range(2):
                    mm = pe.transpose(ptr[:, u, k * P:(k + 1) * P], xn[:, u * D + k * 128:u * D + (k + 1) * 128], ident[0:P, 0:P])
                mm.then_inc(xt_ready, 1)

            tiles(pe, transpose_x)
            pe.wait_ge(xt_stored, NT)
            n = 16 + 1 + 16 + 1 + 13
            pe.wait_ge(sum_asked, 1)
            pe.matmul(ptr[0:P, 0, 0:1], ones[0:P, 0:P], cur[:, 3:4], start=True, stop=True).then_inc(sum_given, 1)
            with pe.Fori(1, n) as j:
                at(pe, sum_asked, j + 1, passed["pe"])
                pe.matmul(ptr[0:P, 0, 0:1], ones[0:P, 0:P], cur[:, 3:4], start=True, stop=True).then_inc(sum_given, 1)
            pe.wait_ge(f_in, 96)
            ffn.pe(pe, lambda k, m: w1[:, k * FFN_H + m * 128:k * FFN_H + (m + 1) * 128], lambda m: w2[:, m * D:(m + 1) * D])

    with ExitStack() as ctx:
        xn = sbuf(ctx, "g_xn", [P, 2 * D])
        ptr = psum(ctx, "g_ptr", 2)
        xn_ready, xt_ready, xt_stored = sem("g_xn_ready"), sem("g_xt_ready"), sem("g_xt_stored")
        row_out = [sem("row_out0"), sem("row_out1")]
        block = ctx.enter_context(nc.Block())

        @block.sync
        def _(sp):
            def store(t, u, i):
                at(sp, xn_ready, t + 1, passed["sp"])
                sp.dma_start(xn2_d[bass.ds(t * P, P), :], xn[:, u * D:(u + 1) * D]).then_inc(row_out[u], 16)

            tiles(sp, store)
            for u in range(2):
                sp.wait_ge(row_out[u], 16 * (NT // 2))

        @block.vector
        def _(dve):
            ch = chain("dve", dve)
            layer_stats(dve, ch, Rt)

            def norm(t, u, i):
                if later(t):
                    at(dve, xt_ready, t - 1, passed["dve"])
                    at(dve, row_out[u], i * 16, passed["dve"])
                dve.tensor_scalar(xn[:, u * D:(u + 1) * D], Rt(t), mean[:, bass.ds(t, 1)], rstd[:, bass.ds(t, 1)],
                                  ALU.subtract, ALU.mult).then_inc(xn_ready, 1)

            tiles(dve, norm)

        @block.scalar
        def _(act):
            finish_stats_act(act)

            def store_xt(t, u, i):
                at(act, xt_ready, t + 1, passed["act"])
                act.copy(XT[:, bass.ds(t * TS, 2 * P)], ptr[:, u, 0:2 * P]).then_inc(xt_stored, 1)

            tiles(act, store_xt)

        @block.tensor
        def _(pe):
            def transpose_x(t, u, i):
                at(pe, xn_ready, t + 1, passed["pe"])
                if later(t):
                    at(pe, xt_stored, t - 1, passed["pe"])
                for k in range(2):
                    mm = pe.transpose(ptr[:, u, k * P:(k + 1) * P], xn[:, u * D + k * 128:u * D + (k + 1) * 128], ident[0:P, 0:P])
                mm.then_inc(xt_ready, 1)

            tiles(pe, transpose_x)

    s56 = ExitStack()
    agg = sbuf(s56, "agg", [128, (NT + 1) * TS])
    with ExitStack() as ctx:
        U = 4
        ids = sbuf(ctx, "ids2", [128, (NT + 1) * P], I16)
        pw_in = sbuf(ctx, "pw_in", [128, U * 4], I32)
        rows = sbuf(ctx, "rows", [128, U * 2 * D])
        hot = sbuf(ctx, "hot2", [128, U * 2 * P])
        pg = psum(ctx, "pg", 4)
        pairs_in = [sem(f"pairs_in{s}") for s in range(U)]
        rows_in = [sem(f"rows_in{s}") for s in range(U)]
        init, hot_ready, win_summed, acc_done = (sem(s) for s in ("g_init", "g_hot_ready", "g_win_summed", "g_acc_done"))
        block = ctx.enter_context(nc.Block())

        @block.sync
        def _(sp):
            def load(i):
                for s in range(U):
                    if not isinstance(i, int):
                        at(sp, win_summed, i * U + s + 1 - U, passed["sp"])
                    start = sp.value_load(win2_s[0:1, bass.ds(i * U + s, 1)], min_val=0, max_val=E)
                    sp.dma_start(pw_in[:, s * 4:(s + 1) * 4],
                                 pairs_d[bass.ds(start, W2), :].rearrange("(p r) c -> p (r c)", p=128)).then_inc(pairs_in[s], 16)

            load(0)
            with sp.Fori(1, NW2 // U) as i:
                load(i)

        @block.gpsimd
        def _(pool):
            fill_iota(pool, ids).then_inc(init, 1)
            pool.memset(agg[:], 0.0).then_inc(init, 1)

            def gather(i):
                for s in range(U):
                    at(pool, pairs_in[s], i * 16 + 16, passed["pool"])
                    for r in range(2):
                        pool.indirect_dma_start(rows[:, (2 * s + r) * D:(2 * s + r + 1) * D], None, xn2_d,
                                                bass.IndirectOffsetOnAxis(ap=pw_in[:, s * 4 + 2 * r:s * 4 + 2 * r + 1].bitcast(U32), axis=0)
                                                ).then_inc(rows_in[s], 16)

            with pool.Fori(0, NW2 // U) as i:
                gather(i)

        @block.vector
        def _(dve):
            dve.wait_ge(init, 2)

            def windows(i):
                b = [dve.value_load(win2_b[0:1, bass.ds(i * U + s, 1)], min_val=0, max_val=NT) for s in range(U)]
                for s in range(U):
                    at(dve, pairs_in[s], i * 16 + 16, passed["dve"])
                    keys = pw_in[:, s * 4:(s + 1) * 4].rearrange("p (r c) -> p r c", c=2)[:, :, 1]
                    dve.tensor_tensor(hot[:, s * 2 * P:(s + 1) * 2 * P].rearrange("p (r n) -> p r n", r=2),
                                      ids[:, bass.ds(b[s] * P, P)].unsqueeze(1).to_broadcast([128, 2, P]),
                                      keys.unsqueeze(2).to_broadcast([128, 2, P]), ALU.is_equal).then_inc(hot_ready, 1)
                for s in range(U):
                    g = i * U + s
                    at(dve, win_summed, g + 1, passed["dve"])
                    if not isinstance(g, int) or g:
                        at(dve, acc_done, g, passed["dve"])
                    tile = agg[:, bass.ds(b[s] * TS, 2 * P)]
                    dve.tensor_tensor(tile, tile, pg[:, s, 0:2 * P], ALU.add).then_inc(acc_done, 1)

            windows(0)
            with dve.Fori(1, NW2 // U) as i:
                windows(i)

        @block.tensor
        def _(pe):
            def windows(i):
                for s in range(U):
                    g = i * U + s
                    at(pe, hot_ready, g + 1, passed["pe"])
                    at(pe, rows_in[s], i * 32 + 32, passed["pe"])
                    if not isinstance(i, int):
                        at(pe, acc_done, g - U + 1, passed["pe"])
                    for r in range(2):
                        for k in range(2):
                            mm = pe.matmul(pg[:, s, k * P:(k + 1) * P], rows[:, (2 * s + r) * D + k * 128:(2 * s + r) * D + (k + 1) * 128],
                                           hot[:, (2 * s + r) * P:(2 * s + r + 1) * P], start=(r == 0 and k == 0), stop=True, skip_group_check=True)
                    mm.then_inc(win_summed, 1)

            windows(0)
            with pe.Fori(1, NW2 // U) as i:
                windows(i)

    with ExitStack() as ctx:
        wq = sbuf(ctx, "m_wq", [128, 2 * 768])
        w1 = sbuf(ctx, "m_w1", [128, 2 * D])
        w2 = sbuf(ctx, "m_w2", [128, 2 * D])
        wp = sbuf(ctx, "m_wp", [128, 2 * D])
        bq_row = sbuf(ctx, "m_bq_row", [P, 768])
        lng = sbuf(ctx, "m_lng", [P, 2 * D])
        lnb = sbuf(ctx, "m_lnb", [P, 2 * D])
        b1 = sbuf(ctx, "m_b1", [128, 2])
        bq = sbuf(ctx, "m_bq", [128, 2])
        b2 = sbuf(ctx, "m_b2", [P, D])
        xs = sbuf(ctx, "m_xs", [128, 2 * TS])
        kv = sbuf(ctx, "m_kv", [128, 2 * 2 * D])
        sq = sbuf(ctx, "m_sq", [128, 2 * 2 * D])
        kn = sbuf(ctx, "m_kn", [P, 2 * 2 * D])
        hm = sbuf(ctx, "m_hm", [P, 2 * 16])
        hv = sbuf(ctx, "m_hv", [P, 2 * 16])
        wqT = sq
        kvn = sbuf(ctx, "m_kvn", [128, 2 * 128])
        mT = kv
        tb = sbuf(ctx, "m_tb", [128, 2])
        bp = sbuf(ctx, "m_bp", [128, 2])
        tmp = sbuf(ctx, "m_tmp", [P, D])
        m_in, xs_ready, kv_ready, kv_c, sq_ready, var_r, sd_r, kn_ready, ctx_done, kv_read = (
            sem("m_" + s) for s in ("in", "xs_ready", "kv_ready", "kv_c", "sq_ready", "var_r", "sd_r", "kn_ready", "ctx_done", "kv_read"))
        q_compact = sem("q_compact")
        fold_pe, fold_dve = sem("m_fold_pe"), sem("m_fold_dve")

        def all_dma(sp):
            sp.dma_start(bq_row[:], bcast_rows(a["L1_mix_b_qkv"], P)).then_inc(m_in, 16)
            load_rows(sp, wq[:], a["L1_mix_w_qkv"]).then_inc(m_in, 16)
            load_rows(sp, w1[:], a["L1_mix_w1"]).then_inc(m_in, 16)
            load_rows(sp, w2[:], a["L1_mix_w2"]).then_inc(m_in, 16)
            load_cols(sp, b1[:], a["L1_mix_b1"], 2).then_inc(m_in, 16)
            sp.dma_start(b2[:], bcast_rows(a["L1_mix_b2"], P)).then_inc(m_in, 16)
            with nc.allow_non_contiguous_dma(reason="a bias per partition"):
                for m in range(2):
                    for h in range(4):
                        o = 96 * (4 * m + h)
                        sp.dma_start(bq[32 * h:32 * h + 32, m:m + 1], a["L1_mix_b_qkv"][o:o + 32].rearrange("(p a) -> p a", a=1)).then_inc(m_in, 16)
            for j, (g_, b_) in enumerate((("kln_g", "kln_b"), ("vln_g", "vln_b"))):
                for dst, name in ((lng, g_), (lnb, b_)):
                    for h in range(HEADS):
                        sp.dma_start(dst[:, h * 64 + j * 32:h * 64 + j * 32 + 32], bcast_rows(a["L1_mix_" + name], P)).then_inc(m_in, 16)

        M_IN = 16 * (6 + 8 + 32)
        with ExitStack() as c1:
            pk = psum(c1, "m_pk", 2)
            pc = psum(c1, "m_pc", 1)
            pf = psum(c1, "m_pf", 4)
            block = c1.enter_context(nc.Block())

            @block.sync
            def _(sp):
                all_dma(sp)

            @block.vector
            def _(dve):
                ch = chain("dve", dve)
                dve.wait_ge(m_in, M_IN)
                bias = bq_row[:].rearrange("p (h c) -> p h c", h=HEADS)[:, :, 32:96]

                def norm_kv(t, u, i):
                    kv_u, sq_u, kn_u = (x[0:P, u * 2 * D:(u + 1) * 2 * D] for x in (kv, sq, kn))
                    m_u, v_u = hm[:, u * 16:(u + 1) * 16], hv[:, u * 16:(u + 1) * 16]
                    kv3 = kv_u.rearrange("p (g d) -> p g d", g=16)
                    at(dve, kv_ready, t + 1, passed["dve"])
                    dve.tensor_tensor(kv_u.rearrange("p (h c) -> p h c", h=HEADS), pk[0:P, u, :].rearrange("p (h c) -> p h c", h=HEADS), bias, ALU.add).then_inc(kv_read, 1)
                    at(dve, kv_read, t + 1, passed["dve"])
                    ch.step(dve.tensor_reduce(m_u, kv3, AX.X, ALU.add))
                    ch.step(dve.tensor_scalar(m_u, m_u, 1.0 / HD, None, ALU.mult))
                    dve.tensor_tensor(kv3, kv3, m_u.unsqueeze(2).to_broadcast([P, 16, HD]), ALU.subtract).then_inc(kv_c, 1)
                    at(dve, sq_ready, t + 1, passed["dve"])
                    ch.step(dve.tensor_reduce(v_u, sq_u.rearrange("p (g d) -> p g d", g=16), AX.X, ALU.add))
                    dve.tensor_scalar(v_u, v_u, 1.0 / HD, EPS, ALU.mult, ALU.add).then_inc(var_r, 1)
                    at(dve, sd_r, t + 1, passed["dve"])
                    ch.step(dve.reciprocal(v_u, v_u))
                    ch.step(dve.tensor_tensor(kv3, kv3, v_u.unsqueeze(2).to_broadcast([P, 16, HD]), ALU.mult))
                    ch.step(dve.tensor_tensor(kv_u, kv_u, lng[:], ALU.mult))
                    if later(t):
                        at(dve, ctx_done, t - 1, passed["dve"])
                    for j in range(2):
                        ins = dve.tensor_tensor(kn_u[:, j * D:(j + 1) * D].rearrange("p (h d) -> p h d", h=HEADS),
                                                kv_u.rearrange("p (h c) -> p h c", h=HEADS)[:, :, j * HD:(j + 1) * HD],
                                                lnb[:].rearrange("p (h c) -> p h c", h=HEADS)[:, :, j * HD:(j + 1) * HD], ALU.add)
                        ins.then_inc(kn_ready, 1)

                tiles(dve, norm_kv, ch, 12)
                dve.wait_ge(ctx_done, NT)
                for m in range(2):
                    ch.step(dve.tensor_scalar(kvn[:, m * 128:(m + 1) * 128], pc[:, 0, m * 128:(m + 1) * 128], 1.0 / N, None, ALU.mult))
                    ch.step(dve.tensor_tensor(kvn[:, m * 128:(m + 1) * 128], kvn[:, m * 128:(m + 1) * 128], blockdiag[:], ALU.mult))
                dve.wait_ge(fold_pe, 1)
                for m in range(2):
                    ch.step(dve.tensor_copy(wqT[:, m * D:(m + 1) * D], pf[:, m, 0:D]))
                dve.sem_inc(fold_dve)
                dve.wait_ge(fold_pe, 2)
                for m in range(2):
                    ch.step(dve.tensor_copy(mT[:, m * D:(m + 1) * D], pf[:, 2 + m, 0:D]))
                    d = mT[:, m * D + m * 128:m * D + (m + 1) * 128]
                    ch.step(dve.tensor_tensor(d, d, ident[:], ALU.add))
                    ch.step(dve.tensor_copy(tb[:, m:m + 1], pf[:, 0, m:m + 1]))
                dve.sem_inc(fold_dve)
                dve.wait_ge(fold_pe, 3)
                for m in range(2):
                    ch.step(dve.tensor_copy(wp[:, m * D:(m + 1) * D], pf[:, 2 + m, 0:D]))
                ch.step(dve.tensor_tensor(bp[:], b1[:], pf[:, 1, 0:2], ALU.add))

            @block.scalar
            def _(act):
                def parts(t, u, i):
                    if later(t):
                        at(act, kv_ready, t - 1, passed["act"])
                    act.copy(xs[:, u * TS:u * TS + 2 * P], XT[:, bass.ds(t * TS, 2 * P)]).then_inc(xs_ready, 1)
                    at(act, kv_c, t + 1, passed["act"])
                    act.activation(sq[0:P, u * 2 * D:(u + 1) * 2 * D], kv[0:P, u * 2 * D:(u + 1) * 2 * D], ACT.Square).then_inc(sq_ready, 1)
                    at(act, var_r, t + 1, passed["act"])
                    act.activation(hv[:, u * 16:(u + 1) * 16], hv[:, u * 16:(u + 1) * 16], ACT.Sqrt).then_inc(sd_r, 1)

                tiles(act, parts)
                act.wait_ge(m_in, M_IN)
                for k in range(2):
                    act.copy(wp[:, k * D:(k + 1) * D].rearrange("p (h c) -> p h c", h=HEADS),
                             wq[:, k * 768:(k + 1) * 768].rearrange("p (h c) -> p h c", h=HEADS)[:, :, 0:32]).then_inc(q_compact, 1)

            @block.tensor
            def _(pe):
                pe.wait_ge(m_in, M_IN)

                def context(t, u):
                    at(pe, kn_ready, 2 * t + 2, passed["pe"])
                    first = isinstance(t, int) and t == 0
                    for m in range(2):
                        mm = pe.matmul(pc[:, 0, m * 128:(m + 1) * 128], kn[:, u * 2 * D + m * 128:u * 2 * D + (m + 1) * 128],
                                       kn[:, u * 2 * D + D + m * 128:u * 2 * D + D + (m + 1) * 128], start=first and m == 0, stop=True, skip_group_check=True)
                    mm.then_inc(ctx_done, 1)

                def project(t, u, i):
                    at(pe, xs_ready, t + 1, passed["pe"])
                    if later(t):
                        at(pe, kv_read, t - 1, passed["pe"])
                    for k in range(2):
                        w = wq[:, k * 768:(k + 1) * 768].rearrange("p (h c) -> p h c", h=HEADS)[:, :, 32:96]
                        mm = pe.matmul(pk[0:P, u, :].rearrange("p (h c) -> p h c", h=HEADS), xs[:, u * TS + k * P:u * TS + (k + 1) * P], w, start=(k == 0), stop=(k == 1))
                    mm.then_inc(kv_ready, 1)
                    if not isinstance(t, int) or t:
                        context(t - 1, 1 - u)

                tiles(pe, project)
                context(NT - 1, 1)
                pe.wait_ge(q_compact, 2)
                for m in range(2):
                    for k in range(2):
                        mm = pe.matmul(pf[:, m, k * 128:(k + 1) * 128], wp[:, k * D + m * 128:k * D + (m + 1) * 128], ident[:], start=True, stop=True)
                mm.then_inc(fold_pe, 1)
                pe.wait_ge(fold_dve, 1)
                for m in range(2):
                    pe.matmul(pf[:, 2 + m, 0:D], kvn[:, m * 128:(m + 1) * 128], wqT[:, m * D:(m + 1) * D], start=True, stop=True)
                for m in range(2):
                    mm = pe.matmul(pf[:, 0, m:m + 1], kvn[:, m * 128:(m + 1) * 128], bq[:, m:m + 1], start=True, stop=True)
                mm.then_inc(fold_pe, 1)
                pe.wait_ge(fold_dve, 2)
                for k in range(2):
                    for m in range(2):
                        pe.matmul(pf[:, 2 + k, 0:D], mT[:, m * D + k * 128:m * D + (k + 1) * 128], w1[:, m * D:(m + 1) * D], start=(m == 0), stop=(m == 1))
                for c in range(2):
                    for m in range(2):
                        mm = pe.matmul(pf[:, 1, c:c + 1], w1[:, m * D + c * 128:m * D + (c + 1) * 128], tb[:, m:m + 1], start=(m == 0), stop=(m == 1))
                mm.then_inc(fold_pe, 1)

        with ExitStack() as c2:
            ffn = Ffn(c2, "m", 2)
            block = c2.enter_context(nc.Block())

            @block.vector
            def _(dve):
                ch = chain("dve", dve)

                def add_y(t, y):
                    ch.step(dve.tensor_tensor(tmp[:], y, b2[:], ALU.add))
                    ch.step(dve.tensor_scalar(sq[0:P, 0:D], Rt(t), mean[:, bass.ds(t, 1)], rstd[:, bass.ds(t, 1)], ALU.subtract, ALU.mult))
                    ch.step(dve.tensor_tensor(tmp[:], tmp[:], sq[0:P, 0:D], ALU.add))
                    ch.step(dve.tensor_tensor(Rt(t), Rt(t), tmp[:], ALU.add))

                ffn.dve(dve, ch, 4, add_y)

            @block.scalar
            def _(act):
                ffn.act(act, ACT.Gelu, lambda m: bp[:, m:m + 1])

            @block.tensor
            def _(pe):
                ffn.pe(pe, lambda k, m: wp[:, k * D + m * 128:k * D + (m + 1) * 128], lambda m: w2[:, m * D:(m + 1) * D])

    with s56, ExitStack() as ctx:
        wl = sbuf(ctx, "s_wl", [128, 2 * D])
        wr = sbuf(ctx, "s_wr", [128, 2 * D])
        wn = sbuf(ctx, "s_wn", [128, 4 * D])
        bl = sbuf(ctx, "s_bl", [P, D])
        gm = sbuf(ctx, "s_gm", [P, D])
        bt = sbuf(ctx, "s_bt", [P, D])
        mu = sbuf(ctx, "s_mu", [P, D])
        gv = sbuf(ctx, "s_gv", [P, D])
        xs = sbuf(ctx, "s_xs", [128, 2 * 2 * TS])
        sq = sbuf(ctx, "s_sq", [P, 2 * D])
        rdeg = sbuf(ctx, "s_rdeg", [P, NT])
        ss = sbuf(ctx, "s_ss", [P, NT])
        pa = psum(ctx, "s_pa", 2)
        pb = psum(ctx, "s_pb", 2)
        pst = psum(ctx, "s_pst", 2)
        pt = psum(ctx, "s_pt", 2)
        s_in, wt_ready, w_stored, xs_ready, ab_ready, o_ready, ss_done, ss_ready, n_ready, sum_ready, c_ready, sq_ready2, var_ready2, sd_ready2, sq_used = (
            sem("s_" + s) for s in ("in", "wt_ready", "w_stored", "xs_ready", "ab_ready", "o_ready", "ss_done", "ss_ready", "n_ready", "sum_ready", "c_ready", "sq_ready2", "var_ready2", "sd_ready2", "sq_used"))
        block = ctx.enter_context(nc.Block())

        sum_steps = sem("s_sum_steps")

        def Ot(t):
            return agg[0:P, bass.ds(t * TS, D)]

        @block.sync
        def _(sp):
            load_rows(sp, wn[:, 0:2 * D], a["L1_gnn_W_l"]).then_inc(s_in, 16)
            load_rows(sp, wn[:, 2 * D:4 * D], a["L1_gnn_W_r"]).then_inc(s_in, 16)
            for dst, name in ((bl, "b_l"), (gm, "gamma"), (bt, "beta")):
                sp.dma_start(dst[:], bcast_rows(a["L1_gnn_" + name], P)).then_inc(s_in, 16)

        @block.vector
        def _(dve):
            ch = chain("dve", dve)
            dve.wait_ge(s_in, 80)
            ch.step(dve.tensor_scalar(rdeg[:], deg_in[:], 1.0, None, ALU.max))
            ch.step(dve.reciprocal(rdeg[:], rdeg[:]))

            def combine(t, u, i):
                at(dve, ab_ready, t + 1, passed["dve"])
                ch.step(dve.scalar_tensor_tensor(out=Ot(t), in0=pa[0:P, u, 0:D], scalar=rdeg[:, bass.ds(t, 1)], in1=bl[:], op0=ALU.mult, op1=ALU.add))
                dve.tensor_tensor(Ot(t), Ot(t), pb[0:P, u, 0:D], ALU.add).then_inc(o_ready, 1)

            tiles(dve, combine, ch, 2)
            dve.wait_ge(ss_ready, 1)
            ch.step(dve.tensor_scalar(ss[:], ss[:], 1e-12, None, ALU.max))
            ch.step(dve.reciprocal(ss[:], ss[:]))

            def unit(t, u, i):
                dve.tensor_scalar(Ot(t), Ot(t), ss[:, bass.ds(t, 1)], None, ALU.mult).then_inc(n_ready, 1)

            tiles(dve, unit)
            dve.wait_ge(sum_ready, 1)
            dve.wait_ge(n_ready, NT)
            ch.step(dve.tensor_scalar(mu[:], pst[0:P, 0, 0:D], 1.0 / N, None, ALU.mult))

            def center(t, u, i):
                dve.tensor_tensor(Ot(t), Ot(t), mu[:], ALU.subtract).then_inc(c_ready, 1)

            tiles(dve, center)
            dve.wait_ge(sum_ready, 2)
            dve.wait_ge(c_ready, NT)
            dve.tensor_scalar(gv[:], pst[0:P, 1, 0:D], 1.0 / N, EPS, ALU.mult, ALU.add).then_inc(var_ready2, 1)
            dve.wait_ge(sd_ready2, 1)
            ch.step(dve.reciprocal(gv[:], gv[:]))
            ch.step(dve.tensor_tensor(gv[:], gv[:], gm[:], ALU.mult))

            def finish(t, u, i):
                ch.step(dve.tensor_tensor(Ot(t), Ot(t), gv[:], ALU.mult))
                ch.step(dve.tensor_tensor(Ot(t), Ot(t), bt[:], ALU.add))
                ch.step(dve.scalar_tensor_tensor(out=Rt(t), in0=Ot(t), scalar=0.0, in1=Rt(t), op0=ALU.max, op1=ALU.add))

            tiles(dve, finish, ch, 6)

        @block.scalar
        def _(act):
            for j in range(2):
                for k in range(2):
                    act.wait_ge(wt_ready, 2 * j + k + 1)
                    act.copy((wl, wr)[j][:, k * D:(k + 1) * D], pt[:, k, 0:D]).then_inc(w_stored, 1)

            def parts(t, u, i):
                if later(t):
                    at(act, ab_ready, t - 1, passed["act"])
                act.copy(xs[:, 2 * u * TS:2 * u * TS + 2 * P], agg[:, bass.ds(t * TS, 2 * P)]).then_inc(xs_ready, 1)
                act.copy(xs[:, (2 * u + 1) * TS:(2 * u + 1) * TS + 2 * P], XT[:, bass.ds(t * TS, 2 * P)]).then_inc(xs_ready, 1)
                at(act, o_ready, t + 1, passed["act"])
                if later(t):
                    at(act, ss_done, t - 1, passed["act"])
                act.activation(sq[:, u * D:(u + 1) * D], Ot(t), ACT.Square, accum_out=ss[:, bass.ds(t, 1)]).then_inc(ss_done, 1)

            tiles(act, parts)
            act.wait_ge(ss_done, NT)
            act.activation(ss[:], ss[:], ACT.Sqrt).then_inc(ss_ready, 1)

            def squares(t, u, i):
                at(act, c_ready, t + 1, passed["act"])
                if later(t):
                    at(act, sq_used, t - 1, passed["act"])
                act.activation(sq[:, u * D:(u + 1) * D], Ot(t), ACT.Square).then_inc(sq_ready2, 1)

            tiles(act, squares)
            act.wait_ge(var_ready2, 1)
            act.activation(gv[:], gv[:], ACT.Sqrt).then_inc(sd_ready2, 1)

        @block.tensor
        def _(pe):
            pe.wait_ge(s_in, 80)
            for j in range(2):
                for k in range(2):
                    if j:
                        pe.wait_ge(w_stored, k + 1)
                    for n in range(2):
                        mm = pe.transpose(pt[:, k, n * 128:(n + 1) * 128], wn[:, (2 * j + n) * D + k * 128:(2 * j + n) * D + (k + 1) * 128], ident[:])
                    mm.then_inc(wt_ready, 1)
            pe.wait_ge(w_stored, 4)

            def project(t, u, i):
                at(pe, xs_ready, 2 * t + 2, passed["pe"])
                if later(t):
                    at(pe, o_ready, t - 1, passed["pe"])
                for p_, w, s in ((pa, wl, 2 * u), (pb, wr, 2 * u + 1)):
                    for k in range(2):
                        mm = pe.matmul(p_[0:P, u, 0:D], xs[:, s * TS + k * P:s * TS + (k + 1) * P], w[:, k * D:(k + 1) * D], start=(k == 0), stop=(k == 1))
                mm.then_inc(ab_ready, 1)

            tiles(pe, project)

            def sum_rows(t, u, i):
                at(pe, n_ready, t + 1, passed["pe"])
                mm = pe.matmul(pst[0:P, 0, 0:D], ones[0:P, 0:P], Ot(t), start=(isinstance(t, int) and t == 0), stop=True, skip_group_check=True)
                return mm

            tiles(pe, lambda t, u, i: sum_rows(t, u, i).then_inc(sum_steps, 1))
            pe.wait_ge(sum_steps, NT)
            pe.sem_inc(sum_ready)

            def sum_squares(t, u, i):
                at(pe, sq_ready2, t + 1, passed["pe"])
                pe.matmul(pst[0:P, 1, 0:D], ones[0:P, 0:P], sq[:, u * D:(u + 1) * D], start=(isinstance(t, int) and t == 0), stop=True, skip_group_check=True).then_inc(sq_used, 1)

            tiles(pe, sum_squares)
            pe.wait_ge(sq_used, NT)
            pe.sem_inc(sum_ready)

    with ExitStack() as ctx:
        w1 = sbuf(ctx, "e_w1", [128, EXPERTS * 2 * EXP_H])
        w2 = sbuf(ctx, "e_w2", [128, EXPERTS * 4 * D])
        b1 = sbuf(ctx, "e_b1", [128, EXPERTS * 4])
        b2 = sbuf(ctx, "e_b2", [P, EXPERTS * D])
        wr = sbuf(ctx, "e_wr", [128, 2 * EXPERTS])
        br = sbuf(ctx, "e_br", [P, EXPERTS])
        gm = sbuf(ctx, "e_gm", [P, D])
        bt = sbuf(ctx, "e_bt", [P, D])
        xn = sbuf(ctx, "e_xn", [P, 2 * D])
        xs = sbuf(ctx, "e_xs", [128, 2 * TS])
        lg = sbuf(ctx, "e_lg", [P, NT * EXPERTS])
        best = sbuf(ctx, "e_best", [P, NT])
        tot = sbuf(ctx, "e_tot", [P, NT])
        rank = sbuf(ctx, "e_rank", [P, NT * EXPERTS])
        cmp = sbuf(ctx, "e_cmp", [P, NT])
        tmp = sbuf(ctx, "e_tmp", [P, D])
        e_in, xn_ready, xt_ready, xt_stored, xs_ready, lg_ready, lg_read, exp_asked, exp_given = (
            sem("e_" + s) for s in ("in", "xn_ready", "xt_ready", "xt_stored", "xs_ready", "lg_ready", "lg_read", "exp_asked", "exp_given"))
        E_IN = 16 * (8 + 2 * 8)

        with ExitStack() as c1:
            ptr = psum(c1, "e_ptr", 2)
            pl = psum(c1, "e_pl", 2)
            block = c1.enter_context(nc.Block())

            @block.sync
            def _(sp):
                for e in range(EXPERTS):
                    load_rows(sp, w1[:, e * 2 * EXP_H:(e + 1) * 2 * EXP_H], a["L1_ffn_W1"][e]).then_inc(e_in, 16)
                    load_rows(sp, w2[:, e * 4 * D:(e + 1) * 4 * D], a["L1_ffn_W2"][e]).then_inc(e_in, 16)
                for dst, v in ((gm, "gamma"), (bt, "beta"), (br, "br")):
                    sp.dma_start(dst[:], bcast_rows(a["L1_ffn_" + v], P)).then_inc(e_in, 16)
                sp.dma_start(b2[:], bcast_rows(a["L1_ffn_b2"].rearrange("e d -> (e d)"), P)).then_inc(e_in, 16)
                load_cols(sp, b1[:], a["L1_ffn_b1"].rearrange("e h -> (e h)"), EXPERTS * 4).then_inc(e_in, 16)
                load_rows(sp, wr[:], a["L1_ffn_Wr"]).then_inc(e_in, 16)
                sp.sem_inc(e_in, 32)

            @block.vector
            def _(dve):
                ch = chain("dve", dve)
                layer_stats(dve, ch, Rt)
                dve.wait_ge(e_in, E_IN)

                def logits(t, u):
                    at(dve, lg_ready, t + 1, passed["dve"])
                    dve.tensor_tensor(lg[:, bass.ds(t * EXPERTS, EXPERTS)], pl[0:P, u, 0:EXPERTS], br[:], ALU.add).then_inc(lg_read, 1)

                def norm(t, u, i):
                    x_u = xn[:, u * D:(u + 1) * D]
                    if later(t):
                        at(dve, xt_ready, t - 1, passed["dve"])
                    ch.step(dve.tensor_scalar(x_u, Rt(t), mean[:, bass.ds(t, 1)], rstd[:, bass.ds(t, 1)], ALU.subtract, ALU.mult))
                    ch.step(dve.tensor_tensor(x_u, x_u, gm[:], ALU.mult))
                    dve.tensor_tensor(x_u, x_u, bt[:], ALU.add).then_inc(xn_ready, 1)
                    if not isinstance(t, int) or t:
                        logits(t - 1, 1 - u)

                tiles(dve, norm, ch, 4)
                logits(NT - 1, 1)
                dve.wait_ge(lg_read, NT)
                l3 = lg[:].rearrange("p (t e) -> p t e", e=EXPERTS)
                r3 = rank[:].rearrange("p (t e) -> p t e", e=EXPERTS)
                ch.step(dve.memset(rank[:], 0.0))
                for e in range(EXPERTS):
                    for f in range(EXPERTS):
                        if e != f:
                            ch.step(dve.tensor_tensor(cmp[:], l3[:, :, f], l3[:, :, e], ALU.is_ge if f < e else ALU.is_gt))
                            ch.step(dve.tensor_tensor(r3[:, :, e], r3[:, :, e], cmp[:], ALU.add))
                ch.step(dve.tensor_reduce(best[:], l3, AX.X, ALU.max))
                ch.step(dve.tensor_tensor(l3, l3, best[:].unsqueeze(2).to_broadcast([P, NT, EXPERTS]), ALU.subtract))
                dve.sem_inc(exp_asked)
                dve.wait_ge(exp_given, 1)
                ch.step(dve.tensor_scalar(rank[:], rank[:], 2.0, None, ALU.is_lt))
                ch.step(dve.tensor_tensor(lg[:], lg[:], rank[:], ALU.mult))
                ch.step(dve.tensor_reduce(tot[:], l3, AX.X, ALU.add))
                ch.step(dve.reciprocal(tot[:], tot[:]))
                ch.step(dve.tensor_tensor(l3, l3, tot[:].unsqueeze(2).to_broadcast([P, NT, EXPERTS]), ALU.mult))

            @block.scalar
            def _(act):
                finish_stats_act(act)

                def store_xt(t, u, i):
                    at(act, xt_ready, t + 1, passed["act"])
                    act.copy(XT[:, bass.ds(t * TS, 2 * P)], ptr[:, u, 0:2 * P]).then_inc(xt_stored, 1)
                    if later(t):
                        at(act, lg_ready, t - 1, passed["act"])
                    act.copy(xs[:, u * TS:u * TS + 2 * P], ptr[:, u, 0:2 * P]).then_inc(xs_ready, 1)

                tiles(act, store_xt)
                act.wait_ge(exp_asked, 1)
                act.activation(lg[:], lg[:], ACT.Exp).then_inc(exp_given, 1)

            @block.tensor
            def _(pe):
                pe.wait_ge(e_in, E_IN)

                def route(t, u):
                    at(pe, xs_ready, t + 1, passed["pe"])
                    if later(t):
                        at(pe, lg_read, t - 1, passed["pe"])
                    for k in range(2):
                        mm = pe.matmul(pl[0:P, u, 0:EXPERTS], xs[:, u * TS + k * P:u * TS + (k + 1) * P], wr[:, k * EXPERTS:(k + 1) * EXPERTS], start=(k == 0), stop=(k == 1))
                    mm.then_inc(lg_ready, 1)

                def transpose_x(t, u, i):
                    at(pe, xn_ready, t + 1, passed["pe"])
                    if later(t):
                        at(pe, xs_ready, t - 1, passed["pe"])
                    for k in range(2):
                        mm = pe.transpose(ptr[:, u, k * P:(k + 1) * P], xn[:, u * D + k * 128:u * D + (k + 1) * 128], ident[0:P, 0:P])
                    mm.then_inc(xt_ready, 1)
                    if not isinstance(t, int) or t:
                        route(t - 1, 1 - u)

                tiles(pe, transpose_x)
                route(NT - 1, 1)

        with ExitStack() as c2:
            ffn = Ffn(c2, "e", EXP_H // 128)
            block = c2.enter_context(nc.Block())

            @block.vector
            def _(dve):
                ch = chain("dve", dve)
                for e in range(EXPERTS):
                    def add_y(t, y):
                        ch.step(dve.tensor_tensor(tmp[:], y, b2[:, e * D:(e + 1) * D], ALU.add))
                        ch.step(dve.scalar_tensor_tensor(out=Rt(t), in0=tmp[:], scalar=lg[:, bass.ds(t * EXPERTS + e, 1)], in1=Rt(t), op0=ALU.mult, op1=ALU.add))

                    ffn.dve(dve, ch, 2, add_y)

            @block.scalar
            def _(act):
                for e in range(EXPERTS):
                    ffn.act(act, ACT.Gelu, lambda m: b1[:, e * 4 + m:e * 4 + m + 1])

            @block.tensor
            def _(pe):
                for e in range(EXPERTS):
                    ffn.pe(pe, lambda k, m: w1[:, (e * 2 + k) * EXP_H + m * 128:(e * 2 + k) * EXP_H + (m + 1) * 128],
                           lambda m: w2[:, (e * 4 + m) * D:(e * 4 + m + 1) * D])

    written = sem("written")
    with nc.Block() as block:
        @block.sync
        def _(sp):
            sp.dma_start(out.rearrange("(t p) d -> p t d", p=P), R[:].rearrange("p (t d) -> p t d", d=TS)).then_inc(written, 16)
            sp.wait_ge(written, 16)
    top.close()


def kernel(**inputs):
    import numpy as np
    import concourse.bacc as bacc
    from concourse.bass_utils import run_bass_kernel_spmd

    nc = bacc.Bacc("TRN2", target_bir_lowering=False, num_devices=1)
    arrays, args = {}, {}
    for name, value in inputs.items():
        value = np.ascontiguousarray(value)
        arrays[f"in_{name}"] = value
        args[name] = nc.dram_tensor(f"in_{name}", value.shape, mybir.dt.from_np(value.dtype), kind="ExternalInput").ap()
    out = nc.dram_tensor("out_nodes", (N, D), F32, kind="ExternalOutput").ap()
    program(nc, args, out)
    result = run_bass_kernel_spmd(nc, [arrays], core_ids=[0])
    return result.results[0]["out_nodes"]
```

```python
from contextlib import ExitStack

import concourse.bass as bass
from concourse import mybir

F32 = mybir.dt.float32
BF16 = mybir.dt.bfloat16
I32 = mybir.dt.int32
U32 = mybir.dt.uint32
I16 = mybir.dt.int16
U16 = mybir.dt.uint16
ALU = mybir.AluOpType
ACT = mybir.ActivationFunctionType
AX = mybir.AxisListType.X

N, D, E, ED = 6250, 256, 200000, 128
P = 125
NT = N // P
EC = E // P
TS = 256
PAD_KEY = 99999
W1 = 512
W2 = 256
NW1 = (E + NT * (W1 - 1)) // W1
NW2 = -(-((E + NT * (W2 - 1)) // W2) // 4) * 4
MAGIC = 12582912.0
EPS = 1e-5
MAX_DEGREE = 512
TOPK = N // 2 - 1
HEADS, HD = 8, 32
FFN_H = 1024
EXPERTS, EXP_H = 8, 512
MW = 256
NWM = (2 * N + EXPERTS * (MW - 1)) // MW


def at(eng, sem, value, passed):
    eng.wait_ge(sem, value)
    eng.sem_inc(passed)


class Chain:

    def __init__(self, eng, sem, passed):
        self.eng, self.sem, self.passed = eng, sem, passed
        self.base, self.k, self.i, self.per = 0, 0, None, 0

    def enter(self, i, per):
        self.i, self.per, self.k = i, per, 0

    def leave(self, times):
        assert self.k == self.per, (self.k, self.per)
        self.base += times * self.per
        self.i, self.k = None, 0

    def step(self, ins):
        ins.then_inc(self.sem, 1)
        self.k += 1
        if self.i is None:
            self.base += 1
            self.k = 0
            self.eng.wait_ge(self.sem, self.base)
        else:
            at(self.eng, self.sem, self.i * self.per + (self.base + self.k), self.passed)


def bcast_rows(ap, rows):
    return ap.rearrange("(a d) -> a d", a=1).to_broadcast([rows, ap.shape[0]])


def program(nc, a, out):
    top = ExitStack()
    uid, section = [0], []

    def sem(name):
        uid[0] += 1
        section.append(nc.alloc_semaphore(f"{name}_{uid[0]}"))
        return section[-1]

    def end_section():
        nc.clear_and_free_semaphores(section)
        nc.all_engine_barrier()
        section.clear()

    def sbuf(ctx, name, shape, dt=F32):
        return ctx.enter_context(nc.sbuf_tensor(name, shape, dt))

    def psum(ctx, name, banks):
        return ctx.enter_context(nc.psum_tensor(name, [128, banks, 512], F32))

    passed = {e: sem("passed_" + e) for e in ("dve", "act", "pe", "sp", "pool")}
    steps = {e: sem("steps_" + e) for e in ("dve", "act", "pool")}
    chains = {}

    def chain(kind, eng):
        if kind not in chains:
            chains[kind] = Chain(eng, steps[kind], passed[kind])
        chains[kind].eng = eng
        return chains[kind]

    def load_values(eng, table, first, count, top_value):
        return nc.values_load_multi_w_load_instructions(table[0:1, bass.ds(first, count)], engines=[eng.engine],
                                                        min_val=0, max_val=top_value)[1]

    rows_d = nc.dram_tensor("rows_by_src", (E + W1, ED + 1), F32, kind="Internal").ap()
    pairs_d = nc.dram_tensor("pairs_by_dst", (E + W2, 2), I32, kind="Internal").ap()
    xn2_d = nc.dram_tensor("xn2_rows", (N, D), F32, kind="Internal").ap()

    moe_x_d = nc.dram_tensor("moe_rows", (2 * N + MW, D), F32, kind="Internal").ap()
    moe_y_d = nc.dram_tensor("moe_results", (NWM * MW, D), F32, kind="Internal").ap()

    R = sbuf(top, "R", [P, NT * TS])
    XT = sbuf(top, "XT", [128, NT * TS])
    ident = sbuf(top, "ident", [128, 128])
    ones = sbuf(top, "ones", [128, 128])
    lower = sbuf(top, "lower", [128, 128])
    blockdiag = sbuf(top, "blockdiag", [128, 128])
    iota_f = sbuf(top, "iota_f", [128, 128])
    win1_b = sbuf(top, "win1_b", [1, NW1], I32)
    win1_s = sbuf(top, "win1_s", [1, NW1], I32)
    win2_b = sbuf(top, "win2_b", [1, NW2], I32)
    win2_s = sbuf(top, "win2_s", [1, NW2], I32)
    unsorted = sbuf(top, "unsorted", [1, 1], I32)
    deg_in = sbuf(top, "deg_in", [P, NT])
    mean = sbuf(top, "mean", [P, NT])
    rstd = sbuf(top, "rstd", [P, NT])
    stats = sbuf(top, "stats", [P, NT * 6])

    def Rt(t):
        return R[:, bass.ds(t * TS, D)]

    def row_stats_loop(dve, ch, read):
        with dve.Fori(0, NT // 2) as i:
            for u in range(2):
                ins = dve.bn_stats(stats[:, bass.ds((i * 2 + u) * 6, 6)], read(i * 2 + u))
            ins.then_inc(stats_done, 1)
        dve.wait_ge(stats_done, stats_target[0])

    stats_done = sem("stats_done")
    stats_target = [0]
    var_ready, sd_ready = sem("var_ready"), sem("sd_ready")
    ln_count = [0, 0]

    def finish_stats_dve(dve, ch):
        s6 = stats[:].rearrange("p (t s) -> p t s", s=6)
        ln_count[0] += 1
        ch.step(dve.tensor_tensor(mean[:], s6[:, :, 1], s6[:, :, 4], ALU.add))
        ch.step(dve.tensor_scalar(mean[:], mean[:], 0.5, None, ALU.mult))
        ch.step(dve.tensor_tensor(rstd[:], s6[:, :, 1], mean[:], ALU.subtract))
        ch.step(dve.tensor_tensor(rstd[:], rstd[:], rstd[:], ALU.mult))
        ch.step(dve.tensor_tensor(s6[:, :, 2], s6[:, :, 2], s6[:, :, 5], ALU.add))
        ch.step(dve.tensor_scalar(s6[:, :, 2], s6[:, :, 2], 1.0 / D, None, ALU.mult))
        ch.step(dve.tensor_tensor(rstd[:], rstd[:], s6[:, :, 2], ALU.add))
        dve.tensor_scalar(rstd[:], rstd[:], EPS, None, ALU.add).then_inc(var_ready, 1)
        dve.wait_ge(sd_ready, ln_count[0])
        ch.step(dve.reciprocal(rstd[:], rstd[:]))

    def finish_stats_act(act):
        ln_count[1] += 1
        act.wait_ge(var_ready, ln_count[1])
        act.activation(rstd[:], rstd[:], ACT.Sqrt).then_inc(sd_ready, 1)

    def layer_stats(dve, ch, read):
        stats_target[0] += NT // 2
        row_stats_loop(dve, ch, read)
        finish_stats_dve(dve, ch)

    def rank_edges(dve, ch, hi, before, mask, rank, pos_f, pos):
        with dve.Fori(0, NT // 2) as i:
            ch.enter(i, 6)
            for u in range(2):
                b = i * 2 + u
                m = mask[:, u * EC:(u + 1) * EC]
                ch.step(dve.tensor_scalar(m, hi[:], iota_f[0:P, bass.ds(b, 1)], None, ALU.is_equal))
                ch.step(dve.tensor_tensor_scan(rank[:], m, m, before[:, bass.ds(b, 1)], ALU.add, ALU.bypass))
                ch.step(dve.copy_predicated(pos_f[:], m.bitcast(U16), rank[:]))
            ch.leave(NT // 2)
        ch.step(dve.tensor_copy(pos[:], pos_f[:]))

    section.clear()

    s01 = ExitStack()
    pair = sbuf(s01, "pair", [P, EC * 2], I32)
    pos_src = sbuf(s01, "pos_src", [P, EC], I32)
    first_dst = sbuf(s01, "first_dst", [P, NT])
    hi_src = sbuf(s01, "hi_src", [P, EC], BF16)
    lo_src = sbuf(s01, "lo_src", [P, EC], BF16)
    hi_dst = sbuf(s01, "hi_dst", [P, EC], BF16)
    lo_dst = sbuf(s01, "lo_dst", [P, EC], BF16)
    iota_b = sbuf(s01, "iota_b", [128, 128], BF16)

    with ExitStack() as ctx:
        src_i = sbuf(ctx, "src_i", [P, EC], I32)
        dst_i = sbuf(ctx, "dst_i", [P, EC], I32)
        src_f = XT[0:P, 0 * EC:1 * EC]
        dst_f = XT[0:P, 1 * EC:2 * EC]
        pos_f = XT[0:P, 2 * EC:3 * EC]
        rank = XT[0:P, 3 * EC:4 * EC]
        mask = sbuf(ctx, "mask", [P, 2 * EC], BF16)
        free_i = sbuf(ctx, "free_i", [128, 128], I32)
        part_i = sbuf(ctx, "part_i", [128, 1], I32)
        fblk_i = sbuf(ctx, "fblk_i", [128, 128], I32)
        pblk_i = sbuf(ctx, "pblk_i", [128, 1], I32)
        fblk_f = sbuf(ctx, "fblk_f", [128, 128])
        small = sbuf(ctx, "small", [128, 8])
        win_i = sbuf(ctx, "win_i", [128, NW2], I32)
        win_f = sbuf(ctx, "win_f", [128, NW2])
        cum = sbuf(ctx, "cum", [128, NW2])
        row = sbuf(ctx, "row", [1, NW2])
        cnt = sbuf(ctx, "cnt", [P, NT])
        tot = sbuf(ctx, "tot", [P, NT])
        first = sbuf(ctx, "first", [P, NT])
        first_src = sbuf(ctx, "first_src", [P, NT])
        col = sbuf(ctx, "col", [64, 8])
        col_i = sbuf(ctx, "col_i", [64, 2], I32)
        pad = sbuf(ctx, "pad", [128, 4 * (ED + 1)])
        pad_i = sbuf(ctx, "pad_i", [128, 2 * W2 // 128], I32)
        next_i = sbuf(ctx, "next_i", [P, 1], I32)
        next_f = sbuf(ctx, "next_f", [P, 1])
        falls = sbuf(ctx, "falls", [P, 2])
        ps = psum(ctx, "ps_sort", 4)

        ids_in, x_in, iotas, pads, consts = (sem(s) for s in ("ids_in", "x_in", "iotas", "pads", "consts"))
        falls_ready, falls_summed = sem("falls_ready"), sem("falls_summed")
        counted, summed, pads_set = sem("counted"), sem("summed"), sem("pads_set")
        block = ctx.enter_context(nc.Block())

        @block.sync
        def _(sp):
            sp.dma_start(src_i[:], a["src"].rearrange("(p c) -> p c", c=EC)).then_inc(ids_in, 16)
            sp.dma_start(dst_i[:], a["dst"].rearrange("(p c) -> p c", c=EC)).then_inc(ids_in, 16)
            dst2 = a["dst"].rearrange("(p c) -> p c", c=EC)
            sp.wait_ge(pads_set, 5)
            with nc.allow_non_contiguous_dma(reason="one number a partition"):
                sp.dma_start(next_i[0:P - 1, :], dst2[1:P, 0:1]).then_inc(ids_in, 16)
            sp.dma_start(R[:].rearrange("p (t d) -> p t d", d=TS),
                         a["x"].rearrange("(t p) d -> p t d", p=P)).then_inc(x_in, 16)
            sp.dma_start(rows_d[E:E + W1, :].rearrange("(p r) c -> p (r c)", p=128), pad[:]).then_inc(pads, 16)
            sp.dma_start(pairs_d[E:E + W2, :].rearrange("(p r) c -> p (r c)", p=128), pad_i[:]).then_inc(pads, 16)
            sp.wait_ge(pads, 32)
            sp.wait_ge(x_in, 16)

        @block.gpsimd
        def _(pool):
            pool.iota(free_i[:], pattern=[[1, 128]], base=0, channel_multiplier=0).then_inc(iotas, 1)
            pool.iota(part_i[:], pattern=[[0, 1]], base=0, channel_multiplier=1).then_inc(iotas, 1)
            pool.iota(fblk_i[:], pattern=[[1, 4], [0, 32]], base=0, channel_multiplier=0).then_inc(iotas, 1)
            pool.iota(win_i[:], pattern=[[1, NW2]], base=0, channel_multiplier=0).then_inc(iotas, 1)
            pool.memset(pad[:], 0.0).then_inc(pads_set, 1)
            pool.memset(pad_i[:], 0).then_inc(pads_set, 1)
            pool.memset(next_i[:], PAD_KEY).then_inc(pads_set, 1)
            pool.wait_ge(pads_set, 3)
            pool.memset(pad[:].rearrange("p (r c) -> p r c", c=ED + 1)[:, :, ED:], float(PAD_KEY)).then_inc(pads_set, 1)
            pool.memset(pad_i[:].rearrange("p (r c) -> p r c", c=2)[:, :, 1:], PAD_KEY).then_inc(pads_set, 1)
            pool.memset(ones[:], 1.0).then_inc(iotas, 1)

        def sort_dve(dve, ch, hi, pos, width, tab_b, tab_s, which, first2, rank_now):
            shift = width.bit_length() - 1
            nw = tab_b.shape[1]
            with dve.Fori(0, NT // 2) as i:
                ch.enter(i, 2)
                for u in range(2):
                    b = i * 2 + u
                    ch.step(dve.tensor_scalar(mask[:, u * EC:(u + 1) * EC], hi[:], iota_f[0:P, bass.ds(b, 1)], 0.0,
                                              ALU.is_equal, ALU.add, accum_out=cnt[:, bass.ds(b, 1)]))
                ch.leave(NT // 2)
            ch.step(dve.tensor_copy(tot[:], cnt[:]))
            dve.sem_inc(counted)
            dve.wait_ge(summed, 1 + 3 * which)
            ch.step(dve.tensor_copy(tot[:], ps[0:P, 0, 64:64 + NT]))
            ch.step(dve.tensor_tensor_scan(first[:], tot[:], tot[:], 0.0, ALU.add, ALU.bypass))
            ch.step(dve.tensor_tensor(first2[:], first[:], tot[:], ALU.subtract))
            ch.step(dve.tensor_tensor(first[:], first2[:], ps[0:P, 0, 0:NT], ALU.add))
            ch.step(dve.tensor_scalar(first2[:], first[:], -1.0, None, ALU.add))
            ch.step(dve.tensor_copy(col[0:NT, 0:1], ps[0:NT, 0, 128:129]))
            ch.step(dve.tensor_scalar(col_i[0:NT, 0:1], col[0:NT, 0:1], float(width - 1), None, ALU.add))
            ch.step(dve.tensor_scalar(col_i[0:NT, 1:2], col_i[0:NT, 0:1], shift, None, ALU.arith_shift_right))
            ch.step(dve.tensor_copy(col[0:NT, 1:2], col_i[0:NT, 1:2]))
            ch.step(dve.scalar_tensor_tensor(out=col[0:NT, 2:3], in0=col[0:NT, 1:2], scalar=-float(width),
                                             in1=col[0:NT, 0:1], op0=ALU.mult, op1=ALU.add))
            dve.sem_inc(counted)
            dve.wait_ge(summed, 2 + 3 * which)
            ch.step(dve.tensor_copy(col[0:NT, 3:4], ps[0:NT, 0, 129:130]))
            ch.step(dve.tensor_scalar(cum[0:NT, 0:nw], win_f[0:NT, 0:nw], col[0:NT, 3:4], None, ALU.is_ge))
            dve.sem_inc(counted)
            dve.wait_ge(summed, 3 + 3 * which)
            h = nw // 2
            for q in range(2):
                ch.step(dve.tensor_copy(tab_b[:, q * h:(q + 1) * h], ps[0:1, 1, 0:h] if q == 0 else ps[0:1, 2, 0:h]))
            for q, bank in ((0, 3), (1, 0)):
                ch.step(dve.scalar_tensor_tensor(out=row[:, q * h:(q + 1) * h], in0=win_f[0:1, q * h:(q + 1) * h],
                                                 scalar=float(width), in1=ps[0:1, bank, 0:h], op0=ALU.mult, op1=ALU.add))
            ch.step(dve.tensor_scalar(tab_s[:], row[:, 0:nw], float(E), None, ALU.min))
            if rank_now:
                rank_edges(dve, ch, hi, first2, mask, rank, pos_f, pos)

        @block.vector
        def _(dve):
            ch = chain("dve", dve)
            dve.wait_ge(iotas, 5)
            ch.step(dve.tensor_copy(iota_f[:], free_i[:]))
            ch.step(dve.tensor_copy(iota_b[:], free_i[:]))
            ch.step(dve.tensor_copy(small[:, 0:1], part_i[:]))
            ch.step(dve.tensor_scalar(ident[:], iota_f[:], small[:, 0:1], None, ALU.is_equal))
            ch.step(dve.tensor_scalar(lower[:], iota_f[:], small[:, 0:1], None, ALU.is_gt))
            ch.step(dve.tensor_scalar(pblk_i[:], part_i[:], 5, None, ALU.arith_shift_right))
            ch.step(dve.tensor_copy(small[:, 1:2], pblk_i[:]))
            ch.step(dve.tensor_copy(fblk_f[:], fblk_i[:]))
            ch.step(dve.tensor_scalar(blockdiag[:], fblk_f[:], small[:, 1:2], None, ALU.is_equal))
            ch.step(dve.tensor_copy(win_f[:], win_i[:]))
            ch.step(dve.memset(pos_f[:], 0.0))
            dve.wait_ge(ids_in, 48)
            for ids, keys, hi, lo, word in ((src_i, src_f, hi_src, lo_src, 0), (dst_i, dst_f, hi_dst, lo_dst, 1)):
                ch.step(dve.tensor_copy(keys[:], ids[:]))
                ch.step(dve.tensor_copy(pair[:].rearrange("p (c w) -> p c w", w=2)[:, :, word], ids[:]))
                ch.step(dve.tensor_scalar(rank[:], keys[:], -float(P // 2), 1.0 / P, ALU.add, ALU.mult))
                ch.step(dve.tensor_scalar(hi[:], rank[:], MAGIC, -MAGIC, ALU.add, ALU.add))
                ch.step(dve.scalar_tensor_tensor(out=lo[:], in0=hi[:], scalar=-float(P), in1=keys[:],
                                                 op0=ALU.mult, op1=ALU.add))
            ch.step(dve.tensor_tensor(rank[:, 0:EC - 1], dst_f[:, 0:EC - 1], dst_f[:, 1:EC], ALU.is_gt))
            ch.step(dve.tensor_reduce(falls[:, 0:1], rank[:, 0:EC - 1], AX.X, ALU.add))
            ch.step(dve.tensor_copy(next_f[:], next_i[:]))
            ch.step(dve.tensor_tensor(falls[:, 1:2], dst_f[:, EC - 1:EC], next_f[:], ALU.is_gt))
            ch.step(dve.tensor_tensor(falls[:, 0:1], falls[:, 0:1], falls[:, 1:2], ALU.add))
            dve.sem_inc(falls_ready)
            dve.wait_ge(falls_summed, 1)
            ch.step(dve.tensor_copy(unsorted[:], ps[0:1, 3, 0:1]))
            sort_dve(dve, ch, hi_src, pos_src, W1, win1_b, win1_s, 0, first_src, True)
            sort_dve(dve, ch, hi_dst, None, W2, win2_b, win2_s, 1, first_dst, False)

        @block.tensor
        def _(pe):
            pe.wait_ge(falls_ready, 1)
            pe.matmul(ps[0:1, 3, 0:1], falls[:, 0:1], ones[0:P, 0:1], start=True, stop=True).then_inc(falls_summed, 1)
            for which, nw in ((0, NW1), (1, NW2)):
                h = nw // 2
                pe.wait_ge(counted, 1 + 3 * which)
                pe.matmul(ps[0:P, 0, 0:NT], lower[0:P, 0:P], cnt[:], start=True, stop=True)
                pe.matmul(ps[0:P, 0, 64:64 + NT], ones[0:P, 0:P], cnt[:], start=True, stop=True)
                pe.matmul(ps[0:NT, 0, 128:129], cnt[:], ones[0:P, 0:1], start=True, stop=True).then_inc(summed, 1)
                pe.wait_ge(counted, 2 + 3 * which)
                pe.matmul(ps[0:NT, 0, 129:130], lower[0:NT, 0:NT], col[0:NT, 1:2], start=True, stop=False)
                pe.matmul(ps[0:NT, 0, 129:130], ident[0:NT, 0:NT], col[0:NT, 1:2], start=False, stop=True).then_inc(summed, 1)
                pe.wait_ge(counted, 3 + 3 * which)
                for q, bank in ((0, 1), (1, 2)):
                    pe.matmul(ps[0:1, bank, 0:h], ones[0:NT, 0:1], cum[0:NT, q * h:(q + 1) * h], start=True, stop=True)
                for q, bank in ((0, 3), (1, 0)):
                    mm = pe.matmul(ps[0:1, bank, 0:h], col[0:NT, 2:3], cum[0:NT, q * h:(q + 1) * h], start=True, stop=True)
                mm.then_inc(summed, 1)

    def tiles(eng, body, ch=None, per=0, n=NT):
        body(0, 0, 0)
        body(1, 1, 0)
        with eng.Fori(1, n // 2) as i:
            if ch:
                ch.base -= per
                ch.enter(i, per)
            body(2 * i, 0, i)
            body(2 * i + 1, 1, i)
        if ch:
            ch.base += per
            ch.leave(n // 2 - 1)

    def later(t):
        return not isinstance(t, int) or t >= 2

    def XTt(t, k):
        return XT[:, bass.ds(t * TS + k * P, P)]

    with ExitStack() as ctx:
        ring = sbuf(ctx, "ring", [P, 2 * 8 * (ED + 1)])
        stage = sbuf(ctx, "stage", [P, 2 * 8], I32)
        w_qkv = sbuf(ctx, "w_qkv", [128, 2 * 768])
        w_out = sbuf(ctx, "w_out", [128, 2 * D])
        w_mix = sbuf(ctx, "w_mix", [128, 2 * D])
        wcv = sbuf(ctx, "wcv", [P, 4 * D])
        nvec = sbuf(ctx, "nvec", [P, 2 * NT])
        b_sum = sbuf(ctx, "b_sum", [P, D])
        gamma = sbuf(ctx, "gamma", [P, D])
        lo1 = sbuf(ctx, "lo1", [P, 2 * 8 * P], BF16)
        hi1 = sbuf(ctx, "hi1", [P, 2 * 8 * NT], BF16)
        deg_out = sbuf(ctx, "deg_out", [P, NT])
        z_idx = sbuf(ctx, "z_idx", [P, NT * 2], I32)
        z_stage = sbuf(ctx, "z_stage", [P, 4], I32)
        z_rows = sbuf(ctx, "z_rows", [P, 2 * 2 * D])
        xn = sbuf(ctx, "xn", [P, 2 * D])
        xs = sbuf(ctx, "xs", [128, 2 * TS])
        cv = sbuf(ctx, "cv", [P, 2 * 2 * D])
        kmax_t = sbuf(ctx, "kmax_t", [128, NT * 2])
        kmax = sbuf(ctx, "kmax", [128, 2])
        neg_kmax = sbuf(ctx, "neg_kmax", [1, D])
        k_exp = sbuf(ctx, "k_exp", [P, 2 * D])
        v_one = sbuf(ctx, "v_one", [P, 2 * 2 * 129])
        q_sb = sbuf(ctx, "q_sb", [P, 2 * D])
        q_m = sbuf(ctx, "q_m", [P, 2 * HEADS])
        q_s = sbuf(ctx, "q_s", [P, 2 * HEADS])
        rsum = sbuf(ctx, "rsum", [128, 2])
        ctxn = sbuf(ctx, "ctxn", [128, 2 * 128])
        ctxt = sbuf(ctx, "ctxt", [128, 2 * 128])
        mixed = sbuf(ctx, "mixed", [P, 2 * D])
        pq = psum(ctx, "pq", 2)
        pkv = psum(ctx, "pkv", 2)
        ptr = psum(ctx, "ptr", 2)
        pctx = psum(ctx, "pctx", 1)
        phist = psum(ctx, "phist", 1)

        weights_in, mix_w_in, v_ones = sem("weights_in"), sem("mix_w_in"), sem("v_ones")
        ring_in = [sem("ring_in0"), sem("ring_in1")]
        ring_out = [sem("ring_out0"), sem("ring_out1")]
        half_staged = sem("half_staged")
        onehot_ready, counted_to, degrees_ready = sem("onehot_ready"), sem("counted_to"), sem("degrees_ready")
        xn_ready, xt_ready, xt_stored = sem("xn_ready"), sem("xt_ready"), sem("xt_stored")
        cv_ready, sg_ready = sem("cv_ready"), sem("sg_ready")
        kt_ready, kt_read, kmax_ready, kmax_row, kmax_row_in = (sem(s) for s in ("kt_ready", "kt_read", "kmax_ready", "kmax_row", "kmax_row_in"))
        qkv_ready, kv_stored, qs_ready, qexp_ready, qn_ready, qt_ready, qt_stored, ctx_done = (
            sem(s) for s in ("qkv_ready", "kv_stored", "qs_ready", "qexp_ready", "qn_ready", "qt_ready", "qt_stored", "ctx_done"))
        xs_ready, qs2_ready = sem("xs_ready"), sem("qs2_ready")
        ctxn_ready, ctxt_ready, ctxt_in, wmix_ready, wmix_in = (sem(s) for s in ("ctxn_ready", "ctxt_ready", "ctxt_in", "wmix_ready", "wmix_in"))
        o_ready, o_read, o_stats = sem("o_ready"), sem("o_read"), sem("o_stats")
        z_in_ = [sem("z_in0"), sem("z_in1")]
        z_used = sem("z_used")
        block = ctx.enter_context(nc.Block())
        attr = a["edge_attr_128"].rearrange("(p c) d -> p c d", c=EC)
        ring4 = ring[:].rearrange("p (h c w) -> p h c w", h=2, c=8)
        pair_w = pair[:].rearrange("p (c w) -> p c w", w=2)

        @block.sync
        def _(sp):
            sp.dma_start(w_qkv[:].rearrange("p (k n) -> p k n", k=2), a["L0_mix_Wqkv"].rearrange("(k p) n -> p k n", p=128)).then_inc(mix_w_in, 16)
            sp.dma_start(w_out[:].rearrange("p (k n) -> p k n", k=2), a["L0_mix_Wout"].rearrange("(k p) n -> p k n", p=128)).then_inc(mix_w_in, 16)
            for j, name in enumerate(("W_cent", "b_cent", "W_vor", "b_vor")):
                v = a["L0_gnn_" + name]
                v = v.rearrange("a d -> (a d)") if len(v.shape) == 2 else v
                sp.dma_start(wcv[:, j * D:(j + 1) * D], bcast_rows(v, P)).then_inc(weights_in, 16)
            sp.dma_start(b_sum[:], bcast_rows(a["L0_gnn_b_sum"], P)).then_inc(weights_in, 16)
            sp.dma_start(gamma[:], bcast_rows(a["L0_mix_gamma"], P)).then_inc(weights_in, 16)
            with nc.allow_non_contiguous_dma(reason="one number a node"):
                for j, name in enumerate(("node_vec1_n2", "node_vec1")):
                    sp.dma_start(nvec[:, j * NT:(j + 1) * NT], a[name].rearrange("(t p) a -> p (t a)", p=P)).then_inc(weights_in, 16)

            def load(i):
                for h in range(2):
                    if not isinstance(i, int):
                        at(sp, ring_out[h], i * 128, passed["sp"])
                    sp.dma_start(ring4[:, h, :, 0:ED], attr[:, bass.ds(i * 16 + h * 8, 8), :]).then_inc(ring_in[h], 16)

            load(0)
            with sp.Fori(1, EC // 16) as i:
                load(i)

        @block.gpsimd
        def _(pool):
            ch = chain("pool", pool)
            pool.memset(v_one[:], 1.0).then_inc(v_ones, 1)

            def stage_half(i, h):
                at(pool, ring_in[h], i * 16 + 16, passed["pool"])
                pool.tensor_copy(ring4[:, h, :, ED], pair_w[:, bass.ds(i * 16 + h * 8, 8), 0]).then_inc(half_staged, 1)
                pool.tensor_copy(stage[:, h * 8:h * 8 + 8], pos_src[:, bass.ds(i * 16 + h * 8, 8)]).then_inc(half_staged, 1)

            def scatter_half(i, h, stage_next):
                at(pool, half_staged, i * 4 + 2 * h + 2, passed["pool"])
                for j in range(8):
                    if j == 5:
                        stage_next()
                    pool.indirect_dma_start(rows_d, bass.IndirectOffsetOnAxis(ap=stage[:, h * 8 + j:h * 8 + j + 1].bitcast(U32), axis=0),
                                            ring4[:, h, j, :], None).then_inc(ring_out[h], 16)

            stage_half(0, 0)
            with pool.Fori(0, EC // 16 - 1) as i:
                scatter_half(i, 0, lambda: stage_half(i, 1))
                scatter_half(i, 1, lambda: stage_half(i + 1, 0))
            scatter_half(EC // 16 - 1, 0, lambda: stage_half(EC // 16 - 1, 1))
            scatter_half(EC // 16 - 1, 1, lambda: None)
            for h in range(2):
                pool.wait_ge(ring_out[h], 128 * (EC // 16))

            pool.wait_ge(degrees_ready, 1)

            def gather_z(t, u, i):
                if later(t):
                    at(pool, z_used, t - 1, passed["pool"])
                ch.step(pool.tensor_copy(z_stage[:, 2 * u:2 * u + 2], z_idx[:, bass.ds(t * 2, 2)]))
                for k, name in enumerate(("L0_gnn_z_in", "L0_gnn_z_out")):
                    pool.indirect_dma_start(z_rows[:, (2 * u + k) * D:(2 * u + k + 1) * D], None, a[name],
                                            bass.IndirectOffsetOnAxis(ap=z_stage[:, 2 * u + k:2 * u + k + 1].bitcast(U32), axis=0)
                                            ).then_inc(z_in_[u], 16)

            tiles(pool, gather_z, ch, 2)

        @block.vector
        def _(dve):
            ch = chain("dve", dve)

            def onehots(lo, hi, which):
                def body(t, u, i):
                    if later(t) or which:
                        at(dve, counted_to, t - 1 + which * (EC // 8), passed["dve"])
                    dve.tensor_tensor(lo1[:, u * 8 * P:(u + 1) * 8 * P].rearrange("p (c n) -> p c n", c=8),
                                      iota_b[0:P, 0:P].unsqueeze(1).to_broadcast([P, 8, P]),
                                      lo[:, bass.ds(t * 8, 8)].unsqueeze(2).to_broadcast([P, 8, P]), ALU.is_equal)
                    dve.tensor_tensor(hi1[:, u * 8 * NT:(u + 1) * 8 * NT].rearrange("p (c n) -> p c n", c=8),
                                      iota_b[0:P, 0:NT].unsqueeze(1).to_broadcast([P, 8, NT]),
                                      hi[:, bass.ds(t * 8, 8)].unsqueeze(2).to_broadcast([P, 8, NT]), ALU.is_equal).then_inc(onehot_ready, 1)
                tiles(dve, body, n=EC // 8)

            onehots(lo_src, hi_src, 0)
            onehots(lo_dst, hi_dst, 1)
            dve.wait_ge(counted_to, 2 * (EC // 8))
            ch.step(dve.tensor_copy(deg_out[:], phist[0:P, 0, 0:NT]))
            ch.step(dve.tensor_copy(deg_in[:], phist[0:P, 0, 64:64 + NT]))
            z3 = z_idx[:].rearrange("p (t k) -> p t k", k=2)
            ch.step(dve.tensor_scalar(z3[:, :, 0], deg_in[:], float(MAX_DEGREE - 1), None, ALU.min))
            ch.step(dve.tensor_scalar(z3[:, :, 1], deg_out[:], float(MAX_DEGREE - 1), None, ALU.min))
            dve.sem_inc(degrees_ready)

            layer_stats(dve, ch, Rt)
            dve.wait_ge(weights_in, 128)

            def add_terms(t, u):
                at(dve, sg_ready, t + 1, passed["dve"])
                for k in range(2):
                    ch.step(dve.tensor_tensor(Rt(t), Rt(t), cv[:, (2 * u + k) * D:(2 * u + k + 1) * D], ALU.add))

            def norm(t, u, i):
                if later(t):
                    at(dve, xt_ready, t - 1, passed["dve"])
                    add_terms(t - 2, u)
                x_u = xn[:, u * D:(u + 1) * D]
                dve.tensor_scalar(x_u, Rt(t), mean[:, bass.ds(t, 1)], rstd[:, bass.ds(t, 1)], ALU.subtract, ALU.mult).then_inc(xn_ready, 1)
                at(dve, xn_ready, t + 1, passed["dve"])
                ch.step(dve.tensor_tensor(Rt(t), Rt(t), x_u, ALU.add))
                for k in range(2):
                    ins = dve.scalar_tensor_tensor(out=cv[:, (2 * u + k) * D:(2 * u + k + 1) * D], in0=wcv[:, 2 * k * D:(2 * k + 1) * D],
                                                   scalar=nvec[:, bass.ds(t + k * NT, 1)], in1=wcv[:, (2 * k + 1) * D:(2 * k + 2) * D],
                                                   op0=ALU.mult, op1=ALU.add)
                ins.then_inc(cv_ready, 1)

            tiles(dve, norm, ch, 6)
            add_terms(NT - 2, 0)
            add_terms(NT - 1, 1)

            def max_k(t, u, i):
                at(dve, kt_ready, t + 1, passed["dve"])
                dve.tensor_reduce(kmax_t[:, bass.ds(t * 2, 2)], pkv[:, u, 0:2 * P].rearrange("p (k n) -> p k n", k=2), AX.X, ALU.max).then_inc(kt_read, 1)

            tiles(dve, max_k)
            dve.wait_ge(kt_read, NT)
            dve.tensor_reduce(kmax[:], kmax_t[:].rearrange("p (t k) -> p k t", k=2), AX.X, ALU.max).then_inc(kmax_ready, 1)
            dve.wait_ge(kmax_row, 1)
            dve.tensor_scalar(neg_kmax[:], pctx[0:1, 0, 0:D], -1.0, None, ALU.mult).then_inc(kmax_row_in, 1)

            def q_softmax(t, u, i):
                at(dve, qkv_ready, t + 1, passed["dve"])
                q3 = pq[0:P, u, 0:D].rearrange("p (h d) -> p h d", h=HEADS)
                s3 = q_sb[:, u * D:(u + 1) * D].rearrange("p (h d) -> p h d", h=HEADS)
                qm, qs = q_m[:, u * HEADS:(u + 1) * HEADS], q_s[:, u * HEADS:(u + 1) * HEADS]
                ch.step(dve.tensor_reduce(qm, q3, AX.X, ALU.max))
                if later(t):
                    at(dve, qt_ready, t - 1, passed["dve"])
                dve.tensor_tensor(s3, q3, qm.unsqueeze(2).to_broadcast([P, HEADS, HD]), ALU.subtract).then_inc(qs_ready, 1)
                at(dve, qexp_ready, t + 1, passed["dve"])
                ch.step(dve.tensor_reduce(qs, s3, AX.X, ALU.add))
                ch.step(dve.reciprocal(qs, qs))
                dve.tensor_tensor(s3, s3, qs.unsqueeze(2).to_broadcast([P, HEADS, HD]), ALU.mult).then_inc(qn_ready, 1)

            tiles(dve, q_softmax, ch, 6)
            dve.wait_ge(ctx_done, NT)
            for m in range(2):
                ch.step(dve.reciprocal(rsum[:, m:m + 1], pctx[:, 0, 129 * m + 128:129 * m + 129]))
                ch.step(dve.tensor_scalar(ctxn[:, m * 128:(m + 1) * 128], pctx[:, 0, 129 * m:129 * m + 128], rsum[:, m:m + 1], None, ALU.mult))
                dve.tensor_tensor(ctxn[:, m * 128:(m + 1) * 128], ctxn[:, m * 128:(m + 1) * 128], blockdiag[:], ALU.mult).then_inc(ctxn_ready, 1)
            dve.wait_ge(ctxt_ready, 2)
            for m in range(2):
                dve.tensor_copy(ctxt[:, m * 128:(m + 1) * 128], ptr[:, m, 0:128]).then_inc(ctxt_in, 1)
            dve.wait_ge(wmix_ready, 2)
            for m in range(2):
                dve.tensor_scalar(w_mix[:, m * D:(m + 1) * D], pq[:, m, 0:D], float(HD) ** -0.5, None, ALU.mult).then_inc(wmix_in, 1)

            stats_target[0] += NT

            def out_stats(t, u, i):
                at(dve, o_read, t + 1, passed["dve"])
                dve.bn_stats(stats[:, bass.ds(t * 6, 6)], XT[0:P, bass.ds(t * TS, D)]).then_inc(stats_done, 1)

            tiles(dve, out_stats)
            dve.wait_ge(stats_done, stats_target[0])
            finish_stats_dve(dve, ch)

            def add_mix(t, u, i):
                m_u = mixed[:, u * D:(u + 1) * D]
                ch.step(dve.tensor_scalar(m_u, XT[0:P, bass.ds(t * TS, D)], mean[:, bass.ds(t, 1)], rstd[:, bass.ds(t, 1)], ALU.subtract, ALU.mult))
                ch.step(dve.tensor_tensor(m_u, m_u, gamma[:], ALU.mult))
                ch.step(dve.tensor_tensor(Rt(t), Rt(t), m_u, ALU.add))
                ch.step(dve.scalar_tensor_tensor(out=Rt(t), in0=b_sum[:], scalar=deg_out[:, bass.ds(t, 1)], in1=Rt(t), op0=ALU.mult, op1=ALU.add))
                at(dve, z_in_[u], i * 32 + 32, passed["dve"])
                for k in range(2):
                    ch.step(dve.tensor_tensor(Rt(t), Rt(t), z_rows[:, (2 * u + k) * D:(2 * u + k + 1) * D], ALU.add))
                dve.sem_inc(z_used)

            tiles(dve, add_mix, ch, 12)

        @block.scalar
        def _(act):
            finish_stats_act(act)

            def store_xt(t, u, i):
                at(act, cv_ready, t + 1, passed["act"])
                act.activation(cv[:, u * 2 * D:(u + 1) * 2 * D], cv[:, u * 2 * D:(u + 1) * 2 * D], ACT.Sigmoid).then_inc(sg_ready, 1)
                at(act, xt_ready, t + 1, passed["act"])
                act.copy(XT[:, bass.ds(t * TS, 2 * P)], ptr[:, u, 0:2 * P]).then_inc(xt_stored, 1)

            tiles(act, store_xt)
            act.wait_ge(v_ones, 1)

            def store_qt(t, u):
                at(act, qt_ready, t + 1, passed["act"])
                act.copy(XT[:, bass.ds(t * TS, 2 * P)], ptr[:, u, 0:2 * P]).then_inc(qt_stored, 1)

            def exps(t, u, i):
                if later(t):
                    at(act, qkv_ready, t - 1, passed["act"])
                act.copy(xs[:, u * TS:u * TS + 2 * P], XT[:, bass.ds(t * TS, 2 * P)]).then_inc(xs_ready, 1)
                at(act, qkv_ready, t + 1, passed["act"])
                if later(t):
                    at(act, ctx_done, t - 1, passed["act"])
                act.activation(k_exp[:, u * D:(u + 1) * D], pkv[0:P, u, 0:D], ACT.Exp).then_inc(kv_stored, 1)
                act.copy(v_one[:, u * 258:(u + 1) * 258].rearrange("p (m c) -> p m c", m=2)[:, :, 0:128],
                         pkv[0:P, u, D:2 * D].rearrange("p (m c) -> p m c", m=2)).then_inc(kv_stored, 1)
                at(act, qs_ready, t + 1, passed["act"])
                act.activation(q_sb[:, u * D:(u + 1) * D], q_sb[:, u * D:(u + 1) * D], ACT.Exp).then_inc(qexp_ready, 1)
                if not isinstance(t, int) or t >= 1:
                    store_qt(t - 1, 1 - u)

            tiles(act, exps)
            store_qt(NT - 1, 1)

            def store_out(t, u, i):
                if later(t):
                    at(act, o_ready, t - 1, passed["act"])
                act.copy(xs[:, u * TS:u * TS + 2 * P], XT[:, bass.ds(t * TS, 2 * P)]).then_inc(qs2_ready, 1)
                at(act, o_ready, t + 1, passed["act"])
                act.copy(XT[0:P, bass.ds(t * TS, D)], pq[0:P, u, 0:D]).then_inc(o_read, 1)

            tiles(act, store_out)
            finish_stats_act(act)

        @block.tensor
        def _(pe):
            def count(which):
                def body(t, u, i):
                    at(pe, onehot_ready, t + 1 + which * (EC // 8), passed["pe"])
                    for j in range(8):
                        mm = pe.matmul(phist[0:P, 0, which * 64:which * 64 + NT], lo1[:, (u * 8 + j) * P:(u * 8 + j + 1) * P],
                                       hi1[:, (u * 8 + j) * NT:(u * 8 + j + 1) * NT],
                                       start=(isinstance(t, int) and t == 0 and j == 0), stop=True, skip_group_check=True)
                    mm.then_inc(counted_to, 1)
                tiles(pe, body, n=EC // 8)

            count(0)
            count(1)

            def transpose_x(t, u, i):
                at(pe, xn_ready, t + 1, passed["pe"])
                if later(t):
                    at(pe, xt_stored, t - 1, passed["pe"])
                for k in range(2):
                    mm = pe.transpose(ptr[:, u, k * P:(k + 1) * P], xn[:, u * D + k * 128:u * D + (k + 1) * 128], ident[0:P, 0:P])
                mm.then_inc(xt_ready, 1)

            tiles(pe, transpose_x)
            pe.wait_ge(mix_w_in, 32)
            pe.wait_ge(xt_stored, NT)

            def k_transposed(t, u, i):
                if later(t):
                    at(pe, kt_read, t - 1, passed["pe"])
                for m in range(2):
                    for k in range(2):
                        mm = pe.matmul(pkv[:, u, m * P:(m + 1) * P], w_qkv[:, k * 768 + D + m * 128:k * 768 + D + (m + 1) * 128],
                                       XTt(t, k), start=(k == 0), stop=(k == 1))
                mm.then_inc(kt_ready, 1)

            tiles(pe, k_transposed)
            pe.wait_ge(kmax_ready, 1)
            for m in range(2):
                mm = pe.matmul(pctx[0:1, 0, m * 128:(m + 1) * 128], kmax[:, m:m + 1], ident[:], start=True, stop=True)
            mm.then_inc(kmax_row, 1)
            pe.wait_ge(kmax_row_in, 1)

            def context(t, u):
                at(pe, kv_stored, 2 * t + 2, passed["pe"])
                first = isinstance(t, int) and t == 0
                for m in range(2):
                    mm = pe.matmul(pctx[:, 0, m * 129:(m + 1) * 129], k_exp[:, u * D + m * 128:u * D + (m + 1) * 128],
                                   v_one[:, u * 258 + m * 129:u * 258 + (m + 1) * 129], start=first and m == 0, stop=True, skip_group_check=True)
                mm.then_inc(ctx_done, 1)
                at(pe, qn_ready, t + 1, passed["pe"])
                if later(t):
                    at(pe, qt_stored, t - 1, passed["pe"])
                for k in range(2):
                    mm = pe.transpose(ptr[:, u, k * P:(k + 1) * P], q_sb[:, u * D + k * 128:u * D + (k + 1) * 128], ident[0:P, 0:P])
                mm.then_inc(qt_ready, 1)

            def qkv(t, u, i):
                at(pe, xs_ready, t + 1, passed["pe"])
                if later(t):
                    at(pe, kv_stored, 2 * t - 2, passed["pe"])
                    at(pe, qs_ready, t - 1, passed["pe"])
                for k in range(2):
                    pe.matmul(pq[0:P, u, 0:D], xs[:, u * TS + k * P:u * TS + (k + 1) * P], w_qkv[:, k * 768:k * 768 + D], start=(k == 0), stop=(k == 1))
                for k in range(2):
                    pe.matmul(pkv[0:P, u, 0:D], xs[:, u * TS + k * P:u * TS + (k + 1) * P], w_qkv[:, k * 768 + D:k * 768 + 2 * D], start=(k == 0), stop=False)
                pe.matmul(pkv[0:P, u, 0:D], ones[0:1, 0:P], neg_kmax[:], start=False, stop=True)
                for k in range(2):
                    mm = pe.matmul(pkv[0:P, u, D:2 * D], xs[:, u * TS + k * P:u * TS + (k + 1) * P], w_qkv[:, k * 768 + 2 * D:k * 768 + 3 * D], start=(k == 0), stop=(k == 1))
                mm.then_inc(qkv_ready, 1)
                if not isinstance(t, int) or t >= 1:
                    context(t - 1, 1 - u)

            tiles(pe, qkv)
            context(NT - 1, 1)
            pe.wait_ge(ctxn_ready, 2)
            pe.wait_ge(qt_stored, NT)
            for m in range(2):
                pe.transpose(ptr[:, m, 0:128], ctxn[:, m * 128:(m + 1) * 128], ident[:]).then_inc(ctxt_ready, 1)
            pe.wait_ge(ctxt_in, 2)
            for m in range(2):
                pe.matmul(pq[:, m, 0:D], ctxt[:, m * 128:(m + 1) * 128], w_out[:, m * D:(m + 1) * D], start=True, stop=True).then_inc(wmix_ready, 1)
            pe.wait_ge(wmix_in, 2)

            def attend(t, u, i):
                at(pe, qs2_ready, t + 1, passed["pe"])
                if later(t):
                    at(pe, o_read, t - 1, passed["pe"])
                for k in range(2):
                    mm = pe.matmul(pq[0:P, u, 0:D], xs[:, u * TS + k * P:u * TS + (k + 1) * P], w_mix[:, k * D:(k + 1) * D], start=(k == 0), stop=(k == 1))
                mm.then_inc(o_ready, 1)

            tiles(pe, attend)

    with s01, ExitStack() as ctx:
        pos_dst = sbuf(ctx, "pos_dst", [P, EC], I32)
        mask = sbuf(ctx, "mask2", [P, 2 * EC], BF16)
        rank, pos_f = XT[0:P, 0:EC], XT[0:P, EC:2 * EC]
        stage = sbuf(ctx, "stage2", [P, 2 * 8], I32)
        pstage = sbuf(ctx, "pstage", [P, 2 * 16], I32)
        pair_out = [sem("pair_out0"), sem("pair_out1")]
        pairs_out, dst_ranked, rank_steps, stage_steps = (sem(s) for s in ("pairs_out", "dst_ranked", "rank_steps", "stage_steps"))
        block = ctx.enter_context(nc.Block())

        @block.sync
        def _(sp):
            falls = sp.value_load(unsorted[0:1, 0:1], min_val=0, max_val=E)
            with sp.If(falls == 0):
                sp.dma_start(pairs_d[0:E, :].rearrange("(p c) w -> p (c w)", p=P), pair[:]).then_inc(pairs_out, 16)
                sp.wait_ge(pairs_out, 16)

        @block.vector
        def _(dve):
            falls = dve.value_load(unsorted[0:1, 0:1], min_val=0, max_val=E)
            with dve.If(falls != 0):
                ch = Chain(dve, rank_steps, passed["dve"])
                ch.step(dve.memset(pos_f, 0.0))
                rank_edges(dve, ch, hi_dst, first_dst, mask, rank, pos_f, pos_dst)
                dve.sem_inc(dst_ranked)

        @block.gpsimd
        def _(pool):
            falls = pool.value_load(unsorted[0:1, 0:1], min_val=0, max_val=E)
            with pool.If(falls != 0):
                ch = Chain(pool, stage_steps, passed["pool"])
                pool.wait_ge(dst_ranked, 1)

                def scatter_pairs(i):
                    for h in range(2):
                        c = i * 16 + h * 8
                        if not isinstance(i, int):
                            at(pool, pair_out[h], i * 128, passed["pool"])
                        pool.tensor_copy(pstage[:, h * 16:h * 16 + 16], pair[:, bass.ds(c * 2, 16)])
                        ch.step(pool.tensor_copy(stage[:, h * 8:h * 8 + 8], pos_dst[:, bass.ds(c, 8)]))
                        for j in range(8):
                            pool.indirect_dma_start(pairs_d, bass.IndirectOffsetOnAxis(ap=stage[:, h * 8 + j:h * 8 + j + 1].bitcast(U32), axis=0),
                                                    pstage[:, h * 16 + 2 * j:h * 16 + 2 * j + 2], None).then_inc(pair_out[h], 16)

                scatter_pairs(0)
                with pool.Fori(1, EC // 16) as i:
                    ch.base -= 2
                    ch.enter(i, 2)
                    scatter_pairs(i)
                    ch.base += 2
                    ch.leave(EC // 16 - 1)
                for h in range(2):
                    pool.wait_ge(pair_out[h], 128 * (EC // 16))

    end_section()

    def fill_iota(pool, ids):
        return pool.iota(ids[:], pattern=[[1, (NT + 1) * P]], base=0, channel_multiplier=0, allow_small_or_imprecise_dtypes=True)

    with ExitStack() as ctx:
        U = 8
        ids = sbuf(ctx, "ids", [128, (NT + 1) * P], I16)
        acc = sbuf(ctx, "acc", [128, (NT + 1) * P])
        win = sbuf(ctx, "win", [128, U * 4 * (ED + 1)])
        hot = sbuf(ctx, "hot", [128, 4 * 4 * P])
        w_sum = sbuf(ctx, "w_sum", [128, D])
        acc_s = sbuf(ctx, "acc_s", [128, 2 * P])
        pw = psum(ctx, "pw", 4)
        py = psum(ctx, "py", 2)
        win_in = [sem(f"win_in{s}") for s in range(U)]
        accs_ready = sem("accs_ready")
        wsum_in, init2, hot_ready, win_summed, acc_done, y_ready, y_added = (
            sem(s) for s in ("wsum_in", "init2", "hot_ready", "win_summed", "acc_done", "y_ready", "y_added"))
        block = ctx.enter_context(nc.Block())

        @block.sync
        def _(sp):
            sp.dma_start(w_sum[:], a["L0_gnn_W_sum"]).then_inc(wsum_in, 16)

            def load(i):
                start = load_values(sp, win1_s, i * U, U, E)
                for s in range(U):
                    if not isinstance(i, int):
                        at(sp, win_summed, i * U + s + 1 - U, passed["sp"])
                    sp.dma_start(win[:, s * 4 * (ED + 1):(s + 1) * 4 * (ED + 1)],
                                 rows_d[bass.ds(start[s], W1), :].rearrange("(p r) c -> p (r c)", p=128)).then_inc(win_in[s], 16)

            load(0)
            with sp.Fori(1, NW1 // U) as i:
                load(i)

        @block.gpsimd
        def _(pool):
            fill_iota(pool, ids).then_inc(init2, 1)
            pool.memset(acc[:], 0.0).then_inc(init2, 1)

        @block.vector
        def _(dve):
            ch = chain("dve", dve)
            dve.wait_ge(init2, 2)

            def add(g, bank, b):
                at(dve, win_summed, g + 1, passed["dve"])
                if not isinstance(g, int) or g:
                    at(dve, acc_done, g, passed["dve"])
                tile = acc[:, bass.ds(b * P, P)]
                dve.tensor_tensor(tile, tile, pw[:, bank, 0:P], ALU.add).then_inc(acc_done, 1)

            def windows(i):
                early = 0 if isinstance(i, int) else 2
                b = load_values(dve, win1_b, i * U - early, U + early, NT)
                for s in range(U):
                    at(dve, win_in[s], i * 16 + 16, passed["dve"])
                    keys = win[:, s * 4 * (ED + 1):(s + 1) * 4 * (ED + 1)].rearrange("p (r c) -> p r c", r=4)[:, :, ED]
                    dve.tensor_tensor(hot[:, (s % 4) * 4 * P:(s % 4 + 1) * 4 * P].rearrange("p (r n) -> p r n", r=4),
                                      ids[:, bass.ds(b[s + early] * P, P)].unsqueeze(1).to_broadcast([128, 4, P]),
                                      keys.unsqueeze(2).to_broadcast([128, 4, P]), ALU.is_equal).then_inc(hot_ready, 1)
                    if early or s >= 2:
                        add(i * U + s - 2, (s - 2) % 4, b[s - 2 + early])

            windows(0)
            with dve.Fori(1, NW1 // U) as i:
                windows(i)
            b = load_values(dve, win1_b, NW1 - 2, 2, NT)
            for k in range(2):
                add(NW1 - 2 + k, (U - 2 + k) % 4, b[k])

            def add_sum(t, u, i):
                at(dve, y_ready, t + 1, passed["dve"])
                dve.tensor_tensor(Rt(t), Rt(t), py[0:P, u, 0:D], ALU.add).then_inc(y_added, 1)

            tiles(dve, add_sum)

        @block.scalar
        def _(act):
            act.wait_ge(acc_done, NW1)

            def stage_acc(t, u, i):
                if later(t):
                    at(act, y_ready, t - 1, passed["act"])
                act.copy(acc_s[:, u * P:(u + 1) * P], acc[:, bass.ds(t * P, P)]).then_inc(accs_ready, 1)

            tiles(act, stage_acc)

        @block.tensor
        def _(pe):
            def windows(i):
                for s in range(U):
                    g = i * U + s
                    at(pe, hot_ready, g + 1, passed["pe"])
                    at(pe, win_in[s], i * 16 + 16, passed["pe"])
                    if not isinstance(i, int) or s >= 4:
                        at(pe, acc_done, g - 3, passed["pe"])
                    for r in range(4):
                        mm = pe.matmul(pw[:, s % 4, 0:P], win[:, (s * 4 + r) * (ED + 1):(s * 4 + r) * (ED + 1) + ED],
                                       hot[:, ((s % 4) * 4 + r) * P:((s % 4) * 4 + r + 1) * P], start=(r == 0), stop=(r == 3))
                    mm.then_inc(win_summed, 1)

            windows(0)
            with pe.Fori(1, NW1 // U) as i:
                windows(i)
            pe.wait_ge(wsum_in, 16)

            def project(t, u, i):
                at(pe, accs_ready, t + 1, passed["pe"])
                if later(t):
                    at(pe, y_added, t - 1, passed["pe"])
                pe.matmul(py[0:P, u, 0:D], acc_s[:, u * P:(u + 1) * P], w_sum[:], start=True, stop=True).then_inc(y_ready, 1)

            tiles(pe, project)

    G, GC = NT // 2, 2 * P

    def groups(eng, body, ch=None, per=0):
        for g in range(3):
            body(g, g % 2)
        with eng.Fori(1, G // 2) as i:
            if ch:
                ch.base -= per
                ch.enter(i, per)
            body(2 * i + 1, 1)
            body(2 * i + 2, 0)
        if ch:
            ch.base += per
            ch.leave(G // 2 - 1)

    def XTg(g, k):
        return XT[:, bass.ds(g * 2 * TS, 2 * TS)].rearrange("p (t c) -> p t c", t=2)[:, :, k * P:(k + 1) * P]

    class Ffn:

        def __init__(self, ctx, name, nm):
            self.nm, self.uses = nm, {"pe": 0, "act": 0, "dve": 0}
            self.hT = sbuf(ctx, name + "_hT", [128, 2 * nm * GC])
            self.ph = psum(ctx, name + "_ph", 4)
            self.py = psum(ctx, name + "_py", 2)
            self.h_ready, self.h_stored, self.y_ready, self.y_added = (sem(name + s) for s in ("_h_ready", "_h_stored", "_y_ready", "_y_added"))

        def hidden(self, u, m):
            return self.hT[:, (u * self.nm + m) * GC:(u * self.nm + m + 1) * GC]

        def pe(self, pe, w1, w2):
            r, nm = self.uses["pe"], self.nm
            self.uses["pe"] += 1

            def second(g, u):
                at(pe, self.h_stored, (g + 1 + r * G) * nm, passed["pe"])
                for v in range(2):
                    if not isinstance(g, int) or g or r:
                        at(pe, self.y_added, 2 * (g + r * G) + v - 1, passed["pe"])
                    for m in range(nm):
                        mm = pe.matmul(self.py[0:P, v, 0:D], self.hidden(u, m)[:, v * P:(v + 1) * P], w2(m), start=(m == 0), stop=(m == nm - 1))
                    mm.then_inc(self.y_ready, 1)

            def body(g, u):
                for m in range(nm):
                    bank = m % 4 if nm >= 4 else 2 * u + m
                    if not isinstance(g, int) or r or g * nm + m >= 4:
                        at(pe, self.h_stored, (g + r * G) * nm + m - 3, passed["pe"])
                    for k in range(2):
                        mm = pe.matmul(self.ph[:, bank, 0:GC].rearrange("p (t c) -> p t c", t=2), w1(k, m), XTg(g, k), start=(k == 0), stop=(k == 1))
                    mm.then_inc(self.h_ready, 1)
                if not isinstance(g, int) or g:
                    second(g - 1, 1 - u)

            groups(pe, body)
            second(G - 1, 0)

        def act(self, act, func, bias):
            r, nm = self.uses["act"], self.nm
            self.uses["act"] += 1

            def body(g, u):
                if not isinstance(g, int) or g >= 2 or r:
                    at(act, self.y_ready, 2 * (g - 1 + r * G), passed["act"])
                for m in range(nm):
                    bank = m % 4 if nm >= 4 else 2 * u + m
                    at(act, self.h_ready, (g + r * G) * nm + m + 1, passed["act"])
                    act.activation(self.hidden(u, m), self.ph[:, bank, 0:GC], func, bias=bias(m)).then_inc(self.h_stored, 1)

            groups(act, body)

        def dve(self, dve, ch, per, body):
            r = self.uses["dve"]
            self.uses["dve"] += 1

            def both(g, u):
                for v in range(2):
                    at(dve, self.y_ready, 2 * (g + r * G) + v + 1, passed["dve"])
                    body(2 * g + v, self.py[0:P, v, 0:D])
                    dve.sem_inc(self.y_added)

            groups(dve, both, ch, per * 4)

    def load_cols(sp, dst, vec, n):
        with nc.allow_non_contiguous_dma(reason="a bias per partition"):
            return sp.dma_start(dst, vec.rearrange("(m p) -> p m", p=128))

    def load_rows(sp, dst, w):
        return sp.dma_start(dst.rearrange("p (k n) -> p k n", n=w.shape[1]), w.rearrange("(k p) n -> p k n", p=128))

    with ExitStack() as ctx:
        w1 = sbuf(ctx, "f_w1", [128, 2 * FFN_H])
        w2 = sbuf(ctx, "f_w2", [128, 8 * D])
        b1 = sbuf(ctx, "f_b1", [128, 8])
        b2 = sbuf(ctx, "f_b2", [P, D])
        wr = sbuf(ctx, "f_wr", [P, D])
        br = sbuf(ctx, "f_br", [P, 1])
        xn = sbuf(ctx, "f_xn", [P, 2 * D])
        prod = sbuf(ctx, "f_prod", [P, 2 * D])
        wt = sbuf(ctx, "f_wt", [P, NT])
        key_i = sbuf(ctx, "key_i", [P, 3 * NT], I32)
        key = sbuf(ctx, "key", [P, 3 * NT])
        hit = sbuf(ctx, "hit", [P, 3 * NT])
        sel = sbuf(ctx, "sel", [P, NT])
        cur = sbuf(ctx, "cur", [P, 8])
        pow2 = sbuf(ctx, "pow2", [P, 16])
        ptr = psum(ctx, "f_ptr", 2)
        ffn = Ffn(ctx, "f", FFN_H // 128)
        f_in, pows, xn_ready, xt_ready, xt_stored, sum_asked, sum_given = (
            sem(s) for s in ("f_in", "pows", "f_xn_ready", "f_xt_ready", "f_xt_stored", "sum_asked", "sum_given"))
        block = ctx.enter_context(nc.Block())

        @block.sync
        def _(sp):
            sp.dma_start(wr[:], bcast_rows(a["L0_ffn_wr"].rearrange("d a -> (d a)"), P)).then_inc(f_in, 16)
            sp.dma_start(br[:], bcast_rows(a["L0_ffn_br"], P)).then_inc(f_in, 16)
            load_rows(sp, w1[:], a["L0_ffn_w1"]).then_inc(f_in, 16)
            load_rows(sp, w2[:], a["L0_ffn_w2"]).then_inc(f_in, 16)
            load_cols(sp, b1[:], a["L0_ffn_b1"], 8).then_inc(f_in, 16)
            sp.dma_start(b2[:], bcast_rows(a["L0_ffn_b2"], P)).then_inc(f_in, 16)

        @block.gpsimd
        def _(pool):
            for j in range(16):
                pool.memset(pow2[:, j:j + 1], float(2 ** (15 - j))).then_inc(pows, 1)
            pool.iota(key_i[:, 2 * NT:3 * NT], pattern=[[-P, NT]], base=8191, channel_multiplier=-1).then_inc(pows, 1)

        @block.vector
        def _(dve):
            ch = chain("dve", dve)
            layer_stats(dve, ch, Rt)
            dve.wait_ge(f_in, 96)

            def norm(t, u, i):
                x_u = xn[:, u * D:(u + 1) * D]
                if later(t):
                    at(dve, xt_ready, t - 1, passed["dve"])
                dve.tensor_scalar(x_u, Rt(t), mean[:, bass.ds(t, 1)], rstd[:, bass.ds(t, 1)], ALU.subtract, ALU.mult).then_inc(xn_ready, 1)
                at(dve, xn_ready, t + 1, passed["dve"])
                ch.step(dve.tensor_tensor(Rt(t), Rt(t), x_u, ALU.add))
                ch.step(dve.tensor_tensor(prod[:, u * D:(u + 1) * D], x_u, wr[:], ALU.mult))
                ch.step(dve.tensor_reduce(wt[:, bass.ds(t, 1)], prod[:, u * D:(u + 1) * D], AX.X, ALU.add))

            tiles(dve, norm, ch, 6)
            ch.step(dve.tensor_scalar(wt[:], wt[:], br[:, 0:1], 0.0, ALU.add, ALU.add))
            ki = [key_i[:, k * NT:(k + 1) * NT] for k in range(3)]
            dve.wait_ge(pows, 17)
            ch.step(dve.tensor_scalar(ki[0], wt[:].bitcast(I32), 31, -2147483648, ALU.arith_shift_right, ALU.bitwise_or))
            ch.step(dve.tensor_tensor(ki[1], ki[0], wt[:].bitcast(I32), ALU.bitwise_xor))
            ch.step(dve.tensor_scalar(ki[0], ki[1], 16, None, ALU.logical_shift_right))
            ch.step(dve.tensor_scalar(ki[1], ki[1], 65535, None, ALU.bitwise_and))
            ch.step(dve.tensor_copy(key[:], key_i[:]))
            need, low, cand, part, gain = (cur[:, j:j + 1] for j in range(5))
            ch.step(dve.memset(need, float(TOPK)))
            ch.step(dve.memset(sel[:], 1.0))
            asked = [0]

            def count(v, threshold, op):
                ch.step(dve.tensor_scalar(hit[:, 0:NT], v, threshold, 0.0, op, ALU.add, accum_out=part))
                dve.sem_inc(sum_asked)

            for level in range(3):
                v, bits = key[:, level * NT:(level + 1) * NT], (16, 16, 13)[level]
                if level:
                    ch.step(dve.tensor_scalar(v, v, 1.0, None, ALU.add))
                    ch.step(dve.tensor_tensor(v, v, sel[:], ALU.mult))
                    ch.step(dve.tensor_scalar(v, v, -1.0, None, ALU.add))
                ch.step(dve.memset(low, 0.0))
                with dve.Fori(0, bits) as j:
                    ch.enter(j, 4)
                    step = pow2[:, bass.ds(j + (16 - bits), 1)]
                    ch.step(dve.tensor_tensor(cand, low, step, ALU.add))
                    count(v, cand, ALU.is_ge)
                    at(dve, sum_given, j + (asked[0] + 1), passed["dve"])
                    ch.step(dve.tensor_scalar(gain, ptr[0:P, 0, 0:1], need, step, ALU.is_ge, ALU.mult))
                    ch.step(dve.tensor_tensor(low, low, gain, ALU.add))
                    ch.leave(bits)
                asked[0] += bits
                if level < 2:
                    count(v, low, ALU.is_gt)
                    asked[0] += 1
                    dve.wait_ge(sum_given, asked[0])
                    ch.step(dve.tensor_copy(gain, ptr[0:P, 0, 0:1]))
                    ch.step(dve.tensor_tensor(need, need, gain, ALU.subtract))
                    ch.step(dve.tensor_scalar(hit[:, (level + 1) * NT:(level + 2) * NT], v, low, None, ALU.is_gt))
                    ch.step(dve.tensor_scalar(sel[:], v, low, None, ALU.is_equal))
                else:
                    ch.step(dve.tensor_scalar(sel[:], v, low, None, ALU.is_ge))
            for k in (1, 2):
                ch.step(dve.tensor_tensor(sel[:], sel[:], hit[:, k * NT:(k + 1) * NT], ALU.max))
            ch.step(dve.tensor_tensor(wt[:], wt[:], sel[:], ALU.mult))

            def add_y(t, y):
                tmp = prod[:, 0:D]
                ch.step(dve.tensor_tensor(tmp, y, b2[:], ALU.add))
                ch.step(dve.scalar_tensor_tensor(out=Rt(t), in0=tmp, scalar=wt[:, bass.ds(t, 1)], in1=Rt(t), op0=ALU.mult, op1=ALU.add))

            ffn.dve(dve, ch, 2, add_y)

        @block.scalar
        def _(act):
            finish_stats_act(act)

            def store_xt(t, u, i):
                at(act, xt_ready, t + 1, passed["act"])
                act.copy(XT[:, bass.ds(t * TS, 2 * P)], ptr[:, u, 0:2 * P]).then_inc(xt_stored, 1)

            tiles(act, store_xt)
            act.wait_ge(f_in, 96)
            ffn.act(act, ACT.Gelu_apprx_tanh, lambda m: b1[:, m:m + 1])

        @block.tensor
        def _(pe):
            def transpose_x(t, u, i):
                at(pe, xn_ready, t + 1, passed["pe"])
                if later(t):
                    at(pe, xt_stored, t - 1, passed["pe"])
                for k in range(2):
                    mm = pe.transpose(ptr[:, u, k * P:(k + 1) * P], xn[:, u * D + k * 128:u * D + (k + 1) * 128], ident[0:P, 0:P])
                mm.then_inc(xt_ready, 1)

            tiles(pe, transpose_x)
            pe.wait_ge(xt_stored, NT)
            n = 16 + 1 + 16 + 1 + 13
            pe.wait_ge(sum_asked, 1)
            pe.matmul(ptr[0:P, 0, 0:1], ones[0:P, 0:P], cur[:, 3:4], start=True, stop=True).then_inc(sum_given, 1)
            with pe.Fori(1, n) as j:
                at(pe, sum_asked, j + 1, passed["pe"])
                pe.matmul(ptr[0:P, 0, 0:1], ones[0:P, 0:P], cur[:, 3:4], start=True, stop=True).then_inc(sum_given, 1)
            pe.wait_ge(f_in, 96)
            ffn.pe(pe, lambda k, m: w1[:, k * FFN_H + m * 128:k * FFN_H + (m + 1) * 128], lambda m: w2[:, m * D:(m + 1) * D])

    with ExitStack() as ctx:
        xn = sbuf(ctx, "g_xn", [P, 2 * D])
        ptr = psum(ctx, "g_ptr", 2)
        xn_ready, xt_ready, xt_stored = sem("g_xn_ready"), sem("g_xt_ready"), sem("g_xt_stored")
        row_out = [sem("row_out0"), sem("row_out1")]
        block = ctx.enter_context(nc.Block())

        @block.sync
        def _(sp):
            def store(t, u, i):
                at(sp, xn_ready, t + 1, passed["sp"])
                sp.dma_start(xn2_d[bass.ds(t * P, P), :], xn[:, u * D:(u + 1) * D]).then_inc(row_out[u], 16)

            tiles(sp, store)
            for u in range(2):
                sp.wait_ge(row_out[u], 16 * (NT // 2))

        @block.vector
        def _(dve):
            ch = chain("dve", dve)
            layer_stats(dve, ch, Rt)

            def norm(t, u, i):
                if later(t):
                    at(dve, xt_ready, t - 1, passed["dve"])
                    at(dve, row_out[u], i * 16, passed["dve"])
                dve.tensor_scalar(xn[:, u * D:(u + 1) * D], Rt(t), mean[:, bass.ds(t, 1)], rstd[:, bass.ds(t, 1)],
                                  ALU.subtract, ALU.mult).then_inc(xn_ready, 1)

            tiles(dve, norm)

        @block.scalar
        def _(act):
            finish_stats_act(act)

            def store_xt(t, u, i):
                at(act, xt_ready, t + 1, passed["act"])
                act.copy(XT[:, bass.ds(t * TS, 2 * P)], ptr[:, u, 0:2 * P]).then_inc(xt_stored, 1)

            tiles(act, store_xt)

        @block.tensor
        def _(pe):
            def transpose_x(t, u, i):
                at(pe, xn_ready, t + 1, passed["pe"])
                if later(t):
                    at(pe, xt_stored, t - 1, passed["pe"])
                for k in range(2):
                    mm = pe.transpose(ptr[:, u, k * P:(k + 1) * P], xn[:, u * D + k * 128:u * D + (k + 1) * 128], ident[0:P, 0:P])
                mm.then_inc(xt_ready, 1)

            tiles(pe, transpose_x)

    s56 = ExitStack()
    agg = sbuf(s56, "agg", [128, (NT + 1) * TS])
    with ExitStack() as ctx:
        U, RU, PU = 16, 8, 8
        ids = sbuf(ctx, "ids2", [128, (NT + 1) * P], I16)
        pw_in = sbuf(ctx, "pw_in", [128, U * 4], I32)
        rows = sbuf(ctx, "rows", [128, RU * 2 * D])
        hot = sbuf(ctx, "hot2", [128, 4 * 2 * P])
        pg = psum(ctx, "pg", 4)
        pairs_in = [sem(f"pairs_in{h}") for h in range(U // PU)]
        rows_in = [sem(f"rows_in{s}") for s in range(RU)]
        init, hot_ready, win_summed, acc_done = (sem(s) for s in ("g_init", "g_hot_ready", "g_win_summed", "g_acc_done"))
        block = ctx.enter_context(nc.Block())

        @block.sync
        def _(sp):
            def load(i):
                start = load_values(sp, win2_s, i * U, U, E)
                for s in range(U):
                    if not isinstance(i, int) and s % PU == 0:
                        at(sp, win_summed, i * U + s + PU - U, passed["sp"])
                    sp.dma_start(pw_in[:, s * 4:(s + 1) * 4],
                                 pairs_d[bass.ds(start[s], W2), :].rearrange("(p r) c -> p (r c)", p=128)).then_inc(pairs_in[s // PU], 16)

            load(0)
            with sp.Fori(1, NW2 // U) as i:
                load(i)

        @block.gpsimd
        def _(pool):
            fill_iota(pool, ids).then_inc(init, 1)
            pool.memset(agg[:], 0.0).then_inc(init, 1)

            def gather(i):
                for s in range(U):
                    if s % PU == 0:
                        at(pool, pairs_in[s // PU], (i + 1) * 16 * PU, passed["pool"])
                    if s % 4 == 0 and (s >= RU or not isinstance(i, int)):
                        at(pool, win_summed, i * U + s + 4 - RU, passed["pool"])
                    for r in range(2):
                        pool.indirect_dma_start(rows[:, (2 * (s % RU) + r) * D:(2 * (s % RU) + r + 1) * D], None, xn2_d,
                                                bass.IndirectOffsetOnAxis(ap=pw_in[:, s * 4 + 2 * r:s * 4 + 2 * r + 1].bitcast(U32), axis=0)
                                                ).then_inc(rows_in[s % RU], 16)

            gather(0)
            with pool.Fori(1, NW2 // U) as i:
                gather(i)

        @block.vector
        def _(dve):
            dve.wait_ge(init, 2)

            def add(g, bank, b):
                at(dve, win_summed, g + 1, passed["dve"])
                if not isinstance(g, int) or g:
                    at(dve, acc_done, g, passed["dve"])
                tile = agg[0:P, bass.ds(b * TS, D)]
                dve.tensor_tensor(tile, tile, pg[0:P, bank, 0:D], ALU.add).then_inc(acc_done, 1)

            def windows(i):
                early = 0 if isinstance(i, int) else 2
                b = load_values(dve, win2_b, i * U - early, U + early, NT)
                for s in range(U):
                    if s % PU == 0:
                        at(dve, pairs_in[s // PU], (i + 1) * 16 * PU, passed["dve"])
                    keys = pw_in[:, s * 4:(s + 1) * 4].rearrange("p (r c) -> p r c", c=2)[:, :, 1]
                    dve.tensor_tensor(hot[:, (s % 4) * 2 * P:(s % 4 + 1) * 2 * P].rearrange("p (r n) -> p r n", r=2),
                                      ids[:, bass.ds(b[s + early] * P, P)].unsqueeze(1).to_broadcast([128, 2, P]),
                                      keys.unsqueeze(2).to_broadcast([128, 2, P]), ALU.is_equal).then_inc(hot_ready, 1)
                    if early or s >= 2:
                        add(i * U + s - 2, (s - 2) % 4, b[s - 2 + early])

            windows(0)
            with dve.Fori(1, NW2 // U) as i:
                windows(i)
            b = load_values(dve, win2_b, NW2 - 2, 2, NT)
            for k in range(2):
                add(NW2 - 2 + k, (U - 2 + k) % 4, b[k])

        @block.tensor
        def _(pe):
            def windows(i):
                for s in range(U):
                    g = i * U + s
                    at(pe, hot_ready, g + 1, passed["pe"])
                    at(pe, rows_in[s % RU], (i * (U // RU) + s // RU + 1) * 32, passed["pe"])
                    if not isinstance(i, int) or s >= 4:
                        at(pe, acc_done, g - 3, passed["pe"])
                    for r in range(2):
                        mm = pe.matmul(pg[0:P, s % 4, 0:D], hot[:, ((s % 4) * 2 + r) * P:((s % 4) * 2 + r + 1) * P],
                                       rows[:, (2 * (s % RU) + r) * D:(2 * (s % RU) + r + 1) * D], start=(r == 0), stop=(r == 1))
                    mm.then_inc(win_summed, 1)

            windows(0)
            with pe.Fori(1, NW2 // U) as i:
                windows(i)

    with ExitStack() as ctx:
        wq = sbuf(ctx, "m_wq", [128, 2 * 768])
        w1 = sbuf(ctx, "m_w1", [128, 2 * D])
        w2 = sbuf(ctx, "m_w2", [128, 2 * D])
        wp = sbuf(ctx, "m_wp", [128, 2 * D])
        bq_row = sbuf(ctx, "m_bq_row", [P, 768])
        lng = sbuf(ctx, "m_lng", [P, 2 * D])
        lnb = sbuf(ctx, "m_lnb", [P, 2 * D])
        b1 = sbuf(ctx, "m_b1", [128, 2])
        bq = sbuf(ctx, "m_bq", [128, 2])
        b2 = sbuf(ctx, "m_b2", [P, D])
        xs = sbuf(ctx, "m_xs", [128, 2 * TS])
        kv = sbuf(ctx, "m_kv", [128, 2 * 2 * D])
        sq = sbuf(ctx, "m_sq", [128, 2 * 2 * D])
        kn = sbuf(ctx, "m_kn", [P, 2 * 2 * D])
        hm = sbuf(ctx, "m_hm", [P, 2 * 16])
        hv = sbuf(ctx, "m_hv", [P, 2 * 16])
        wqT = sq
        kvn = sbuf(ctx, "m_kvn", [128, 2 * 128])
        mT = kv
        tb = sbuf(ctx, "m_tb", [128, 2])
        bp = sbuf(ctx, "m_bp", [128, 2])
        tmp = sbuf(ctx, "m_tmp", [P, D])
        m_in, xs_ready, kv_ready, kv_c, sq_ready, var_r, sd_r, kn_ready, ctx_done, kv_read = (
            sem("m_" + s) for s in ("in", "xs_ready", "kv_ready", "kv_c", "sq_ready", "var_r", "sd_r", "kn_ready", "ctx_done", "kv_read"))
        q_compact = sem("q_compact")
        fold_pe, fold_dve = sem("m_fold_pe"), sem("m_fold_dve")

        def all_dma(sp):
            sp.dma_start(bq_row[:], bcast_rows(a["L1_mix_b_qkv"], P)).then_inc(m_in, 16)
            load_rows(sp, wq[:], a["L1_mix_w_qkv"]).then_inc(m_in, 16)
            load_rows(sp, w1[:], a["L1_mix_w1"]).then_inc(m_in, 16)
            load_rows(sp, w2[:], a["L1_mix_w2"]).then_inc(m_in, 16)
            load_cols(sp, b1[:], a["L1_mix_b1"], 2).then_inc(m_in, 16)
            sp.dma_start(b2[:], bcast_rows(a["L1_mix_b2"], P)).then_inc(m_in, 16)
            with nc.allow_non_contiguous_dma(reason="a bias per partition"):
                for m in range(2):
                    for h in range(4):
                        o = 96 * (4 * m + h)
                        sp.dma_start(bq[32 * h:32 * h + 32, m:m + 1], a["L1_mix_b_qkv"][o:o + 32].rearrange("(p a) -> p a", a=1)).then_inc(m_in, 16)
            for j, (g_, b_) in enumerate((("kln_g", "kln_b"), ("vln_g", "vln_b"))):
                for dst, name in ((lng, g_), (lnb, b_)):
                    for h in range(HEADS):
                        sp.dma_start(dst[:, h * 64 + j * 32:h * 64 + j * 32 + 32], bcast_rows(a["L1_mix_" + name], P)).then_inc(m_in, 16)

        M_IN = 16 * (6 + 8 + 32)
        with ExitStack() as c1:
            pk = psum(c1, "m_pk", 2)
            pc = psum(c1, "m_pc", 1)
            pf = psum(c1, "m_pf", 4)
            block = c1.enter_context(nc.Block())

            @block.sync
            def _(sp):
                all_dma(sp)

            @block.vector
            def _(dve):
                ch = chain("dve", dve)
                dve.wait_ge(m_in, M_IN)
                bias = bq_row[:].rearrange("p (h c) -> p h c", h=HEADS)[:, :, 32:96]

                def norm_kv(t, u, i):
                    kv_u, sq_u, kn_u = (x[0:P, u * 2 * D:(u + 1) * 2 * D] for x in (kv, sq, kn))
                    m_u, v_u = hm[:, u * 16:(u + 1) * 16], hv[:, u * 16:(u + 1) * 16]
                    kv3 = kv_u.rearrange("p (g d) -> p g d", g=16)
                    at(dve, kv_ready, t + 1, passed["dve"])
                    dve.tensor_tensor(kv_u.rearrange("p (h c) -> p h c", h=HEADS), pk[0:P, u, :].rearrange("p (h c) -> p h c", h=HEADS), bias, ALU.add).then_inc(kv_read, 1)
                    at(dve, kv_read, t + 1, passed["dve"])
                    ch.step(dve.tensor_reduce(m_u, kv3, AX.X, ALU.add))
                    ch.step(dve.tensor_scalar(m_u, m_u, 1.0 / HD, None, ALU.mult))
                    dve.tensor_tensor(kv3, kv3, m_u.unsqueeze(2).to_broadcast([P, 16, HD]), ALU.subtract).then_inc(kv_c, 1)
                    at(dve, sq_ready, t + 1, passed["dve"])
                    ch.step(dve.tensor_reduce(v_u, sq_u.rearrange("p (g d) -> p g d", g=16), AX.X, ALU.add))
                    dve.tensor_scalar(v_u, v_u, 1.0 / HD, EPS, ALU.mult, ALU.add).then_inc(var_r, 1)
                    at(dve, sd_r, t + 1, passed["dve"])
                    ch.step(dve.reciprocal(v_u, v_u))
                    ch.step(dve.tensor_tensor(kv3, kv3, v_u.unsqueeze(2).to_broadcast([P, 16, HD]), ALU.mult))
                    ch.step(dve.tensor_tensor(kv_u, kv_u, lng[:], ALU.mult))
                    if later(t):
                        at(dve, ctx_done, t - 1, passed["dve"])
                    for j in range(2):
                        ins = dve.tensor_tensor(kn_u[:, j * D:(j + 1) * D].rearrange("p (h d) -> p h d", h=HEADS),
                                                kv_u.rearrange("p (h c) -> p h c", h=HEADS)[:, :, j * HD:(j + 1) * HD],
                                                lnb[:].rearrange("p (h c) -> p h c", h=HEADS)[:, :, j * HD:(j + 1) * HD], ALU.add)
                        ins.then_inc(kn_ready, 1)

                tiles(dve, norm_kv, ch, 12)
                dve.wait_ge(ctx_done, NT)
                for m in range(2):
                    ch.step(dve.tensor_scalar(kvn[:, m * 128:(m + 1) * 128], pc[:, 0, m * 128:(m + 1) * 128], 1.0 / N, None, ALU.mult))
                    ch.step(dve.tensor_tensor(kvn[:, m * 128:(m + 1) * 128], kvn[:, m * 128:(m + 1) * 128], blockdiag[:], ALU.mult))
                dve.wait_ge(fold_pe, 1)
                for m in range(2):
                    ch.step(dve.tensor_copy(wqT[:, m * D:(m + 1) * D], pf[:, m, 0:D]))
                dve.sem_inc(fold_dve)
                dve.wait_ge(fold_pe, 2)
                for m in range(2):
                    ch.step(dve.tensor_copy(mT[:, m * D:(m + 1) * D], pf[:, 2 + m, 0:D]))
                    d = mT[:, m * D + m * 128:m * D + (m + 1) * 128]
                    ch.step(dve.tensor_tensor(d, d, ident[:], ALU.add))
                    ch.step(dve.tensor_copy(tb[:, m:m + 1], pf[:, 0, m:m + 1]))
                dve.sem_inc(fold_dve)
                dve.wait_ge(fold_pe, 3)
                for m in range(2):
                    ch.step(dve.tensor_copy(wp[:, m * D:(m + 1) * D], pf[:, 2 + m, 0:D]))
                ch.step(dve.tensor_tensor(bp[:], b1[:], pf[:, 1, 0:2], ALU.add))

            @block.scalar
            def _(act):
                def parts(t, u, i):
                    if later(t):
                        at(act, kv_ready, t - 1, passed["act"])
                    act.copy(xs[:, u * TS:u * TS + 2 * P], XT[:, bass.ds(t * TS, 2 * P)]).then_inc(xs_ready, 1)
                    at(act, kv_c, t + 1, passed["act"])
                    act.activation(sq[0:P, u * 2 * D:(u + 1) * 2 * D], kv[0:P, u * 2 * D:(u + 1) * 2 * D], ACT.Square).then_inc(sq_ready, 1)
                    at(act, var_r, t + 1, passed["act"])
                    act.activation(hv[:, u * 16:(u + 1) * 16], hv[:, u * 16:(u + 1) * 16], ACT.Sqrt).then_inc(sd_r, 1)

                tiles(act, parts)
                act.wait_ge(m_in, M_IN)
                for k in range(2):
                    act.copy(wp[:, k * D:(k + 1) * D].rearrange("p (h c) -> p h c", h=HEADS),
                             wq[:, k * 768:(k + 1) * 768].rearrange("p (h c) -> p h c", h=HEADS)[:, :, 0:32]).then_inc(q_compact, 1)

            @block.tensor
            def _(pe):
                pe.wait_ge(m_in, M_IN)

                def context(t, u):
                    at(pe, kn_ready, 2 * t + 2, passed["pe"])
                    first = isinstance(t, int) and t == 0
                    for m in range(2):
                        mm = pe.matmul(pc[:, 0, m * 128:(m + 1) * 128], kn[:, u * 2 * D + m * 128:u * 2 * D + (m + 1) * 128],
                                       kn[:, u * 2 * D + D + m * 128:u * 2 * D + D + (m + 1) * 128], start=first and m == 0, stop=True, skip_group_check=True)
                    mm.then_inc(ctx_done, 1)

                def project(t, u, i):
                    at(pe, xs_ready, t + 1, passed["pe"])
                    if later(t):
                        at(pe, kv_read, t - 1, passed["pe"])
                    for k in range(2):
                        w = wq[:, k * 768:(k + 1) * 768].rearrange("p (h c) -> p h c", h=HEADS)[:, :, 32:96]
                        mm = pe.matmul(pk[0:P, u, :].rearrange("p (h c) -> p h c", h=HEADS), xs[:, u * TS + k * P:u * TS + (k + 1) * P], w, start=(k == 0), stop=(k == 1))
                    mm.then_inc(kv_ready, 1)
                    if not isinstance(t, int) or t:
                        context(t - 1, 1 - u)

                tiles(pe, project)
                context(NT - 1, 1)
                pe.wait_ge(q_compact, 2)
                for m in range(2):
                    for k in range(2):
                        mm = pe.matmul(pf[:, m, k * 128:(k + 1) * 128], wp[:, k * D + m * 128:k * D + (m + 1) * 128], ident[:], start=True, stop=True)
                mm.then_inc(fold_pe, 1)
                pe.wait_ge(fold_dve, 1)
                for m in range(2):
                    pe.matmul(pf[:, 2 + m, 0:D], kvn[:, m * 128:(m + 1) * 128], wqT[:, m * D:(m + 1) * D], start=True, stop=True)
                for m in range(2):
                    mm = pe.matmul(pf[:, 0, m:m + 1], kvn[:, m * 128:(m + 1) * 128], bq[:, m:m + 1], start=True, stop=True)
                mm.then_inc(fold_pe, 1)
                pe.wait_ge(fold_dve, 2)
                for k in range(2):
                    for m in range(2):
                        pe.matmul(pf[:, 2 + k, 0:D], mT[:, m * D + k * 128:m * D + (k + 1) * 128], w1[:, m * D:(m + 1) * D], start=(m == 0), stop=(m == 1))
                for c in range(2):
                    for m in range(2):
                        mm = pe.matmul(pf[:, 1, c:c + 1], w1[:, m * D + c * 128:m * D + (c + 1) * 128], tb[:, m:m + 1], start=(m == 0), stop=(m == 1))
                mm.then_inc(fold_pe, 1)

        with ExitStack() as c2:
            ffn = Ffn(c2, "m", 2)
            block = c2.enter_context(nc.Block())

            @block.vector
            def _(dve):
                ch = chain("dve", dve)

                def add_y(t, y):
                    ch.step(dve.tensor_tensor(tmp[:], y, b2[:], ALU.add))
                    ch.step(dve.tensor_scalar(sq[0:P, 0:D], Rt(t), mean[:, bass.ds(t, 1)], rstd[:, bass.ds(t, 1)], ALU.subtract, ALU.mult))
                    ch.step(dve.tensor_tensor(tmp[:], tmp[:], sq[0:P, 0:D], ALU.add))
                    ch.step(dve.tensor_tensor(Rt(t), Rt(t), tmp[:], ALU.add))

                ffn.dve(dve, ch, 4, add_y)

            @block.scalar
            def _(act):
                ffn.act(act, ACT.Gelu, lambda m: bp[:, m:m + 1])

            @block.tensor
            def _(pe):
                ffn.pe(pe, lambda k, m: wp[:, k * D + m * 128:k * D + (m + 1) * 128], lambda m: w2[:, m * D:(m + 1) * D])

    with s56, ExitStack() as ctx:
        wl = sbuf(ctx, "s_wl", [128, 2 * D])
        wr = sbuf(ctx, "s_wr", [128, 2 * D])
        wn = sbuf(ctx, "s_wn", [128, 4 * D])
        bl = sbuf(ctx, "s_bl", [P, D])
        gm = sbuf(ctx, "s_gm", [P, D])
        bt = sbuf(ctx, "s_bt", [P, D])
        mu = sbuf(ctx, "s_mu", [P, D])
        gv = sbuf(ctx, "s_gv", [P, D])
        xs = sbuf(ctx, "s_xs", [128, 2 * 2 * TS])
        sq = sbuf(ctx, "s_sq", [P, 2 * D])
        rdeg = sbuf(ctx, "s_rdeg", [P, NT])
        ss = sbuf(ctx, "s_ss", [P, NT])
        pa = psum(ctx, "s_pa", 2)
        ptr = psum(ctx, "s_ptr", 2)
        ag = sbuf(ctx, "s_ag", [P, 2 * D])
        pst = psum(ctx, "s_pst", 2)
        pt = psum(ctx, "s_pt", 2)
        s_in, wt_ready, w_stored, xs_ready, ab_ready, o_ready, ss_done, ss_ready, n_ready, sum_ready, c_ready, sq_ready2, var_ready2, sd_ready2, sq_used = (
            sem("s_" + s) for s in ("in", "wt_ready", "w_stored", "xs_ready", "ab_ready", "o_ready", "ss_done", "ss_ready", "n_ready", "sum_ready", "c_ready", "sq_ready2", "var_ready2", "sd_ready2", "sq_used"))
        block = ctx.enter_context(nc.Block())

        sum_steps, ag_ready, ag_transposed = sem("s_sum_steps"), sem("s_ag_ready"), sem("s_ag_transposed")

        def Ot(t):
            return agg[0:P, bass.ds(t * TS, D)]

        @block.sync
        def _(sp):
            load_rows(sp, wn[:, 0:2 * D], a["L1_gnn_W_l"]).then_inc(s_in, 16)
            load_rows(sp, wn[:, 2 * D:4 * D], a["L1_gnn_W_r"]).then_inc(s_in, 16)
            for dst, name in ((bl, "b_l"), (gm, "gamma"), (bt, "beta")):
                sp.dma_start(dst[:], bcast_rows(a["L1_gnn_" + name], P)).then_inc(s_in, 16)

        @block.vector
        def _(dve):
            ch = chain("dve", dve)
            dve.wait_ge(s_in, 80)
            ch.step(dve.tensor_scalar(rdeg[:], deg_in[:], 1.0, None, ALU.max))
            ch.step(dve.reciprocal(rdeg[:], rdeg[:]))

            def combine(t, u):
                at(dve, ab_ready, t + 1, passed["dve"])
                dve.tensor_tensor(Ot(t), pa[0:P, u, 0:D], bl[:], ALU.add).then_inc(o_ready, 1)

            def scale(t, u, i):
                if later(t):
                    at(dve, ag_transposed, t - 1, passed["dve"])
                dve.tensor_scalar(ag[:, u * D:(u + 1) * D], Ot(t), rdeg[:, bass.ds(t, 1)], None, ALU.mult).then_inc(ag_ready, 1)
                if not isinstance(t, int) or t:
                    at(dve, ag_ready, t, passed["dve"])
                    combine(t - 1, 1 - u)

            tiles(dve, scale)
            dve.wait_ge(ag_ready, NT)
            combine(NT - 1, 1)
            dve.wait_ge(o_ready, NT)
            dve.wait_ge(ss_ready, 1)
            ch.step(dve.tensor_scalar(ss[:], ss[:], 1e-12, None, ALU.max))
            ch.step(dve.reciprocal(ss[:], ss[:]))

            def unit(t, u, i):
                dve.tensor_scalar(Ot(t), Ot(t), ss[:, bass.ds(t, 1)], None, ALU.mult).then_inc(n_ready, 1)

            tiles(dve, unit)
            dve.wait_ge(sum_ready, 1)
            dve.wait_ge(n_ready, NT)
            ch.step(dve.tensor_scalar(mu[:], pst[0:P, 0, 0:D], 1.0 / N, None, ALU.mult))

            def center(t, u, i):
                dve.tensor_tensor(Ot(t), Ot(t), mu[:], ALU.subtract).then_inc(c_ready, 1)

            tiles(dve, center)
            dve.wait_ge(sum_ready, 2)
            dve.wait_ge(c_ready, NT)
            dve.tensor_scalar(gv[:], pst[0:P, 1, 0:D], 1.0 / N, EPS, ALU.mult, ALU.add).then_inc(var_ready2, 1)
            dve.wait_ge(sd_ready2, 1)
            ch.step(dve.reciprocal(gv[:], gv[:]))
            ch.step(dve.tensor_tensor(gv[:], gv[:], gm[:], ALU.mult))

            def finish(t, u, i):
                ch.step(dve.tensor_tensor(Ot(t), Ot(t), gv[:], ALU.mult))
                ch.step(dve.tensor_tensor(Ot(t), Ot(t), bt[:], ALU.add))
                ch.step(dve.scalar_tensor_tensor(out=Rt(t), in0=Ot(t), scalar=0.0, in1=Rt(t), op0=ALU.max, op1=ALU.add))

            tiles(dve, finish, ch, 6)

        @block.scalar
        def _(act):
            for j in range(2):
                for k in range(2):
                    act.wait_ge(wt_ready, 2 * j + k + 1)
                    act.copy((wl, wr)[j][:, k * D:(k + 1) * D], pt[:, k, 0:D]).then_inc(w_stored, 1)

            def square(t, u):
                at(act, o_ready, t + 1, passed["act"])
                if later(t):
                    at(act, ss_done, t - 1, passed["act"])
                act.activation(sq[:, u * D:(u + 1) * D], Ot(t), ACT.Square, accum_out=ss[:, bass.ds(t, 1)]).then_inc(ss_done, 1)

            def parts(t, u, i):
                if later(t):
                    at(act, ab_ready, t - 1, passed["act"])
                act.copy(xs[:, (2 * u + 1) * TS:(2 * u + 1) * TS + 2 * P], XT[:, bass.ds(t * TS, 2 * P)]).then_inc(xs_ready, 1)
                at(act, ag_transposed, t + 1, passed["act"])
                act.copy(xs[:, 2 * u * TS:2 * u * TS + 2 * P], ptr[:, u, 0:2 * P]).then_inc(xs_ready, 1)
                if not isinstance(t, int) or t:
                    square(t - 1, 1 - u)

            tiles(act, parts)
            square(NT - 1, 1)
            act.wait_ge(ss_done, NT)
            act.activation(ss[:], ss[:], ACT.Sqrt).then_inc(ss_ready, 1)

            def squares(t, u, i):
                at(act, c_ready, t + 1, passed["act"])
                if later(t):
                    at(act, sq_used, t - 1, passed["act"])
                act.activation(sq[:, u * D:(u + 1) * D], Ot(t), ACT.Square).then_inc(sq_ready2, 1)

            tiles(act, squares)
            act.wait_ge(var_ready2, 1)
            act.activation(gv[:], gv[:], ACT.Sqrt).then_inc(sd_ready2, 1)

        @block.tensor
        def _(pe):
            pe.wait_ge(s_in, 80)
            for j in range(2):
                for k in range(2):
                    if j:
                        pe.wait_ge(w_stored, k + 1)
                    for n in range(2):
                        mm = pe.transpose(pt[:, k, n * 128:(n + 1) * 128], wn[:, (2 * j + n) * D + k * 128:(2 * j + n) * D + (k + 1) * 128], ident[:])
                    mm.then_inc(wt_ready, 1)
            pe.wait_ge(w_stored, 4)

            def project(t, u):
                at(pe, xs_ready, 2 * t + 2, passed["pe"])
                if later(t):
                    at(pe, o_ready, t - 1, passed["pe"])
                for j, w in enumerate((wl, wr)):
                    for k in range(2):
                        mm = pe.matmul(pa[0:P, u, 0:D], xs[:, (2 * u + j) * TS + k * P:(2 * u + j) * TS + (k + 1) * P], w[:, k * D:(k + 1) * D],
                                       start=(j == 0 and k == 0), stop=(j == 1 and k == 1))
                mm.then_inc(ab_ready, 1)

            def transpose_ag(t, u, i):
                at(pe, ag_ready, t + 1, passed["pe"])
                if later(t):
                    at(pe, xs_ready, 2 * t - 2, passed["pe"])
                for k in range(2):
                    mm = pe.transpose(ptr[:, u, k * P:(k + 1) * P], ag[:, u * D + k * 128:u * D + (k + 1) * 128], ident[0:P, 0:P])
                mm.then_inc(ag_transposed, 1)
                if not isinstance(t, int) or t:
                    project(t - 1, 1 - u)

            tiles(pe, transpose_ag)
            project(NT - 1, 1)

            def sum_rows(t, u, i):
                at(pe, n_ready, t + 1, passed["pe"])
                mm = pe.matmul(pst[0:P, 0, 0:D], ones[0:P, 0:P], Ot(t), start=(isinstance(t, int) and t == 0), stop=True, skip_group_check=True)
                return mm

            tiles(pe, lambda t, u, i: sum_rows(t, u, i).then_inc(sum_steps, 1))
            pe.wait_ge(sum_steps, NT)
            pe.sem_inc(sum_ready)

            def sum_squares(t, u, i):
                at(pe, sq_ready2, t + 1, passed["pe"])
                pe.matmul(pst[0:P, 1, 0:D], ones[0:P, 0:P], sq[:, u * D:(u + 1) * D], start=(isinstance(t, int) and t == 0), stop=True, skip_group_check=True).then_inc(sq_used, 1)

            tiles(pe, sum_squares)
            pe.wait_ge(sq_used, NT)
            pe.sem_inc(sum_ready)

    end_section()

    def pipelined(eng, body, n):
        for t in range(4):
            body(t, t % 2, t // 2)
        with eng.Fori(2, n // 2) as i:
            body(2 * i, 0, i)
            body(2 * i + 1, 1, i)

    with ExitStack() as ctx:
        KE, NH = EXPERTS, EXP_H // 128
        w1 = sbuf(ctx, "e_w1", [128, KE * 2 * EXP_H])
        w2 = sbuf(ctx, "e_w2", [128, KE * NH * D])
        b1 = sbuf(ctx, "e_b1", [128, KE * NH])
        b2 = sbuf(ctx, "e_b2", [128, KE * D])
        share = sbuf(ctx, "e_share", [P, NT * 2])
        pos_x = sbuf(ctx, "e_pos_x", [P, NT * 2], I32)
        pos_y = sbuf(ctx, "e_pos_y", [P, NT * 2], I32)
        win_e = sbuf(ctx, "e_win_e", [1, NWM], I32)
        win_s = sbuf(ctx, "e_win_s", [1, NWM], I32)
        e_in = sem("e_in")
        E_IN = 16 * (6 + 2 * KE)

        with ExitStack() as c1:
            wr = sbuf(c1, "e_wr", [128, 2 * KE])
            br = sbuf(c1, "e_br", [P, KE])
            gm = sbuf(c1, "e_gm", [P, D])
            bt = sbuf(c1, "e_bt", [P, D])
            xn = sbuf(c1, "e_xn", [P, 2 * D])
            xs = sbuf(c1, "e_xs", [128, 2 * TS])
            lg = sbuf(c1, "e_lg", [P, NT * KE])
            best = sbuf(c1, "e_best", [P, NT])
            tot = sbuf(c1, "e_tot", [P, NT])
            rank = sbuf(c1, "e_rank", [P, NT * KE])
            prod = sbuf(c1, "e_prod", [P, NT * KE])
            place = sbuf(c1, "e_place", [P, NT * KE])
            cmp = sbuf(c1, "e_cmp", [P, NWM * KE])
            got = sbuf(c1, "e_got", [P, NT])
            e8 = sbuf(c1, "e_e8", [P, 8 * KE])
            e8_i = sbuf(c1, "e_e8_i", [P, KE], I32)
            zero = sbuf(c1, "e_zero", [128, 2 * D])
            xr = sbuf(c1, "e_xr", [P, 2 * D])
            stage = sbuf(c1, "e_stage", [P, 2 * 2], I32)
            ptr = psum(c1, "e_ptr", 2)
            pl = psum(c1, "e_pl", 2)
            pn = psum(c1, "e_pn", 1)
            xn_ready, xn_kept, xt_ready, xs_ready, lg_ready, lg_read, exp_asked, exp_given, n_asked, n_given, zero_set, pad_out, placed, xr_ready = (
                sem("e_" + s) for s in ("xn_ready", "xn_kept", "xt_ready", "xs_ready", "lg_ready", "lg_read", "exp_asked", "exp_given",
                                        "n_asked", "n_given", "zero_set", "pad_out", "placed", "xr_ready"))
            row_sent = [sem("e_row_sent0"), sem("e_row_sent1")]
            block = c1.enter_context(nc.Block())

            def kept(t):
                return XT[0:P, bass.ds(t * TS, D)]

            @block.sync
            def _(sp):
                for dst, v in ((gm, "gamma"), (bt, "beta"), (br, "br")):
                    sp.dma_start(dst[:], bcast_rows(a["L1_ffn_" + v], P)).then_inc(e_in, 16)
                load_rows(sp, wr[:], a["L1_ffn_Wr"]).then_inc(e_in, 16)
                for e in range(KE):
                    load_rows(sp, w1[:, e * 2 * EXP_H:(e + 1) * 2 * EXP_H], a["L1_ffn_W1"][e]).then_inc(e_in, 16)
                    load_rows(sp, w2[:, e * NH * D:(e + 1) * NH * D], a["L1_ffn_W2"][e]).then_inc(e_in, 16)
                sp.dma_start(b2[:], bcast_rows(a["L1_ffn_b2"].rearrange("e d -> (e d)"), 128)).then_inc(e_in, 16)
                load_cols(sp, b1[:], a["L1_ffn_b1"].rearrange("e h -> (e h)"), KE * NH).then_inc(e_in, 16)
                sp.wait_ge(zero_set, 1)
                sp.dma_start(moe_x_d[2 * N:2 * N + MW, :].rearrange("(p r) c -> p (r c)", p=128), zero[:]).then_inc(pad_out, 16)
                sp.wait_ge(pad_out, 16)

            @block.gpsimd
            def _(pool):
                ch = chain("pool", pool)
                pool.memset(zero[:], 0.0).then_inc(zero_set, 1)
                pool.wait_ge(placed, 1)

                def scatter(t, u, i):
                    at(pool, xr_ready, t + 1, passed["pool"])
                    ch.step(pool.tensor_copy(stage[:, 2 * u:2 * u + 2], pos_x[:, bass.ds(t * 2, 2)]))
                    for k in range(2):
                        pool.indirect_dma_start(moe_x_d, bass.IndirectOffsetOnAxis(ap=stage[:, 2 * u + k:2 * u + k + 1].bitcast(U32), axis=0),
                                                xr[:, u * D:(u + 1) * D], None).then_inc(row_sent[u], 16)

                tiles(pool, scatter, ch, 2)
                for u in range(2):
                    pool.wait_ge(row_sent[u], 32 * (NT // 2))

            @block.vector
            def _(dve):
                ch = chain("dve", dve)
                layer_stats(dve, ch, Rt)
                dve.wait_ge(e_in, E_IN)

                def logits(t, u):
                    at(dve, lg_ready, t + 1, passed["dve"])
                    dve.tensor_tensor(lg[:, bass.ds(t * KE, KE)], pl[0:P, u, 0:KE], br[:], ALU.add).then_inc(lg_read, 1)

                def norm(t, u, i):
                    x_u = xn[:, u * D:(u + 1) * D]
                    if later(t):
                        at(dve, xt_ready, t - 1, passed["dve"])
                        at(dve, xn_kept, t - 1, passed["dve"])
                    ch.step(dve.tensor_scalar(x_u, Rt(t), mean[:, bass.ds(t, 1)], rstd[:, bass.ds(t, 1)], ALU.subtract, ALU.mult))
                    ch.step(dve.tensor_tensor(x_u, x_u, gm[:], ALU.mult))
                    dve.tensor_tensor(x_u, x_u, bt[:], ALU.add).then_inc(xn_ready, 1)
                    if not isinstance(t, int) or t:
                        logits(t - 1, 1 - u)

                tiles(dve, norm, ch, 4)
                logits(NT - 1, 1)
                dve.wait_ge(lg_read, NT)
                l3 = lg[:].rearrange("p (t e) -> p t e", e=KE)
                r3 = rank[:].rearrange("p (t e) -> p t e", e=KE)
                ch.step(dve.memset(rank[:], 0.0))
                for e in range(KE):
                    for f in range(KE):
                        if e != f:
                            ch.step(dve.tensor_tensor(got[:], l3[:, :, f], l3[:, :, e], ALU.is_ge if f < e else ALU.is_gt))
                            ch.step(dve.tensor_tensor(r3[:, :, e], r3[:, :, e], got[:], ALU.add))
                p3 = prod[:].rearrange("p (t e) -> p t e", e=KE)
                o3 = place[:].rearrange("p (t e) -> p t e", e=KE)
                cnt, tot8, first8, ends, wins, delta, over = (e8[:, j * KE:(j + 1) * KE] for j in range(7))
                ch.step(dve.tensor_scalar(prod[:], rank[:], 2.0, None, ALU.is_lt))
                ch.step(dve.tensor_reduce(cnt, prod[:].rearrange("p (t e) -> p e t", e=KE), AX.X, ALU.add))
                dve.sem_inc(n_asked)
                ch.step(dve.tensor_reduce(best[:], l3, AX.X, ALU.max))
                ch.step(dve.tensor_tensor(l3, l3, best[:].unsqueeze(2).to_broadcast([P, NT, KE]), ALU.subtract))
                dve.sem_inc(exp_asked)
                dve.wait_ge(exp_given, 1)
                ch.step(dve.tensor_tensor(lg[:], lg[:], prod[:], ALU.mult))
                ch.step(dve.tensor_reduce(tot[:], l3, AX.X, ALU.add))
                ch.step(dve.reciprocal(tot[:], tot[:]))
                ch.step(dve.tensor_tensor(l3, l3, tot[:].unsqueeze(2).to_broadcast([P, NT, KE]), ALU.mult))
                dve.wait_ge(n_given, 1)
                ch.step(dve.tensor_copy(tot8, pn[0:P, 0, 0:KE]))
                ch.step(dve.tensor_tensor_scan(first8, tot8, tot8, 0.0, ALU.add, ALU.bypass))
                ch.step(dve.tensor_tensor(first8, first8, tot8, ALU.subtract))
                ch.step(dve.tensor_scalar(e8_i[:], tot8, float(MW - 1), None, ALU.add))
                ch.step(dve.tensor_scalar(e8_i[:], e8_i[:], MW.bit_length() - 1, None, ALU.arith_shift_right))
                ch.step(dve.tensor_copy(wins, e8_i[:]))
                ch.step(dve.tensor_tensor_scan(ends, wins, wins, 0.0, ALU.add, ALU.bypass))
                ch.step(dve.tensor_tensor(delta, ends, wins, ALU.subtract))
                ch.step(dve.scalar_tensor_tensor(out=delta, in0=delta, scalar=float(MW), in1=first8, op0=ALU.mult, op1=ALU.subtract))
                ch.step(dve.scalar_tensor_tensor(out=over, in0=wins, scalar=-float(MW), in1=tot8, op0=ALU.mult, op1=ALU.add))
                ch.step(dve.scalar_tensor_tensor(out=first8, in0=pn[0:P, 0, 8:8 + KE], scalar=-1.0, in1=first8, op0=ALU.add, op1=ALU.add))
                for e in range(KE):
                    ch.step(dve.tensor_tensor_scan(o3[:, :, e], p3[:, :, e], p3[:, :, e], first8[:, e:e + 1], ALU.add, ALU.bypass))

                def pick(k, values, out):
                    ch.step(dve.tensor_scalar(prod[:], rank[:], float(k), None, ALU.is_equal))
                    ch.step(dve.tensor_tensor(prod[:], prod[:], values, ALU.mult))
                    ch.step(dve.tensor_reduce(got[:], p3, AX.X, ALU.add))
                    ch.step(dve.tensor_copy(out[:].rearrange("p (t k) -> p t k", k=2)[:, :, k], got[:]))

                for k in range(2):
                    pick(k, place[:], pos_x)
                dve.sem_inc(placed)
                for k in range(2):
                    pick(k, lg[:], share)
                ch.step(dve.tensor_tensor(o3, o3, delta.unsqueeze(1).to_broadcast([P, NT, KE]), ALU.add))
                for k in range(2):
                    pick(k, place[:], pos_y)
                c3 = cmp[:].rearrange("p (w e) -> p w e", e=KE)
                ch.step(dve.tensor_tensor(c3, iota_f[0:P, 0:NWM].unsqueeze(2).to_broadcast([P, NWM, KE]),
                                          ends.unsqueeze(1).to_broadcast([P, NWM, KE]), ALU.is_ge))
                ch.step(dve.tensor_reduce(prod[:, 0:NWM], c3, AX.X, ALU.add))
                ch.step(dve.tensor_scalar(win_e[:], prod[0:1, 0:NWM], float(KE - 1), None, ALU.min))
                ch.step(dve.tensor_tensor(c3, c3, over.unsqueeze(1).to_broadcast([P, NWM, KE]), ALU.mult))
                ch.step(dve.tensor_reduce(prod[:, 0:NWM], c3, AX.X, ALU.add))
                ch.step(dve.scalar_tensor_tensor(out=prod[:, 0:NWM], in0=iota_f[0:P, 0:NWM], scalar=float(MW), in1=prod[:, 0:NWM],
                                                 op0=ALU.mult, op1=ALU.add))
                ch.step(dve.tensor_scalar(win_s[:], prod[0:1, 0:NWM], float(2 * N), None, ALU.min))

            @block.scalar
            def _(act):
                finish_stats_act(act)

                def store_xs(t, u, i):
                    at(act, xn_ready, t + 1, passed["act"])
                    act.copy(kept(t), xn[:, u * D:(u + 1) * D]).then_inc(xn_kept, 1)
                    at(act, xt_ready, t + 1, passed["act"])
                    if later(t):
                        at(act, lg_ready, t - 1, passed["act"])
                    act.copy(xs[:, u * TS:u * TS + 2 * P], ptr[:, u, 0:2 * P]).then_inc(xs_ready, 1)

                tiles(act, store_xs)
                act.wait_ge(exp_asked, 1)
                act.activation(lg[:], lg[:], ACT.Exp).then_inc(exp_given, 1)
                act.wait_ge(xn_kept, NT)

                def send(t, u, i):
                    if later(t):
                        at(act, row_sent[u], i * 32, passed["act"])
                    act.copy(xr[:, u * D:(u + 1) * D], kept(t)).then_inc(xr_ready, 1)

                tiles(act, send)

            @block.tensor
            def _(pe):
                pe.wait_ge(e_in, E_IN)

                def route(t, u):
                    at(pe, xs_ready, t + 1, passed["pe"])
                    if later(t):
                        at(pe, lg_read, t - 1, passed["pe"])
                    for k in range(2):
                        mm = pe.matmul(pl[0:P, u, 0:KE], xs[:, u * TS + k * P:u * TS + (k + 1) * P], wr[:, k * KE:(k + 1) * KE], start=(k == 0), stop=(k == 1))
                    mm.then_inc(lg_ready, 1)

                def transpose_x(t, u, i):
                    at(pe, xn_ready, t + 1, passed["pe"])
                    if later(t):
                        at(pe, xs_ready, t - 1, passed["pe"])
                    for k in range(2):
                        mm = pe.transpose(ptr[:, u, k * P:(k + 1) * P], xn[:, u * D + k * 128:u * D + (k + 1) * 128], ident[0:P, 0:P])
                    mm.then_inc(xt_ready, 1)
                    if not isinstance(t, int) or t:
                        route(t - 1, 1 - u)

                tiles(pe, transpose_x)
                route(NT - 1, 1)
                pe.wait_ge(n_asked, 1)
                pe.matmul(pn[0:P, 0, 0:KE], ones[0:P, 0:P], e8[:, 0:KE], start=True, stop=True)
                pe.matmul(pn[0:P, 0, 8:8 + KE], lower[0:P, 0:P], e8[:, 0:KE], start=True, stop=True).then_inc(n_given, 1)

        with ExitStack() as c2:
            sizes = (2 * 2 * D, 2 * 2 * MW, 2 * 2 * EXP_H, 2 * NH * MW, 2 * 2 * D)
            xw, xT, w1s, hT, yw = (XT[:, sum(sizes[:j]):sum(sizes[:j + 1])] for j in range(5))
            ph = psum(c2, "e_ph", 4)
            py = psum(c2, "e_py", 2)
            pt = psum(c2, "e_pt", 2)
            xw_in = [sem("e_xw_in0"), sem("e_xw_in1")]
            y_out = [sem("e_y_out0"), sem("e_y_out1")]
            transposed, xT_copied, w1_staged, h_ready, h_stored, y_ready, y_added = (
                sem("e_" + s) for s in ("transposed", "xT_copied", "w1_staged", "h_ready", "h_stored", "y_ready", "y_added"))
            block = c2.enter_context(nc.Block())

            @block.sync
            def _(sp):
                def load(t, u, i):
                    start = load_values(sp, win_s, t, 1, 2 * N)[0]
                    if later(t):
                        at(sp, transposed, t - 1, passed["sp"])
                    sp.dma_start(xw[:, u * 2 * D:(u + 1) * 2 * D],
                                 moe_x_d[bass.ds(start, MW), :].rearrange("(p r) c -> p (r c)", p=128)).then_inc(xw_in[u], 16)

                tiles(sp, load, n=NWM)

            @block.gpsimd
            def _(pool):
                def store(t, u, i):
                    at(pool, y_added, 2 * t + 2, passed["pool"])
                    pool.dma_start(moe_y_d[bass.ds(t * MW, MW), :].rearrange("(p r) c -> p (r c)", p=128),
                                   yw[:, u * 2 * D:(u + 1) * 2 * D]).then_inc(y_out[u], 16)

                tiles(pool, store, n=NWM)
                for u in range(2):
                    pool.wait_ge(y_out[u], 16 * (NWM // 2))

            @block.vector
            def _(dve):
                def add(t, u, i):
                    e = load_values(dve, win_e, t, 1, KE - 1)[0]
                    if later(t):
                        at(dve, y_out[u], i * 16, passed["dve"])
                    for v in range(2):
                        at(dve, y_ready, 2 * t + v + 1, passed["dve"])
                        dve.tensor_tensor(yw[:, (2 * u + v) * D:(2 * u + v + 1) * D], py[:, v, 0:D], b2[:, bass.ds(e * D, D)], ALU.add).then_inc(y_added, 1)

                def body(t, u, i):
                    e = load_values(dve, win_e, t, 1, KE - 1)[0]
                    if later(t):
                        at(dve, h_ready, NH * (t - 1), passed["dve"])
                    dve.tensor_copy(w1s[:, u * 2 * EXP_H:(u + 1) * 2 * EXP_H], w1[:, bass.ds(e * 2 * EXP_H, 2 * EXP_H)]).then_inc(w1_staged, 1)
                    if not isinstance(t, int) or t:
                        add(t - 1, 1 - u, i - 1 + u)

                pipelined(dve, body, NWM)
                add(NWM - 1, 1, NWM // 2 - 1)

            @block.scalar
            def _(act):
                def body(t, u, i):
                    e = load_values(act, win_e, t, 1, KE - 1)[0]
                    at(act, transposed, t + 1, passed["act"])
                    act.copy(xT[:, u * 2 * MW:(u + 1) * 2 * MW], pt[:, u, :]).then_inc(xT_copied, 1)
                    if later(t):
                        at(act, y_ready, 2 * t - 2, passed["act"])
                    for m in range(NH):
                        at(act, h_ready, NH * t + m + 1, passed["act"])
                        act.activation(hT[:, (u * NH + m) * MW:(u * NH + m + 1) * MW], ph[:, m, 0:MW], ACT.Gelu,
                                       bias=b1[:, bass.ds(e * NH + m, 1)]).then_inc(h_stored, 1)

                tiles(act, body, n=NWM)

            @block.tensor
            def _(pe):
                def second(t, u):
                    e = load_values(pe, win_e, t, 1, KE - 1)[0]
                    at(pe, h_stored, NH * (t + 1), passed["pe"])
                    for v in range(2):
                        if not isinstance(t, int) or t:
                            at(pe, y_added, 2 * t + v - 1, passed["pe"])
                        for m in range(NH):
                            mm = pe.matmul(py[:, v, 0:D], hT[:, (u * NH + m) * MW + v * 128:(u * NH + m) * MW + (v + 1) * 128],
                                           w2[:, bass.ds((e * NH + m) * D, D)], start=(m == 0), stop=(m == NH - 1))
                        mm.then_inc(y_ready, 1)

                def body(t, u, i):
                    at(pe, xw_in[u], i * 16 + 16, passed["pe"])
                    if later(t):
                        at(pe, xT_copied, t - 1, passed["pe"])
                    for k in range(2):
                        for v in range(2):
                            mm = pe.transpose(pt[:, u, k * MW + v * 128:k * MW + (v + 1) * 128],
                                              xw[:, (2 * u + v) * D + k * 128:(2 * u + v) * D + (k + 1) * 128], ident[:])
                    mm.then_inc(transposed, 1)
                    if not isinstance(t, int) or t:
                        second(t - 1, 1 - u)
                    at(pe, w1_staged, t + 1, passed["pe"])
                    at(pe, xT_copied, t + 1, passed["pe"])
                    for m in range(NH):
                        for k in range(2):
                            mm = pe.matmul(ph[:, m, 0:MW], w1s[:, (2 * u + k) * EXP_H + m * 128:(2 * u + k) * EXP_H + (m + 1) * 128],
                                           xT[:, (2 * u + k) * MW:(2 * u + k + 1) * MW], start=(k == 0), stop=(k == 1))
                        mm.then_inc(h_ready, 1)

                tiles(pe, body, n=NWM)
                second(NWM - 1, 1)

        with ExitStack() as c3:
            yg = sbuf(c3, "e_yg", [P, 2 * 2 * D])
            stage = sbuf(c3, "e_stage2", [P, 2 * 2], I32)
            yg_in = [sem("e_yg_in0"), sem("e_yg_in1")]
            written = [sem("written0"), sem("written1")]
            yg_used = sem("e_yg_used")
            block = c3.enter_context(nc.Block())

            @block.gpsimd
            def _(pool):
                ch = chain("pool", pool)

                def gather(t, u, i):
                    if later(t):
                        at(pool, yg_used, t - 1, passed["pool"])
                    ch.step(pool.tensor_copy(stage[:, 2 * u:2 * u + 2], pos_y[:, bass.ds(t * 2, 2)]))
                    for k in range(2):
                        pool.indirect_dma_start(yg[:, (2 * u + k) * D:(2 * u + k + 1) * D], None, moe_y_d,
                                                bass.IndirectOffsetOnAxis(ap=stage[:, 2 * u + k:2 * u + k + 1].bitcast(U32), axis=0)
                                                ).then_inc(yg_in[u], 16)

                tiles(pool, gather, ch, 2)

            @block.vector
            def _(dve):
                ch = chain("dve", dve)

                def add(t, u, i):
                    at(dve, yg_in[u], i * 32 + 32, passed["dve"])
                    for k in range(2):
                        ch.step(dve.scalar_tensor_tensor(out=Rt(t), in0=yg[:, (2 * u + k) * D:(2 * u + k + 1) * D],
                                                         scalar=share[:, bass.ds(t * 2 + k, 1)], in1=Rt(t), op0=ALU.mult, op1=ALU.add))
                    dve.sem_inc(yg_used)

                tiles(dve, add, ch, 4)

            @block.sync
            def _(sp):
                def store(t, u, i):
                    at(sp, yg_used, t + 1, passed["sp"])
                    sp.dma_start(out[bass.ds(t * P, P), :], Rt(t)).then_inc(written[u], 16)

                tiles(sp, store)
                for u in range(2):
                    sp.wait_ge(written[u], 16 * (NT // 2))
    top.close()


def kernel(**inputs):
    import numpy as np
    import concourse.bacc as bacc
    from concourse.bass_utils import run_bass_kernel_spmd

    nc = bacc.Bacc("TRN2", target_bir_lowering=False, num_devices=1)
    arrays, args = {}, {}
    for name, value in inputs.items():
        value = np.ascontiguousarray(value)
        arrays[f"in_{name}"] = value
        args[name] = nc.dram_tensor(f"in_{name}", value.shape, mybir.dt.from_np(value.dtype), kind="ExternalInput").ap()
    out = nc.dram_tensor("out_nodes", (N, D), F32, kind="ExternalOutput").ap()
    program(nc, args, out)
    result = run_bass_kernel_spmd(nc, [arrays], core_ids=[0])
    return result.results[0]["out_nodes"]
```

```python
from contextlib import ExitStack

import concourse.bass as bass
from concourse import mybir

F32 = mybir.dt.float32
BF16 = mybir.dt.bfloat16
I32 = mybir.dt.int32
U32 = mybir.dt.uint32
I16 = mybir.dt.int16
U16 = mybir.dt.uint16
ALU = mybir.AluOpType
ACT = mybir.ActivationFunctionType
AX = mybir.AxisListType.X

N, D, E, ED = 6250, 256, 200000, 128
P = 125
NT = N // P
EC = E // P
TS = 256
PAD_KEY = 99999
W1 = 512
W2 = 256
NW1 = (E + NT * (W1 - 1)) // W1
NW2 = -(-((E + NT * (W2 - 1)) // W2) // 4) * 4
MAGIC = 12582912.0
EPS = 1e-5
MAX_DEGREE = 512
TOPK = N // 2 - 1
HEADS, HD = 8, 32
FFN_H = 1024
EXPERTS, EXP_H = 8, 512
MW = 256
NWM = (2 * N + EXPERTS * (MW - 1)) // MW


def at(eng, sem, value, passed):
    eng.wait_ge(sem, value)
    eng.sem_inc(passed)


class Chain:

    def __init__(self, eng, sem, passed):
        self.eng, self.sem, self.passed = eng, sem, passed
        self.base, self.k, self.i, self.per = 0, 0, None, 0

    def enter(self, i, per):
        self.i, self.per, self.k = i, per, 0

    def leave(self, times):
        assert self.k == self.per, (self.k, self.per)
        self.base += times * self.per
        self.i, self.k = None, 0

    def step(self, ins):
        ins.then_inc(self.sem, 1)
        self.k += 1
        if self.i is None:
            self.base += 1
            self.k = 0
            self.eng.wait_ge(self.sem, self.base)
        else:
            at(self.eng, self.sem, self.i * self.per + (self.base + self.k), self.passed)


def bcast_rows(ap, rows):
    return ap.rearrange("(a d) -> a d", a=1).to_broadcast([rows, ap.shape[0]])


def program(nc, a, out):
    top = ExitStack()
    uid, section = [0], []

    def sem(name):
        uid[0] += 1
        section.append(nc.alloc_semaphore(f"{name}_{uid[0]}"))
        return section[-1]

    def end_section():
        nc.clear_and_free_semaphores(section)
        nc.all_engine_barrier()
        section.clear()

    def sbuf(ctx, name, shape, dt=F32):
        return ctx.enter_context(nc.sbuf_tensor(name, shape, dt))

    def psum(ctx, name, banks):
        return ctx.enter_context(nc.psum_tensor(name, [128, banks, 512], F32))

    passed = {e: sem("passed_" + e) for e in ("dve", "act", "pe", "sp", "pool")}
    steps = {e: sem("steps_" + e) for e in ("dve", "act", "pool")}
    chains = {}

    def chain(kind, eng):
        if kind not in chains:
            chains[kind] = Chain(eng, steps[kind], passed[kind])
        chains[kind].eng = eng
        return chains[kind]

    def load_values(eng, table, first, count, top_value):
        return nc.values_load_multi_w_load_instructions(table[0:1, bass.ds(first, count)], engines=[eng.engine],
                                                        min_val=0, max_val=top_value)[1]

    rows_d = nc.dram_tensor("rows_by_src", (E + W1, ED + 1), F32, kind="Internal").ap()
    pairs_d = nc.dram_tensor("pairs_by_dst", (E + W2, 2), I32, kind="Internal").ap()
    xn2_d = nc.dram_tensor("xn2_rows", (N, D), F32, kind="Internal").ap()

    moe_x_d = nc.dram_tensor("moe_rows", (2 * N + MW, D), F32, kind="Internal").ap()
    moe_y_d = nc.dram_tensor("moe_results", (NWM * MW, D), F32, kind="Internal").ap()

    R = sbuf(top, "R", [P, NT * TS])
    XT = sbuf(top, "XT", [128, NT * TS])
    ident = sbuf(top, "ident", [128, 128])
    ones = sbuf(top, "ones", [128, 128])
    lower = sbuf(top, "lower", [128, 128])
    blockdiag = sbuf(top, "blockdiag", [128, 128])
    iota_f = sbuf(top, "iota_f", [128, 128])
    win2_b = sbuf(top, "win2_b", [1, NW2], I32)
    win2_s = sbuf(top, "win2_s", [1, NW2], I32)
    unsorted = sbuf(top, "unsorted", [1, 1], I32)
    deg_in = sbuf(top, "deg_in", [P, NT])
    mean = sbuf(top, "mean", [P, NT])
    rstd = sbuf(top, "rstd", [P, NT])
    stats = sbuf(top, "stats", [P, NT * 6])

    def Rt(t):
        return R[:, bass.ds(t * TS, D)]

    def row_stats_loop(dve, ch, read):
        with dve.Fori(0, NT // 2) as i:
            for u in range(2):
                ins = dve.bn_stats(stats[:, bass.ds((i * 2 + u) * 6, 6)], read(i * 2 + u))
            ins.then_inc(stats_done, 1)
        dve.wait_ge(stats_done, stats_target[0])

    stats_done = sem("stats_done")
    stats_target = [0]
    var_ready, sd_ready = sem("var_ready"), sem("sd_ready")
    ln_count = [0, 0]

    def finish_stats_dve(dve, ch):
        s6 = stats[:].rearrange("p (t s) -> p t s", s=6)
        ln_count[0] += 1
        ch.step(dve.tensor_tensor(mean[:], s6[:, :, 1], s6[:, :, 4], ALU.add))
        ch.step(dve.tensor_scalar(mean[:], mean[:], 0.5, None, ALU.mult))
        ch.step(dve.tensor_tensor(rstd[:], s6[:, :, 1], mean[:], ALU.subtract))
        ch.step(dve.tensor_tensor(rstd[:], rstd[:], rstd[:], ALU.mult))
        ch.step(dve.tensor_tensor(s6[:, :, 2], s6[:, :, 2], s6[:, :, 5], ALU.add))
        ch.step(dve.tensor_scalar(s6[:, :, 2], s6[:, :, 2], 1.0 / D, None, ALU.mult))
        ch.step(dve.tensor_tensor(rstd[:], rstd[:], s6[:, :, 2], ALU.add))
        dve.tensor_scalar(rstd[:], rstd[:], EPS, None, ALU.add).then_inc(var_ready, 1)
        dve.wait_ge(sd_ready, ln_count[0])
        ch.step(dve.reciprocal(rstd[:], rstd[:]))

    def finish_stats_act(act):
        ln_count[1] += 1
        act.wait_ge(var_ready, ln_count[1])
        act.activation(rstd[:], rstd[:], ACT.Sqrt).then_inc(sd_ready, 1)

    def layer_stats(dve, ch, read):
        stats_target[0] += NT // 2
        row_stats_loop(dve, ch, read)
        finish_stats_dve(dve, ch)

    def sort_dve(dve, ch, tools, hi, width, tab_b, tab_s, first2):
        mask, cnt, tot, first, col, col_i, cum, row, win_f, ps, counted, summed = tools
        shift = width.bit_length() - 1
        nw = tab_b.shape[1]
        with dve.Fori(0, NT // 2) as i:
            ch.enter(i, 2)
            for u in range(2):
                b = i * 2 + u
                ch.step(dve.tensor_scalar(mask[:, u * EC:(u + 1) * EC], hi[:], iota_f[0:P, bass.ds(b, 1)], 0.0,
                                          ALU.is_equal, ALU.add, accum_out=cnt[:, bass.ds(b, 1)]))
            ch.leave(NT // 2)
        ch.step(dve.tensor_copy(tot[:], cnt[:]))
        dve.sem_inc(counted)
        dve.wait_ge(summed, 1)
        ch.step(dve.tensor_copy(tot[:], ps[0:P, 0, 64:64 + NT]))
        ch.step(dve.tensor_tensor_scan(first[:], tot[:], tot[:], 0.0, ALU.add, ALU.bypass))
        ch.step(dve.tensor_tensor(first2[:], first[:], tot[:], ALU.subtract))
        ch.step(dve.tensor_tensor(first[:], first2[:], ps[0:P, 0, 0:NT], ALU.add))
        ch.step(dve.tensor_scalar(first2[:], first[:], -1.0, None, ALU.add))
        ch.step(dve.tensor_copy(col[0:NT, 0:1], ps[0:NT, 0, 128:129]))
        ch.step(dve.tensor_scalar(col_i[0:NT, 0:1], col[0:NT, 0:1], float(width - 1), None, ALU.add))
        ch.step(dve.tensor_scalar(col_i[0:NT, 1:2], col_i[0:NT, 0:1], shift, None, ALU.arith_shift_right))
        ch.step(dve.tensor_copy(col[0:NT, 1:2], col_i[0:NT, 1:2]))
        ch.step(dve.scalar_tensor_tensor(out=col[0:NT, 2:3], in0=col[0:NT, 1:2], scalar=-float(width),
                                         in1=col[0:NT, 0:1], op0=ALU.mult, op1=ALU.add))
        dve.sem_inc(counted)
        dve.wait_ge(summed, 2)
        ch.step(dve.tensor_copy(col[0:NT, 3:4], ps[0:NT, 0, 129:130]))
        ch.step(dve.tensor_scalar(cum[0:NT, 0:nw], win_f[0:NT, 0:nw], col[0:NT, 3:4], None, ALU.is_ge))
        dve.sem_inc(counted)
        dve.wait_ge(summed, 3)
        h = nw // 2
        for q in range(2):
            ch.step(dve.tensor_copy(tab_b[:, q * h:(q + 1) * h], ps[0:1, 1, 0:h] if q == 0 else ps[0:1, 2, 0:h]))
        for q, bank in ((0, 3), (1, 0)):
            ch.step(dve.scalar_tensor_tensor(out=row[:, q * h:(q + 1) * h], in0=win_f[0:1, q * h:(q + 1) * h],
                                             scalar=float(width), in1=ps[0:1, bank, 0:h], op0=ALU.mult, op1=ALU.add))
        ch.step(dve.tensor_scalar(tab_s[:], row[:, 0:nw], float(E), None, ALU.min))

    def sort_pe(pe, tools, nw):
        mask, cnt, tot, first, col, col_i, cum, row, win_f, ps, counted, summed = tools
        h = nw // 2
        pe.wait_ge(counted, 1)
        pe.matmul(ps[0:P, 0, 0:NT], lower[0:P, 0:P], cnt[:], start=True, stop=True)
        pe.matmul(ps[0:P, 0, 64:64 + NT], ones[0:P, 0:P], cnt[:], start=True, stop=True)
        pe.matmul(ps[0:NT, 0, 128:129], cnt[:], ones[0:P, 0:1], start=True, stop=True).then_inc(summed, 1)
        pe.wait_ge(counted, 2)
        pe.matmul(ps[0:NT, 0, 129:130], lower[0:NT, 0:NT], col[0:NT, 1:2], start=True, stop=False)
        pe.matmul(ps[0:NT, 0, 129:130], ident[0:NT, 0:NT], col[0:NT, 1:2], start=False, stop=True).then_inc(summed, 1)
        pe.wait_ge(counted, 3)
        for q, bank in ((0, 1), (1, 2)):
            pe.matmul(ps[0:1, bank, 0:h], ones[0:NT, 0:1], cum[0:NT, q * h:(q + 1) * h], start=True, stop=True)
        for q, bank in ((0, 3), (1, 0)):
            mm = pe.matmul(ps[0:1, bank, 0:h], col[0:NT, 2:3], cum[0:NT, q * h:(q + 1) * h], start=True, stop=True)
        mm.then_inc(summed, 1)

    def rank_edges(dve, ch, hi, before, mask, rank, pos_f, pos):
        with dve.Fori(0, NT // 2) as i:
            ch.enter(i, 6)
            for u in range(2):
                b = i * 2 + u
                m = mask[:, u * EC:(u + 1) * EC]
                ch.step(dve.tensor_scalar(m, hi[:], iota_f[0:P, bass.ds(b, 1)], None, ALU.is_equal))
                ch.step(dve.tensor_tensor_scan(rank[:], m, m, before[:, bass.ds(b, 1)], ALU.add, ALU.bypass))
                ch.step(dve.copy_predicated(pos_f[:], m.bitcast(U16), rank[:]))
            ch.leave(NT // 2)
        ch.step(dve.tensor_copy(pos[:], pos_f[:]))

    section.clear()

    s12 = ExitStack()
    win1_b = sbuf(s12, "win1_b", [1, NW1], I32)
    win1_s = sbuf(s12, "win1_s", [1, NW1], I32)
    z_idx = sbuf(s12, "z_idx", [P, NT * 2], I32)
    win_f = XT[:, 4 * EC:4 * EC + NW2]
    s01 = ExitStack()
    pair = sbuf(s01, "pair", [P, EC * 2], I32)
    pos_src = sbuf(s01, "pos_src", [P, EC], I32)
    first_dst = sbuf(s01, "first_dst", [P, NT])
    hi_src = sbuf(s01, "hi_src", [P, EC], BF16)
    lo_src = sbuf(s01, "lo_src", [P, EC], BF16)
    hi_dst = sbuf(s01, "hi_dst", [P, EC], BF16)
    lo_dst = sbuf(s01, "lo_dst", [P, EC], BF16)
    iota_b = sbuf(s01, "iota_b", [128, 128], BF16)

    with ExitStack() as ctx:
        src_i = sbuf(ctx, "src_i", [P, EC], I32)
        dst_i = sbuf(ctx, "dst_i", [P, EC], I32)
        src_f = XT[0:P, 0 * EC:1 * EC]
        dst_f = XT[0:P, 1 * EC:2 * EC]
        pos_f = XT[0:P, 2 * EC:3 * EC]
        rank = XT[0:P, 3 * EC:4 * EC]
        mask = sbuf(ctx, "mask", [P, 2 * EC], BF16)
        free_i = sbuf(ctx, "free_i", [128, 128], I32)
        part_i = sbuf(ctx, "part_i", [128, 1], I32)
        fblk_i = sbuf(ctx, "fblk_i", [128, 128], I32)
        pblk_i = sbuf(ctx, "pblk_i", [128, 1], I32)
        fblk_f = sbuf(ctx, "fblk_f", [128, 128])
        small = sbuf(ctx, "small", [128, 8])
        win_i = sbuf(ctx, "win_i", [128, NW2], I32)
        cum = sbuf(ctx, "cum", [128, NW2])
        row = sbuf(ctx, "row", [1, NW2])
        cnt = sbuf(ctx, "cnt", [P, NT])
        tot = sbuf(ctx, "tot", [P, NT])
        first = sbuf(ctx, "first", [P, NT])
        first_src = sbuf(ctx, "first_src", [P, NT])
        col = sbuf(ctx, "col", [64, 8])
        col_i = sbuf(ctx, "col_i", [64, 2], I32)
        pad = sbuf(ctx, "pad", [128, 4 * (ED + 1)])
        pad_i = sbuf(ctx, "pad_i", [128, 2 * W2 // 128], I32)
        next_i = sbuf(ctx, "next_i", [P, 1], I32)
        next_f = sbuf(ctx, "next_f", [P, 1])
        falls = sbuf(ctx, "falls", [P, 2])
        ps = psum(ctx, "ps_sort", 4)

        ids_in, x_in, iotas, pads = (sem(s) for s in ("ids_in", "x_in", "iotas", "pads"))
        falls_ready, falls_summed = sem("falls_ready"), sem("falls_summed")
        counted, summed, pads_set = sem("counted"), sem("summed"), sem("pads_set")
        src_tools = (mask, cnt, tot, first, col, col_i, cum, row, win_f, ps, counted, summed)
        block = ctx.enter_context(nc.Block())

        @block.sync
        def _(sp):
            sp.dma_start(src_i[:], a["src"].rearrange("(p c) -> p c", c=EC)).then_inc(ids_in, 16)
            sp.dma_start(dst_i[:], a["dst"].rearrange("(p c) -> p c", c=EC)).then_inc(ids_in, 16)
            dst2 = a["dst"].rearrange("(p c) -> p c", c=EC)
            sp.wait_ge(pads_set, 5)
            with nc.allow_non_contiguous_dma(reason="one number a partition"):
                sp.dma_start(next_i[0:P - 1, :], dst2[1:P, 0:1]).then_inc(ids_in, 16)
            sp.dma_start(R[:].rearrange("p (t d) -> p t d", d=TS),
                         a["x"].rearrange("(t p) d -> p t d", p=P)).then_inc(x_in, 16)
            sp.dma_start(rows_d[E:E + W1, :].rearrange("(p r) c -> p (r c)", p=128), pad[:]).then_inc(pads, 16)
            sp.dma_start(pairs_d[E:E + W2, :].rearrange("(p r) c -> p (r c)", p=128), pad_i[:]).then_inc(pads, 16)
            sp.wait_ge(pads, 32)
            sp.wait_ge(x_in, 16)

        @block.gpsimd
        def _(pool):
            pool.iota(free_i[:], pattern=[[1, 128]], base=0, channel_multiplier=0).then_inc(iotas, 1)
            pool.iota(part_i[:], pattern=[[0, 1]], base=0, channel_multiplier=1).then_inc(iotas, 1)
            pool.iota(fblk_i[:], pattern=[[1, 4], [0, 32]], base=0, channel_multiplier=0).then_inc(iotas, 1)
            pool.iota(win_i[:], pattern=[[1, NW2]], base=0, channel_multiplier=0).then_inc(iotas, 1)
            pool.memset(pad[:], 0.0).then_inc(pads_set, 1)
            pool.memset(pad_i[:], 0).then_inc(pads_set, 1)
            pool.memset(next_i[:], PAD_KEY).then_inc(pads_set, 1)
            pool.wait_ge(pads_set, 3)
            pool.memset(pad[:].rearrange("p (r c) -> p r c", c=ED + 1)[:, :, ED:], float(PAD_KEY)).then_inc(pads_set, 1)
            pool.memset(pad_i[:].rearrange("p (r c) -> p r c", c=2)[:, :, 1:], PAD_KEY).then_inc(pads_set, 1)
            pool.memset(ones[:], 1.0).then_inc(iotas, 1)

        @block.vector
        def _(dve):
            ch = chain("dve", dve)
            dve.wait_ge(iotas, 5)
            ch.step(dve.tensor_copy(iota_f[:], free_i[:]))
            ch.step(dve.tensor_copy(iota_b[:], free_i[:]))
            ch.step(dve.tensor_copy(small[:, 0:1], part_i[:]))
            ch.step(dve.tensor_scalar(ident[:], iota_f[:], small[:, 0:1], None, ALU.is_equal))
            ch.step(dve.tensor_scalar(lower[:], iota_f[:], small[:, 0:1], None, ALU.is_gt))
            ch.step(dve.tensor_scalar(pblk_i[:], part_i[:], 5, None, ALU.arith_shift_right))
            ch.step(dve.tensor_copy(small[:, 1:2], pblk_i[:]))
            ch.step(dve.tensor_copy(fblk_f[:], fblk_i[:]))
            ch.step(dve.tensor_scalar(blockdiag[:], fblk_f[:], small[:, 1:2], None, ALU.is_equal))
            ch.step(dve.tensor_copy(win_f[:], win_i[:]))
            ch.step(dve.memset(pos_f[:], 0.0))
            dve.wait_ge(ids_in, 48)
            for ids, keys, hi, lo, word in ((src_i, src_f, hi_src, lo_src, 0), (dst_i, dst_f, hi_dst, lo_dst, 1)):
                ch.step(dve.tensor_copy(keys[:], ids[:]))
                ch.step(dve.tensor_copy(pair[:].rearrange("p (c w) -> p c w", w=2)[:, :, word], ids[:]))
                ch.step(dve.tensor_scalar(rank[:], keys[:], -float(P // 2), 1.0 / P, ALU.add, ALU.mult))
                ch.step(dve.tensor_scalar(hi[:], rank[:], MAGIC, -MAGIC, ALU.add, ALU.add))
                ch.step(dve.scalar_tensor_tensor(out=lo[:], in0=hi[:], scalar=-float(P), in1=keys[:],
                                                 op0=ALU.mult, op1=ALU.add))
            ch.step(dve.tensor_tensor(rank[:, 0:EC - 1], dst_f[:, 0:EC - 1], dst_f[:, 1:EC], ALU.is_gt))
            ch.step(dve.tensor_reduce(falls[:, 0:1], rank[:, 0:EC - 1], AX.X, ALU.add))
            ch.step(dve.tensor_copy(next_f[:], next_i[:]))
            ch.step(dve.tensor_tensor(falls[:, 1:2], dst_f[:, EC - 1:EC], next_f[:], ALU.is_gt))
            ch.step(dve.tensor_tensor(falls[:, 0:1], falls[:, 0:1], falls[:, 1:2], ALU.add))
            dve.sem_inc(falls_ready)
            dve.wait_ge(falls_summed, 1)
            ch.step(dve.tensor_copy(unsorted[:], ps[0:1, 3, 0:1]))
            sort_dve(dve, ch, src_tools, hi_src, W1, win1_b, win1_s, first_src)
            rank_edges(dve, ch, hi_src, first_src, mask, rank, pos_f, pos_src)

        @block.tensor
        def _(pe):
            pe.wait_ge(falls_ready, 1)
            pe.matmul(ps[0:1, 3, 0:1], falls[:, 0:1], ones[0:P, 0:1], start=True, stop=True).then_inc(falls_summed, 1)
            sort_pe(pe, src_tools, NW1)

    def tiles(eng, body, ch=None, per=0, n=NT):
        body(0, 0, 0)
        body(1, 1, 0)
        with eng.Fori(1, n // 2) as i:
            if ch:
                ch.base -= per
                ch.enter(i, per)
            body(2 * i, 0, i)
            body(2 * i + 1, 1, i)
        if ch:
            ch.base += per
            ch.leave(n // 2 - 1)

    def later(t):
        return not isinstance(t, int) or t >= 2

    def XTt(t, k):
        return XT[:, bass.ds(t * TS + k * P, P)]

    with ExitStack() as ctx:
        HC = 16
        ring = sbuf(ctx, "ring", [P, 2 * HC * (ED + 1)])
        stage = sbuf(ctx, "stage", [P, 2 * HC], I32)
        w_qkv = sbuf(ctx, "w_qkv", [128, 2 * 768])
        w_out = sbuf(ctx, "w_out", [128, 2 * D])
        w_mix = sbuf(ctx, "w_mix", [128, 2 * D])
        wcv = sbuf(ctx, "wcv", [P, 4 * D])
        nvec = sbuf(ctx, "nvec", [P, 2 * NT])
        b_sum = sbuf(ctx, "b_sum", [P, D])
        gamma = sbuf(ctx, "gamma", [P, D])
        lo1 = sbuf(ctx, "lo1", [P, 2 * 8 * P], BF16)
        hi1 = sbuf(ctx, "hi1", [P, 2 * 8 * NT], BF16)
        deg_out = sbuf(ctx, "deg_out", [P, NT])
        xn = sbuf(ctx, "xn", [P, 2 * D])
        xs = sbuf(ctx, "xs", [128, 2 * TS])
        cv = sbuf(ctx, "cv", [P, 2 * 2 * D])
        kmax_t = sbuf(ctx, "kmax_t", [128, NT * 2])
        kmax = sbuf(ctx, "kmax", [128, 2])
        neg_kmax = sbuf(ctx, "neg_kmax", [1, D])
        k_exp = sbuf(ctx, "k_exp", [P, 2 * D])
        v_one = sbuf(ctx, "v_one", [P, 2 * 2 * 129])
        q_sb = sbuf(ctx, "q_sb", [P, 2 * D])
        q_m = sbuf(ctx, "q_m", [P, 2 * HEADS])
        q_s = sbuf(ctx, "q_s", [P, 2 * HEADS])
        rsum = sbuf(ctx, "rsum", [128, 2])
        ctxn = sbuf(ctx, "ctxn", [128, 2 * 128])
        ctxt = sbuf(ctx, "ctxt", [128, 2 * 128])
        mixed = sbuf(ctx, "mixed", [P, 2 * D])
        pqkv = psum(ctx, "pqkv", 4)
        pq, pkv = pqkv[:, 0:2, :], pqkv[:, 2:4, :]
        dst_tools = (XT[0:P, 5 * EC:6 * EC].bitcast(BF16), sbuf(ctx, "d_cnt", [P, NT]), sbuf(ctx, "d_tot", [P, NT]),
                     sbuf(ctx, "d_first", [P, NT]), sbuf(ctx, "d_col", [64, 8]), sbuf(ctx, "d_col_i", [64, 2], I32),
                     XT[:, 0:NW2], XT[0:1, NW2:2 * NW2], win_f, pqkv, sem("d_counted"), sem("d_summed"))
        ptr = psum(ctx, "ptr", 2)
        pctx = psum(ctx, "pctx", 1)
        phist = psum(ctx, "phist", 1)

        weights_in, mix_w_in, v_ones = sem("weights_in"), sem("mix_w_in"), sem("v_ones")
        ring_in = [sem("ring_in0"), sem("ring_in1")]
        ring_out = [sem("ring_out0"), sem("ring_out1")]
        half_staged = sem("half_staged")
        onehot_ready, counted_to = sem("onehot_ready"), sem("counted_to")
        xn_ready, xt_ready, xt_stored = sem("xn_ready"), sem("xt_ready"), sem("xt_stored")
        cv_ready, sg_ready = sem("cv_ready"), sem("sg_ready")
        kt_ready, kt_read, kmax_ready, kmax_row, kmax_row_in = (sem(s) for s in ("kt_ready", "kt_read", "kmax_ready", "kmax_row", "kmax_row_in"))
        qkv_ready, kv_stored, qs_ready, qexp_ready, qn_ready, qt_ready, qt_stored, ctx_done = (
            sem(s) for s in ("qkv_ready", "kv_stored", "qs_ready", "qexp_ready", "qn_ready", "qt_ready", "qt_stored", "ctx_done"))
        xs_ready, qs2_ready = sem("xs_ready"), sem("qs2_ready")
        ctxn_ready, ctxt_ready, ctxt_in, wmix_ready, wmix_in = (sem(s) for s in ("ctxn_ready", "ctxt_ready", "ctxt_in", "wmix_ready", "wmix_in"))
        o_ready, o_read = sem("o_ready"), sem("o_read")
        block = ctx.enter_context(nc.Block())
        attr = a["edge_attr_128"].rearrange("(p c) d -> p c d", c=EC)
        ring4 = ring[:].rearrange("p (h c w) -> p h c w", h=2, c=HC)
        pair_w = pair[:].rearrange("p (c w) -> p c w", w=2)

        @block.sync
        def _(sp):
            sp.dma_start(w_qkv[:].rearrange("p (k n) -> p k n", k=2), a["L0_mix_Wqkv"].rearrange("(k p) n -> p k n", p=128)).then_inc(mix_w_in, 16)
            sp.dma_start(w_out[:].rearrange("p (k n) -> p k n", k=2), a["L0_mix_Wout"].rearrange("(k p) n -> p k n", p=128)).then_inc(mix_w_in, 16)
            for j, name in enumerate(("W_cent", "b_cent", "W_vor", "b_vor")):
                v = a["L0_gnn_" + name]
                v = v.rearrange("a d -> (a d)") if len(v.shape) == 2 else v
                sp.dma_start(wcv[:, j * D:(j + 1) * D], bcast_rows(v, P)).then_inc(weights_in, 16)
            sp.dma_start(b_sum[:], bcast_rows(a["L0_gnn_b_sum"], P)).then_inc(weights_in, 16)
            sp.dma_start(gamma[:], bcast_rows(a["L0_mix_gamma"], P)).then_inc(weights_in, 16)
            with nc.allow_non_contiguous_dma(reason="one number a node"):
                for j, name in enumerate(("node_vec1_n2", "node_vec1")):
                    sp.dma_start(nvec[:, j * NT:(j + 1) * NT], a[name].rearrange("(t p) a -> p (t a)", p=P)).then_inc(weights_in, 16)

            def load(i):
                for h in range(2):
                    if not isinstance(i, int):
                        at(sp, ring_out[h], i * 16 * HC, passed["sp"])
                    sp.dma_start(ring4[:, h, :, 0:ED], attr[:, bass.ds((2 * i + h) * HC, HC), :]).then_inc(ring_in[h], 16)

            load(0)
            with sp.Fori(1, EC // (2 * HC)) as i:
                load(i)

        @block.gpsimd
        def _(pool):
            pool.memset(v_one[:], 1.0).then_inc(v_ones, 1)

            def stage_half(i, h):
                at(pool, ring_in[h], i * 16 + 16, passed["pool"])
                pool.tensor_copy(ring4[:, h, :, ED], pair_w[:, bass.ds((2 * i + h) * HC, HC), 0]).then_inc(half_staged, 1)
                pool.tensor_copy(stage[:, h * HC:(h + 1) * HC], pos_src[:, bass.ds((2 * i + h) * HC, HC)]).then_inc(half_staged, 1)

            def scatter_half(i, h, stage_next):
                at(pool, half_staged, i * 4 + 2 * h + 2, passed["pool"])
                for j in range(HC):
                    if j == HC - 3:
                        stage_next()
                    pool.indirect_dma_start(rows_d, bass.IndirectOffsetOnAxis(ap=stage[:, h * HC + j:h * HC + j + 1].bitcast(U32), axis=0),
                                            ring4[:, h, j, :], None).then_inc(ring_out[h], 16)

            stage_half(0, 0)
            with pool.Fori(0, EC // (2 * HC) - 1) as i:
                scatter_half(i, 0, lambda: stage_half(i, 1))
                scatter_half(i, 1, lambda: stage_half(i + 1, 0))
            scatter_half(EC // (2 * HC) - 1, 0, lambda: stage_half(EC // (2 * HC) - 1, 1))
            scatter_half(EC // (2 * HC) - 1, 1, lambda: None)
            for h in range(2):
                pool.wait_ge(ring_out[h], 16 * HC * (EC // (2 * HC)))

        @block.vector
        def _(dve):
            ch = chain("dve", dve)

            def onehots(lo, hi, which):
                def body(t, u, i):
                    if later(t) or which:
                        at(dve, counted_to, t - 1 + which * (EC // 8), passed["dve"])
                    dve.tensor_tensor(lo1[:, u * 8 * P:(u + 1) * 8 * P].rearrange("p (c n) -> p c n", c=8),
                                      iota_b[0:P, 0:P].unsqueeze(1).to_broadcast([P, 8, P]),
                                      lo[:, bass.ds(t * 8, 8)].unsqueeze(2).to_broadcast([P, 8, P]), ALU.is_equal)
                    dve.tensor_tensor(hi1[:, u * 8 * NT:(u + 1) * 8 * NT].rearrange("p (c n) -> p c n", c=8),
                                      iota_b[0:P, 0:NT].unsqueeze(1).to_broadcast([P, 8, NT]),
                                      hi[:, bass.ds(t * 8, 8)].unsqueeze(2).to_broadcast([P, 8, NT]), ALU.is_equal).then_inc(onehot_ready, 1)
                tiles(dve, body, n=EC // 8)

            sort_dve(dve, ch, dst_tools, hi_dst, W2, win2_b, win2_s, first_dst)
            onehots(lo_src, hi_src, 0)
            onehots(lo_dst, hi_dst, 1)
            dve.wait_ge(counted_to, 2 * (EC // 8))
            ch.step(dve.tensor_copy(deg_out[:], phist[0:P, 0, 0:NT]))
            ch.step(dve.tensor_copy(deg_in[:], phist[0:P, 0, 64:64 + NT]))
            z3 = z_idx[:].rearrange("p (t k) -> p t k", k=2)
            ch.step(dve.tensor_scalar(z3[:, :, 0], deg_in[:], float(MAX_DEGREE - 1), None, ALU.min))
            ch.step(dve.tensor_scalar(z3[:, :, 1], deg_out[:], float(MAX_DEGREE - 1), None, ALU.min))

            layer_stats(dve, ch, Rt)
            dve.wait_ge(weights_in, 128)

            def add_terms(t, u):
                at(dve, sg_ready, t + 1, passed["dve"])
                for k in range(2):
                    ch.step(dve.tensor_tensor(Rt(t), Rt(t), cv[:, (2 * u + k) * D:(2 * u + k + 1) * D], ALU.add))

            def norm(t, u, i):
                if later(t):
                    at(dve, xt_ready, t - 1, passed["dve"])
                    add_terms(t - 2, u)
                x_u = xn[:, u * D:(u + 1) * D]
                dve.tensor_scalar(x_u, Rt(t), mean[:, bass.ds(t, 1)], rstd[:, bass.ds(t, 1)], ALU.subtract, ALU.mult).then_inc(xn_ready, 1)
                at(dve, xn_ready, t + 1, passed["dve"])
                ch.step(dve.tensor_tensor(Rt(t), Rt(t), x_u, ALU.add))
                for k in range(2):
                    ins = dve.scalar_tensor_tensor(out=cv[:, (2 * u + k) * D:(2 * u + k + 1) * D], in0=wcv[:, 2 * k * D:(2 * k + 1) * D],
                                                   scalar=nvec[:, bass.ds(t + k * NT, 1)], in1=wcv[:, (2 * k + 1) * D:(2 * k + 2) * D],
                                                   op0=ALU.mult, op1=ALU.add)
                ins.then_inc(cv_ready, 1)

            tiles(dve, norm, ch, 6)
            add_terms(NT - 2, 0)
            add_terms(NT - 1, 1)

            def max_k(t, u, i):
                at(dve, kt_ready, t + 1, passed["dve"])
                dve.tensor_reduce(kmax_t[:, bass.ds(t * 2, 2)], pkv[:, u, 0:2 * P].rearrange("p (k n) -> p k n", k=2), AX.X, ALU.max).then_inc(kt_read, 1)

            tiles(dve, max_k)
            dve.wait_ge(kt_read, NT)
            dve.tensor_reduce(kmax[:], kmax_t[:].rearrange("p (t k) -> p k t", k=2), AX.X, ALU.max).then_inc(kmax_ready, 1)
            dve.wait_ge(kmax_row, 1)
            dve.tensor_scalar(neg_kmax[:], pctx[0:1, 0, 0:D], -1.0, None, ALU.mult).then_inc(kmax_row_in, 1)

            def q_softmax(t, u, i):
                at(dve, qkv_ready, t + 1, passed["dve"])
                q3 = pq[0:P, u, 0:D].rearrange("p (h d) -> p h d", h=HEADS)
                s3 = q_sb[:, u * D:(u + 1) * D].rearrange("p (h d) -> p h d", h=HEADS)
                qm, qs = q_m[:, u * HEADS:(u + 1) * HEADS], q_s[:, u * HEADS:(u + 1) * HEADS]
                ch.step(dve.tensor_reduce(qm, q3, AX.X, ALU.max))
                if later(t):
                    at(dve, qt_ready, t - 1, passed["dve"])
                dve.tensor_tensor(s3, q3, qm.unsqueeze(2).to_broadcast([P, HEADS, HD]), ALU.subtract).then_inc(qs_ready, 1)
                at(dve, qexp_ready, t + 1, passed["dve"])
                ch.step(dve.tensor_reduce(qs, s3, AX.X, ALU.add))
                ch.step(dve.reciprocal(qs, qs))
                dve.tensor_tensor(s3, s3, qs.unsqueeze(2).to_broadcast([P, HEADS, HD]), ALU.mult).then_inc(qn_ready, 1)

            tiles(dve, q_softmax, ch, 6)
            dve.wait_ge(ctx_done, NT)
            for m in range(2):
                ch.step(dve.reciprocal(rsum[:, m:m + 1], pctx[:, 0, 129 * m + 128:129 * m + 129]))
                ch.step(dve.tensor_scalar(ctxn[:, m * 128:(m + 1) * 128], pctx[:, 0, 129 * m:129 * m + 128], rsum[:, m:m + 1], None, ALU.mult))
                dve.tensor_tensor(ctxn[:, m * 128:(m + 1) * 128], ctxn[:, m * 128:(m + 1) * 128], blockdiag[:], ALU.mult).then_inc(ctxn_ready, 1)
            dve.wait_ge(ctxt_ready, 2)
            for m in range(2):
                dve.tensor_copy(ctxt[:, m * 128:(m + 1) * 128], ptr[:, m, 0:128]).then_inc(ctxt_in, 1)
            dve.wait_ge(wmix_ready, 2)
            for m in range(2):
                dve.tensor_scalar(w_mix[:, m * D:(m + 1) * D], pq[:, m, 0:D], float(HD) ** -0.5, None, ALU.mult).then_inc(wmix_in, 1)

            stats_target[0] += NT

            def out_stats(t, u, i):
                at(dve, o_read, t + 1, passed["dve"])
                dve.bn_stats(stats[:, bass.ds(t * 6, 6)], XT[0:P, bass.ds(t * TS, D)]).then_inc(stats_done, 1)

            tiles(dve, out_stats)
            dve.wait_ge(stats_done, stats_target[0])
            finish_stats_dve(dve, ch)

            def add_mix(t, u, i):
                m_u = mixed[:, u * D:(u + 1) * D]
                ch.step(dve.tensor_scalar(m_u, XT[0:P, bass.ds(t * TS, D)], mean[:, bass.ds(t, 1)], rstd[:, bass.ds(t, 1)], ALU.subtract, ALU.mult))
                ch.step(dve.tensor_tensor(m_u, m_u, gamma[:], ALU.mult))
                ch.step(dve.tensor_tensor(Rt(t), Rt(t), m_u, ALU.add))
                ch.step(dve.scalar_tensor_tensor(out=Rt(t), in0=b_sum[:], scalar=deg_out[:, bass.ds(t, 1)], in1=Rt(t), op0=ALU.mult, op1=ALU.add))

            tiles(dve, add_mix, ch, 8)

        @block.scalar
        def _(act):
            finish_stats_act(act)

            def store_xt(t, u, i):
                at(act, cv_ready, t + 1, passed["act"])
                act.activation(cv[:, u * 2 * D:(u + 1) * 2 * D], cv[:, u * 2 * D:(u + 1) * 2 * D], ACT.Sigmoid).then_inc(sg_ready, 1)
                at(act, xt_ready, t + 1, passed["act"])
                act.copy(XT[:, bass.ds(t * TS, 2 * P)], ptr[:, u, 0:2 * P]).then_inc(xt_stored, 1)

            tiles(act, store_xt)
            act.wait_ge(v_ones, 1)

            def store_qt(t, u):
                at(act, qt_ready, t + 1, passed["act"])
                act.copy(XT[:, bass.ds(t * TS, 2 * P)], ptr[:, u, 0:2 * P]).then_inc(qt_stored, 1)

            def exps(t, u, i):
                if later(t):
                    at(act, qkv_ready, t - 1, passed["act"])
                act.copy(xs[:, u * TS:u * TS + 2 * P], XT[:, bass.ds(t * TS, 2 * P)]).then_inc(xs_ready, 1)
                at(act, qkv_ready, t + 1, passed["act"])
                if later(t):
                    at(act, ctx_done, t - 1, passed["act"])
                act.activation(k_exp[:, u * D:(u + 1) * D], pkv[0:P, u, 0:D], ACT.Exp).then_inc(kv_stored, 1)
                act.copy(v_one[:, u * 258:(u + 1) * 258].rearrange("p (m c) -> p m c", m=2)[:, :, 0:128],
                         pkv[0:P, u, D:2 * D].rearrange("p (m c) -> p m c", m=2)).then_inc(kv_stored, 1)
                at(act, qs_ready, t + 1, passed["act"])
                act.activation(q_sb[:, u * D:(u + 1) * D], q_sb[:, u * D:(u + 1) * D], ACT.Exp).then_inc(qexp_ready, 1)
                if not isinstance(t, int) or t >= 1:
                    store_qt(t - 1, 1 - u)

            tiles(act, exps)
            store_qt(NT - 1, 1)

            def store_out(t, u, i):
                if later(t):
                    at(act, o_ready, t - 1, passed["act"])
                act.copy(xs[:, u * TS:u * TS + 2 * P], XT[:, bass.ds(t * TS, 2 * P)]).then_inc(qs2_ready, 1)
                at(act, o_ready, t + 1, passed["act"])
                act.copy(XT[0:P, bass.ds(t * TS, D)], pq[0:P, u, 0:D]).then_inc(o_read, 1)

            tiles(act, store_out)
            finish_stats_act(act)

        @block.tensor
        def _(pe):
            def count(which):
                def body(t, u, i):
                    at(pe, onehot_ready, t + 1 + which * (EC // 8), passed["pe"])
                    for j in range(8):
                        mm = pe.matmul(phist[0:P, 0, which * 64:which * 64 + NT], lo1[:, (u * 8 + j) * P:(u * 8 + j + 1) * P],
                                       hi1[:, (u * 8 + j) * NT:(u * 8 + j + 1) * NT],
                                       start=(isinstance(t, int) and t == 0 and j == 0), stop=True, skip_group_check=True)
                    mm.then_inc(counted_to, 1)
                tiles(pe, body, n=EC // 8)

            sort_pe(pe, dst_tools, NW2)
            count(0)
            count(1)

            def transpose_x(t, u, i):
                at(pe, xn_ready, t + 1, passed["pe"])
                if later(t):
                    at(pe, xt_stored, t - 1, passed["pe"])
                for k in range(2):
                    mm = pe.transpose(ptr[:, u, k * P:(k + 1) * P], xn[:, u * D + k * 128:u * D + (k + 1) * 128], ident[0:P, 0:P])
                mm.then_inc(xt_ready, 1)

            tiles(pe, transpose_x)
            pe.wait_ge(mix_w_in, 32)
            pe.wait_ge(xt_stored, NT)

            def k_transposed(t, u, i):
                if later(t):
                    at(pe, kt_read, t - 1, passed["pe"])
                for m in range(2):
                    for k in range(2):
                        mm = pe.matmul(pkv[:, u, m * P:(m + 1) * P], w_qkv[:, k * 768 + D + m * 128:k * 768 + D + (m + 1) * 128],
                                       XTt(t, k), start=(k == 0), stop=(k == 1))
                mm.then_inc(kt_ready, 1)

            tiles(pe, k_transposed)
            pe.wait_ge(kmax_ready, 1)
            for m in range(2):
                mm = pe.matmul(pctx[0:1, 0, m * 128:(m + 1) * 128], kmax[:, m:m + 1], ident[:], start=True, stop=True)
            mm.then_inc(kmax_row, 1)
            pe.wait_ge(kmax_row_in, 1)

            def context(t, u):
                at(pe, kv_stored, 2 * t + 2, passed["pe"])
                first = isinstance(t, int) and t == 0
                for m in range(2):
                    mm = pe.matmul(pctx[:, 0, m * 129:(m + 1) * 129], k_exp[:, u * D + m * 128:u * D + (m + 1) * 128],
                                   v_one[:, u * 258 + m * 129:u * 258 + (m + 1) * 129], start=first and m == 0, stop=True, skip_group_check=True)
                mm.then_inc(ctx_done, 1)
                at(pe, qn_ready, t + 1, passed["pe"])
                if later(t):
                    at(pe, qt_stored, t - 1, passed["pe"])
                for k in range(2):
                    mm = pe.transpose(ptr[:, u, k * P:(k + 1) * P], q_sb[:, u * D + k * 128:u * D + (k + 1) * 128], ident[0:P, 0:P])
                mm.then_inc(qt_ready, 1)

            def qkv(t, u, i):
                at(pe, xs_ready, t + 1, passed["pe"])
                if later(t):
                    at(pe, kv_stored, 2 * t - 2, passed["pe"])
                    at(pe, qs_ready, t - 1, passed["pe"])
                for k in range(2):
                    pe.matmul(pq[0:P, u, 0:D], xs[:, u * TS + k * P:u * TS + (k + 1) * P], w_qkv[:, k * 768:k * 768 + D], start=(k == 0), stop=(k == 1))
                for k in range(2):
                    pe.matmul(pkv[0:P, u, 0:D], xs[:, u * TS + k * P:u * TS + (k + 1) * P], w_qkv[:, k * 768 + D:k * 768 + 2 * D], start=(k == 0), stop=False)
                pe.matmul(pkv[0:P, u, 0:D], ones[0:1, 0:P], neg_kmax[:], start=False, stop=True)
                for k in range(2):
                    mm = pe.matmul(pkv[0:P, u, D:2 * D], xs[:, u * TS + k * P:u * TS + (k + 1) * P], w_qkv[:, k * 768 + 2 * D:k * 768 + 3 * D], start=(k == 0), stop=(k == 1))
                mm.then_inc(qkv_ready, 1)
                if not isinstance(t, int) or t >= 1:
                    context(t - 1, 1 - u)

            tiles(pe, qkv)
            context(NT - 1, 1)
            pe.wait_ge(ctxn_ready, 2)
            pe.wait_ge(qt_stored, NT)
            for m in range(2):
                pe.transpose(ptr[:, m, 0:128], ctxn[:, m * 128:(m + 1) * 128], ident[:]).then_inc(ctxt_ready, 1)
            pe.wait_ge(ctxt_in, 2)
            for m in range(2):
                pe.matmul(pq[:, m, 0:D], ctxt[:, m * 128:(m + 1) * 128], w_out[:, m * D:(m + 1) * D], start=True, stop=True).then_inc(wmix_ready, 1)
            pe.wait_ge(wmix_in, 2)

            def attend(t, u, i):
                at(pe, qs2_ready, t + 1, passed["pe"])
                if later(t):
                    at(pe, o_read, t - 1, passed["pe"])
                for k in range(2):
                    mm = pe.matmul(pq[0:P, u, 0:D], xs[:, u * TS + k * P:u * TS + (k + 1) * P], w_mix[:, k * D:(k + 1) * D], start=(k == 0), stop=(k == 1))
                mm.then_inc(o_ready, 1)

            tiles(pe, attend)

    with s01, ExitStack() as ctx:
        pos_dst = sbuf(ctx, "pos_dst", [P, EC], I32)
        mask = sbuf(ctx, "mask2", [P, 2 * EC], BF16)
        rank, pos_f = XT[0:P, 0:EC], XT[0:P, EC:2 * EC]
        stage = sbuf(ctx, "stage2", [P, 2 * 8], I32)
        pstage = sbuf(ctx, "pstage", [P, 2 * 16], I32)
        pair_out = [sem("pair_out0"), sem("pair_out1")]
        pairs_out, dst_ranked, rank_steps, stage_steps = (sem(s) for s in ("pairs_out", "dst_ranked", "rank_steps", "stage_steps"))
        block = ctx.enter_context(nc.Block())

        @block.sync
        def _(sp):
            falls = sp.value_load(unsorted[0:1, 0:1], min_val=0, max_val=E)
            with sp.If(falls == 0):
                sp.dma_start(pairs_d[0:E, :].rearrange("(p c) w -> p (c w)", p=P), pair[:]).then_inc(pairs_out, 16)
                sp.wait_ge(pairs_out, 16)

        @block.vector
        def _(dve):
            falls = dve.value_load(unsorted[0:1, 0:1], min_val=0, max_val=E)
            with dve.If(falls != 0):
                ch = Chain(dve, rank_steps, passed["dve"])
                ch.step(dve.memset(pos_f, 0.0))
                rank_edges(dve, ch, hi_dst, first_dst, mask, rank, pos_f, pos_dst)
                dve.sem_inc(dst_ranked)

        @block.gpsimd
        def _(pool):
            falls = pool.value_load(unsorted[0:1, 0:1], min_val=0, max_val=E)
            with pool.If(falls != 0):
                ch = Chain(pool, stage_steps, passed["pool"])
                pool.wait_ge(dst_ranked, 1)

                def scatter_pairs(i):
                    for h in range(2):
                        c = i * 16 + h * 8
                        if not isinstance(i, int):
                            at(pool, pair_out[h], i * 128, passed["pool"])
                        pool.tensor_copy(pstage[:, h * 16:h * 16 + 16], pair[:, bass.ds(c * 2, 16)])
                        ch.step(pool.tensor_copy(stage[:, h * 8:h * 8 + 8], pos_dst[:, bass.ds(c, 8)]))
                        for j in range(8):
                            pool.indirect_dma_start(pairs_d, bass.IndirectOffsetOnAxis(ap=stage[:, h * 8 + j:h * 8 + j + 1].bitcast(U32), axis=0),
                                                    pstage[:, h * 16 + 2 * j:h * 16 + 2 * j + 2], None).then_inc(pair_out[h], 16)

                scatter_pairs(0)
                with pool.Fori(1, EC // 16) as i:
                    ch.base -= 2
                    ch.enter(i, 2)
                    scatter_pairs(i)
                    ch.base += 2
                    ch.leave(EC // 16 - 1)
                for h in range(2):
                    pool.wait_ge(pair_out[h], 128 * (EC // 16))

    end_section()

    def fill_iota(pool, ids):
        return pool.iota(ids[:], pattern=[[1, (NT + 1) * P]], base=0, channel_multiplier=0, allow_small_or_imprecise_dtypes=True)

    with s12, ExitStack() as ctx:
        U = 8
        ids = sbuf(ctx, "ids", [128, (NT + 1) * P], I16)
        acc = sbuf(ctx, "acc", [128, (NT + 1) * P])
        win = sbuf(ctx, "win", [128, U * 4 * (ED + 1)])
        hot = sbuf(ctx, "hot", [128, 4 * 4 * P])
        w_sum = sbuf(ctx, "w_sum", [128, D])
        acc_s = sbuf(ctx, "acc_s", [128, 2 * P])
        z_stage = sbuf(ctx, "z_stage", [P, 4], I32)
        z_rows = sbuf(ctx, "z_rows", [P, 2 * 2 * D])
        pw = psum(ctx, "pw", 4)
        py = psum(ctx, "py", 2)
        win_in = [sem(f"win_in{s}") for s in range(U)]
        z_rows_in = [sem("z_rows_in0"), sem("z_rows_in1")]
        z_added = sem("z_added")
        accs_ready = sem("accs_ready")
        wsum_in, init2, hot_ready, win_summed, acc_done, y_ready, y_added = (
            sem(s) for s in ("wsum_in", "init2", "hot_ready", "win_summed", "acc_done", "y_ready", "y_added"))
        block = ctx.enter_context(nc.Block())

        @block.sync
        def _(sp):
            sp.dma_start(w_sum[:], a["L0_gnn_W_sum"]).then_inc(wsum_in, 16)

            def load(i):
                start = load_values(sp, win1_s, i * U, U, E)
                for s in range(U):
                    if not isinstance(i, int):
                        at(sp, win_summed, i * U + s + 1 - U, passed["sp"])
                    sp.dma_start(win[:, s * 4 * (ED + 1):(s + 1) * 4 * (ED + 1)],
                                 rows_d[bass.ds(start[s], W1), :].rearrange("(p r) c -> p (r c)", p=128)).then_inc(win_in[s], 16)

            load(0)
            with sp.Fori(1, NW1 // U) as i:
                load(i)

        @block.gpsimd
        def _(pool):
            fill_iota(pool, ids).then_inc(init2, 1)
            pool.memset(acc[:], 0.0).then_inc(init2, 1)
            ch = chain("pool", pool)

            def gather_z(t, u):
                ch.step(pool.tensor_copy(z_stage[:, 2 * u:2 * u + 2], z_idx[:, bass.ds(t * 2, 2)]))
                for k, name in enumerate(("L0_gnn_z_in", "L0_gnn_z_out")):
                    pool.indirect_dma_start(z_rows[:, (2 * u + k) * D:(2 * u + k + 1) * D], None, a[name],
                                            bass.IndirectOffsetOnAxis(ap=z_stage[:, 2 * u + k:2 * u + k + 1].bitcast(U32), axis=0)
                                            ).then_inc(z_rows_in[u], 16)

            def add_z(t, u, i):
                at(pool, z_rows_in[u], i * 32 + 32, passed["pool"])
                for k in range(2):
                    ch.step(pool.tensor_tensor(Rt(t), Rt(t), z_rows[:, (2 * u + k) * D:(2 * u + k + 1) * D], ALU.add))

            gather_z(0, 0)
            with pool.Fori(0, NT // 2 - 1) as i:
                ch.enter(i, 6)
                gather_z(2 * i + 1, 1)
                add_z(2 * i, 0, i)
                gather_z(2 * i + 2, 0)
                add_z(2 * i + 1, 1, i)
                ch.leave(NT // 2 - 1)
            gather_z(NT - 1, 1)
            add_z(NT - 2, 0, NT // 2 - 1)
            add_z(NT - 1, 1, NT // 2 - 1)
            pool.sem_inc(z_added)

        @block.vector
        def _(dve):
            ch = chain("dve", dve)
            dve.wait_ge(init2, 2)

            def add(g, bank, b):
                at(dve, win_summed, g + 1, passed["dve"])
                if not isinstance(g, int) or g:
                    at(dve, acc_done, g, passed["dve"])
                tile = acc[:, bass.ds(b * P, P)]
                dve.tensor_tensor(tile, tile, pw[:, bank, 0:P], ALU.add).then_inc(acc_done, 1)

            def windows(i):
                early = 0 if isinstance(i, int) else 2
                b = load_values(dve, win1_b, i * U - early, U + early, NT)
                for s in range(U):
                    at(dve, win_in[s], i * 16 + 16, passed["dve"])
                    keys = win[:, s * 4 * (ED + 1):(s + 1) * 4 * (ED + 1)].rearrange("p (r c) -> p r c", r=4)[:, :, ED]
                    dve.tensor_tensor(hot[:, (s % 4) * 4 * P:(s % 4 + 1) * 4 * P].rearrange("p (r n) -> p r n", r=4),
                                      ids[:, bass.ds(b[s + early] * P, P)].unsqueeze(1).to_broadcast([128, 4, P]),
                                      keys.unsqueeze(2).to_broadcast([128, 4, P]), ALU.is_equal).then_inc(hot_ready, 1)
                    if early or s >= 2:
                        add(i * U + s - 2, (s - 2) % 4, b[s - 2 + early])

            windows(0)
            with dve.Fori(1, NW1 // U) as i:
                windows(i)
            b = load_values(dve, win1_b, NW1 - 2, 2, NT)
            for k in range(2):
                add(NW1 - 2 + k, (U - 2 + k) % 4, b[k])

            dve.wait_ge(z_added, 1)

            def add_sum(t, u, i):
                at(dve, y_ready, t + 1, passed["dve"])
                dve.tensor_tensor(Rt(t), Rt(t), py[0:P, u, 0:D], ALU.add).then_inc(y_added, 1)

            tiles(dve, add_sum)

        @block.scalar
        def _(act):
            act.wait_ge(acc_done, NW1)

            def stage_acc(t, u, i):
                if later(t):
                    at(act, y_ready, t - 1, passed["act"])
                act.copy(acc_s[:, u * P:(u + 1) * P], acc[:, bass.ds(t * P, P)]).then_inc(accs_ready, 1)

            tiles(act, stage_acc)

        @block.tensor
        def _(pe):
            def windows(i):
                for s in range(U):
                    g = i * U + s
                    at(pe, hot_ready, g + 1, passed["pe"])
                    at(pe, win_in[s], i * 16 + 16, passed["pe"])
                    if not isinstance(i, int) or s >= 4:
                        at(pe, acc_done, g - 3, passed["pe"])
                    for r in range(4):
                        mm = pe.matmul(pw[:, s % 4, 0:P], win[:, (s * 4 + r) * (ED + 1):(s * 4 + r) * (ED + 1) + ED],
                                       hot[:, ((s % 4) * 4 + r) * P:((s % 4) * 4 + r + 1) * P], start=(r == 0), stop=(r == 3))
                    mm.then_inc(win_summed, 1)

            windows(0)
            with pe.Fori(1, NW1 // U) as i:
                windows(i)
            pe.wait_ge(wsum_in, 16)

            def project(t, u, i):
                at(pe, accs_ready, t + 1, passed["pe"])
                if later(t):
                    at(pe, y_added, t - 1, passed["pe"])
                pe.matmul(py[0:P, u, 0:D], acc_s[:, u * P:(u + 1) * P], w_sum[:], start=True, stop=True).then_inc(y_ready, 1)

            tiles(pe, project)

    G, GC = NT // 2, 2 * P

    def groups(eng, body, ch=None, per=0):
        for g in range(3):
            body(g, g % 2)
        with eng.Fori(1, G // 2) as i:
            if ch:
                ch.base -= per
                ch.enter(i, per)
            body(2 * i + 1, 1)
            body(2 * i + 2, 0)
        if ch:
            ch.base += per
            ch.leave(G // 2 - 1)

    def XTg(g, k):
        return XT[:, bass.ds(g * 2 * TS, 2 * TS)].rearrange("p (t c) -> p t c", t=2)[:, :, k * P:(k + 1) * P]

    class Ffn:

        def __init__(self, ctx, name, nm):
            self.nm, self.uses = nm, {"pe": 0, "act": 0, "dve": 0}
            self.hT = sbuf(ctx, name + "_hT", [128, 2 * nm * GC])
            self.ph = psum(ctx, name + "_ph", 4)
            self.py = psum(ctx, name + "_py", 2)
            self.h_ready, self.h_stored, self.y_ready, self.y_added = (sem(name + s) for s in ("_h_ready", "_h_stored", "_y_ready", "_y_added"))

        def hidden(self, u, m):
            return self.hT[:, (u * self.nm + m) * GC:(u * self.nm + m + 1) * GC]

        def pe(self, pe, w1, w2):
            r, nm = self.uses["pe"], self.nm
            self.uses["pe"] += 1

            def second(g, u):
                at(pe, self.h_stored, (g + 1 + r * G) * nm, passed["pe"])
                for v in range(2):
                    if not isinstance(g, int) or g or r:
                        at(pe, self.y_added, 2 * (g + r * G) + v - 1, passed["pe"])
                    for m in range(nm):
                        mm = pe.matmul(self.py[0:P, v, 0:D], self.hidden(u, m)[:, v * P:(v + 1) * P], w2(m), start=(m == 0), stop=(m == nm - 1))
                    mm.then_inc(self.y_ready, 1)

            def body(g, u):
                for m in range(nm):
                    bank = m % 4 if nm >= 4 else 2 * u + m
                    if not isinstance(g, int) or r or g * nm + m >= 4:
                        at(pe, self.h_stored, (g + r * G) * nm + m - 3, passed["pe"])
                    for k in range(2):
                        mm = pe.matmul(self.ph[:, bank, 0:GC].rearrange("p (t c) -> p t c", t=2), w1(k, m), XTg(g, k), start=(k == 0), stop=(k == 1))
                    mm.then_inc(self.h_ready, 1)
                if not isinstance(g, int) or g:
                    second(g - 1, 1 - u)

            groups(pe, body)
            second(G - 1, 0)

        def act(self, act, func, bias):
            r, nm = self.uses["act"], self.nm
            self.uses["act"] += 1

            def body(g, u):
                if not isinstance(g, int) or g >= 2 or r:
                    at(act, self.y_ready, 2 * (g - 1 + r * G), passed["act"])
                for m in range(nm):
                    bank = m % 4 if nm >= 4 else 2 * u + m
                    at(act, self.h_ready, (g + r * G) * nm + m + 1, passed["act"])
                    act.activation(self.hidden(u, m), self.ph[:, bank, 0:GC], func, bias=bias(m)).then_inc(self.h_stored, 1)

            groups(act, body)

        def dve(self, dve, ch, per, body):
            r = self.uses["dve"]
            self.uses["dve"] += 1

            def both(g, u):
                for v in range(2):
                    at(dve, self.y_ready, 2 * (g + r * G) + v + 1, passed["dve"])
                    body(2 * g + v, self.py[0:P, v, 0:D])
                    dve.sem_inc(self.y_added)

            groups(dve, both, ch, per * 4)

    def load_cols(sp, dst, vec, n):
        with nc.allow_non_contiguous_dma(reason="a bias per partition"):
            return sp.dma_start(dst, vec.rearrange("(m p) -> p m", p=128))

    def load_rows(sp, dst, w):
        return sp.dma_start(dst.rearrange("p (k n) -> p k n", n=w.shape[1]), w.rearrange("(k p) n -> p k n", p=128))

    with ExitStack() as ctx:
        w1 = sbuf(ctx, "f_w1", [128, 2 * FFN_H])
        w2 = sbuf(ctx, "f_w2", [128, 8 * D])
        b1 = sbuf(ctx, "f_b1", [128, 8])
        b2 = sbuf(ctx, "f_b2", [P, D])
        wr = sbuf(ctx, "f_wr", [P, D])
        br = sbuf(ctx, "f_br", [P, 1])
        xn = sbuf(ctx, "f_xn", [P, 4 * D])
        prod = sbuf(ctx, "f_prod", [P, 2 * D])
        wt = sbuf(ctx, "f_wt", [P, NT])
        key_i = sbuf(ctx, "key_i", [P, 3 * NT], I32)
        key = sbuf(ctx, "key", [P, 3 * NT])
        hit = sbuf(ctx, "hit", [P, 3 * NT])
        sel = sbuf(ctx, "sel", [P, NT])
        cur = sbuf(ctx, "cur", [P, 8])
        pow2 = sbuf(ctx, "pow2", [P, 16])
        ptr = psum(ctx, "f_ptr", 2)
        ffn = Ffn(ctx, "f", FFN_H // 128)
        w_in = sem("f_w_in")
        f_in, pows, xn_ready, xt_ready, xt_stored, sum_asked, sum_given = (
            sem(s) for s in ("f_in", "pows", "f_xn_ready", "f_xt_ready", "f_xt_stored", "sum_asked", "sum_given"))
        block = ctx.enter_context(nc.Block())

        @block.sync
        def _(sp):
            sp.dma_start(wr[:], bcast_rows(a["L0_ffn_wr"].rearrange("d a -> (d a)"), P)).then_inc(f_in, 16)
            sp.dma_start(br[:], bcast_rows(a["L0_ffn_br"], P)).then_inc(f_in, 16)
            load_rows(sp, w1[:], a["L0_ffn_w1"]).then_inc(w_in, 16)
            load_rows(sp, w2[:], a["L0_ffn_w2"]).then_inc(w_in, 16)
            load_cols(sp, b1[:], a["L0_ffn_b1"], 8).then_inc(w_in, 16)
            sp.dma_start(b2[:], bcast_rows(a["L0_ffn_b2"], P)).then_inc(w_in, 16)

        @block.gpsimd
        def _(pool):
            for j in range(16):
                pool.memset(pow2[:, j:j + 1], float(2 ** (15 - j))).then_inc(pows, 1)
            pool.iota(key_i[:, 2 * NT:3 * NT], pattern=[[-P, NT]], base=8191, channel_multiplier=-1).then_inc(pows, 1)

        @block.vector
        def _(dve):
            ch = chain("dve", dve)
            layer_stats(dve, ch, Rt)
            dve.wait_ge(f_in, 32)

            def norm(g, u):
                x2 = xn[:, u * 2 * D:(u + 1) * 2 * D]
                if not isinstance(g, int) or g >= 2:
                    at(dve, xt_ready, 2 * g - 2, passed["dve"])
                for v in range(2):
                    t = 2 * g + v
                    dve.tensor_scalar(x2[:, v * D:(v + 1) * D], Rt(t), mean[:, bass.ds(t, 1)], rstd[:, bass.ds(t, 1)],
                                      ALU.subtract, ALU.mult).then_inc(xn_ready, 1)
                at(dve, xn_ready, 2 * g + 2, passed["dve"])
                r2 = R[:, bass.ds(g * 2 * TS, 2 * TS)]
                dve.tensor_tensor(prod[:].rearrange("p (v d) -> p v d", v=2), x2.rearrange("p (v d) -> p v d", v=2),
                                  wr[:].unsqueeze(1).to_broadcast([P, 2, D]), ALU.mult)
                ch.step(dve.tensor_tensor(r2, r2, x2, ALU.add))
                ch.step(dve.tensor_reduce(wt[:, bass.ds(g * 2, 2)], prod[:].rearrange("p (v d) -> p v d", v=2), AX.X, ALU.add))

            groups(dve, norm, ch, 4)
            ch.step(dve.tensor_scalar(wt[:], wt[:], br[:, 0:1], 0.0, ALU.add, ALU.add))
            ki = [key_i[:, k * NT:(k + 1) * NT] for k in range(3)]
            dve.wait_ge(pows, 17)
            ch.step(dve.tensor_scalar(ki[0], wt[:].bitcast(I32), 31, -2147483648, ALU.arith_shift_right, ALU.bitwise_or))
            ch.step(dve.tensor_tensor(ki[1], ki[0], wt[:].bitcast(I32), ALU.bitwise_xor))
            ch.step(dve.tensor_scalar(ki[0], ki[1], 16, None, ALU.logical_shift_right))
            ch.step(dve.tensor_scalar(ki[1], ki[1], 65535, None, ALU.bitwise_and))
            ch.step(dve.tensor_copy(key[:], key_i[:]))
            need, low, cand, part, gain = (cur[:, j:j + 1] for j in range(5))
            ch.step(dve.memset(need, float(TOPK)))
            ch.step(dve.memset(sel[:], 1.0))
            asked = [0]

            def count(v, threshold, op):
                ch.step(dve.tensor_scalar(hit[:, 0:NT], v, threshold, 0.0, op, ALU.add, accum_out=part))
                dve.sem_inc(sum_asked)

            for level in range(3):
                v, bits = key[:, level * NT:(level + 1) * NT], (16, 16, 13)[level]
                if level:
                    ch.step(dve.tensor_scalar(v, v, 1.0, None, ALU.add))
                    ch.step(dve.tensor_tensor(v, v, sel[:], ALU.mult))
                    ch.step(dve.tensor_scalar(v, v, -1.0, None, ALU.add))
                ch.step(dve.memset(low, 0.0))
                with dve.Fori(0, bits) as j:
                    ch.enter(j, 4)
                    step = pow2[:, bass.ds(j + (16 - bits), 1)]
                    ch.step(dve.tensor_tensor(cand, low, step, ALU.add))
                    count(v, cand, ALU.is_ge)
                    at(dve, sum_given, j + (asked[0] + 1), passed["dve"])
                    ch.step(dve.tensor_scalar(gain, ptr[0:P, 0, 0:1], need, step, ALU.is_ge, ALU.mult))
                    ch.step(dve.tensor_tensor(low, low, gain, ALU.add))
                    ch.leave(bits)
                asked[0] += bits
                if level < 2:
                    count(v, low, ALU.is_gt)
                    asked[0] += 1
                    dve.wait_ge(sum_given, asked[0])
                    ch.step(dve.tensor_copy(gain, ptr[0:P, 0, 0:1]))
                    ch.step(dve.tensor_tensor(need, need, gain, ALU.subtract))
                    ch.step(dve.tensor_scalar(hit[:, (level + 1) * NT:(level + 2) * NT], v, low, None, ALU.is_gt))
                    ch.step(dve.tensor_scalar(sel[:], v, low, None, ALU.is_equal))
                else:
                    ch.step(dve.tensor_scalar(sel[:], v, low, None, ALU.is_ge))
            for k in (1, 2):
                ch.step(dve.tensor_tensor(sel[:], sel[:], hit[:, k * NT:(k + 1) * NT], ALU.max))
            ch.step(dve.tensor_tensor(wt[:], wt[:], sel[:], ALU.mult))

            def add_y(t, y):
                tmp = prod[:, 0:D]
                ch.step(dve.tensor_tensor(tmp, y, b2[:], ALU.add))
                ch.step(dve.scalar_tensor_tensor(out=Rt(t), in0=tmp, scalar=wt[:, bass.ds(t, 1)], in1=Rt(t), op0=ALU.mult, op1=ALU.add))

            dve.wait_ge(w_in, 64)
            ffn.dve(dve, ch, 2, add_y)

        @block.scalar
        def _(act):
            finish_stats_act(act)

            def store_xt(t, u, i):
                at(act, xt_ready, t + 1, passed["act"])
                act.copy(XT[:, bass.ds(t * TS, 2 * P)], ptr[:, u, 0:2 * P]).then_inc(xt_stored, 1)

            tiles(act, store_xt)
            act.wait_ge(w_in, 64)
            ffn.act(act, ACT.Gelu_apprx_tanh, lambda m: b1[:, m:m + 1])

        @block.tensor
        def _(pe):
            def transpose_x(g, u):
                for v in range(2):
                    t = 2 * g + v
                    at(pe, xn_ready, t + 1, passed["pe"])
                    if not isinstance(g, int) or g:
                        at(pe, xt_stored, t - 1, passed["pe"])
                    for k in range(2):
                        o = (2 * u + v) * D + k * 128
                        mm = pe.transpose(ptr[:, v, k * P:(k + 1) * P], xn[:, o:o + 128], ident[0:P, 0:P])
                    mm.then_inc(xt_ready, 1)

            groups(pe, transpose_x)
            pe.wait_ge(xt_stored, NT)
            n = 16 + 1 + 16 + 1 + 13
            pe.wait_ge(sum_asked, 1)
            pe.matmul(ptr[0:P, 0, 0:1], ones[0:P, 0:P], cur[:, 3:4], start=True, stop=True).then_inc(sum_given, 1)
            with pe.Fori(1, n) as j:
                at(pe, sum_asked, j + 1, passed["pe"])
                pe.matmul(ptr[0:P, 0, 0:1], ones[0:P, 0:P], cur[:, 3:4], start=True, stop=True).then_inc(sum_given, 1)
            pe.wait_ge(w_in, 64)
            ffn.pe(pe, lambda k, m: w1[:, k * FFN_H + m * 128:k * FFN_H + (m + 1) * 128], lambda m: w2[:, m * D:(m + 1) * D])

    with ExitStack() as ctx:
        xn = sbuf(ctx, "g_xn", [P, 2 * D])
        ptr = psum(ctx, "g_ptr", 2)
        xn_ready, xt_ready, xt_stored = sem("g_xn_ready"), sem("g_xt_ready"), sem("g_xt_stored")
        row_out = [sem("row_out0"), sem("row_out1")]
        block = ctx.enter_context(nc.Block())

        @block.sync
        def _(sp):
            def store(t, u, i):
                at(sp, xn_ready, t + 1, passed["sp"])
                sp.dma_start(xn2_d[bass.ds(t * P, P), :], xn[:, u * D:(u + 1) * D]).then_inc(row_out[u], 16)

            tiles(sp, store)
            for u in range(2):
                sp.wait_ge(row_out[u], 16 * (NT // 2))

        @block.vector
        def _(dve):
            ch = chain("dve", dve)
            layer_stats(dve, ch, Rt)

            def norm(t, u, i):
                if later(t):
                    at(dve, xt_ready, t - 1, passed["dve"])
                    at(dve, row_out[u], i * 16, passed["dve"])
                dve.tensor_scalar(xn[:, u * D:(u + 1) * D], Rt(t), mean[:, bass.ds(t, 1)], rstd[:, bass.ds(t, 1)],
                                  ALU.subtract, ALU.mult).then_inc(xn_ready, 1)

            tiles(dve, norm)

        @block.scalar
        def _(act):
            finish_stats_act(act)

            def store_xt(t, u, i):
                at(act, xt_ready, t + 1, passed["act"])
                act.copy(XT[:, bass.ds(t * TS, 2 * P)], ptr[:, u, 0:2 * P]).then_inc(xt_stored, 1)

            tiles(act, store_xt)

        @block.tensor
        def _(pe):
            def transpose_x(t, u, i):
                at(pe, xn_ready, t + 1, passed["pe"])
                if later(t):
                    at(pe, xt_stored, t - 1, passed["pe"])
                for k in range(2):
                    mm = pe.transpose(ptr[:, u, k * P:(k + 1) * P], xn[:, u * D + k * 128:u * D + (k + 1) * 128], ident[0:P, 0:P])
                mm.then_inc(xt_ready, 1)

            tiles(pe, transpose_x)

    s56 = ExitStack()
    agg = sbuf(s56, "agg", [128, (NT + 1) * TS])
    mix = ExitStack()
    kvn = sbuf(mix, "m_kvn", [128, 2 * 128])
    with ExitStack() as ctx:
        wkv = sbuf(ctx, "m_wkv", [128, 2 * 2 * D])
        bkv = sbuf(ctx, "m_bkv", [P, 2 * D])
        lng = sbuf(ctx, "m_lng", [P, 2 * HD])
        lnb = sbuf(ctx, "m_lnb", [P, 2 * HD])
        xs = sbuf(ctx, "m_xs", [128, TS])
        kv = sbuf(ctx, "m_kv", [P, 2 * D])
        kn = sbuf(ctx, "m_kn", [P, 2 * D])
        sq = kn
        hm = sbuf(ctx, "m_hm", [P, 16])
        hv = sbuf(ctx, "m_hv", [P, 16])
        pk = psum(ctx, "m_pk", 1)
        pc = psum(ctx, "m_pc", 1)
        m_in, xs_ready, kv_ready, kv_c, sq_ready, var_r, sd_r, kn_ready, ctx_done, kv_read = (
            sem("m_" + s) for s in ("in", "xs_ready", "kv_ready", "kv_c", "sq_ready", "var_r", "sd_r", "kn_ready", "ctx_done", "kv_read"))
        M_IN = 16 * (2 + HEADS + 4)
        U, RU, PU = 16, 8, 8
        ids = sbuf(ctx, "ids2", [128, (NT + 1) * P], I16)
        pw_in = sbuf(ctx, "pw_in", [128, U * 4], I32)
        rows = sbuf(ctx, "rows", [128, RU * 2 * D])
        hot = sbuf(ctx, "hot2", [128, 4 * 2 * P])
        pg = psum(ctx, "pg", 4)
        pairs_in = [sem(f"pairs_in{h}") for h in range(U // PU)]
        rows_in = [sem(f"rows_in{s}") for s in range(RU)]
        init, hot_ready, win_summed, acc_done = (sem(s) for s in ("g_init", "g_hot_ready", "g_win_summed", "g_acc_done"))
        block = ctx.enter_context(nc.Block())

        @block.sync
        def _(sp):
            heads = a["L1_mix_w_qkv"].rearrange("(k p) (h c) -> p k h c", p=128, h=HEADS)
            for k in range(2):
                sp.dma_start(wkv[:, k * 2 * D:(k + 1) * 2 * D].rearrange("p (h c) -> p h c", h=HEADS), heads[:, k, :, HD:3 * HD]).then_inc(m_in, 16)
            for h in range(HEADS):
                sp.dma_start(bkv[:, h * 2 * HD:(h + 1) * 2 * HD], bcast_rows(a["L1_mix_b_qkv"][(3 * h + 1) * HD:(3 * h + 3) * HD], P)).then_inc(m_in, 16)
            for dst, names in ((lng, ("kln_g", "vln_g")), (lnb, ("kln_b", "vln_b"))):
                for j, name in enumerate(names):
                    sp.dma_start(dst[:, j * HD:(j + 1) * HD], bcast_rows(a["L1_mix_" + name], P)).then_inc(m_in, 16)

            def load(i):
                start = load_values(sp, win2_s, i * U, U, E)
                for s in range(U):
                    if not isinstance(i, int) and s % PU == 0:
                        at(sp, win_summed, i * U + s + PU - U, passed["sp"])
                    sp.dma_start(pw_in[:, s * 4:(s + 1) * 4],
                                 pairs_d[bass.ds(start[s], W2), :].rearrange("(p r) c -> p (r c)", p=128)).then_inc(pairs_in[s // PU], 16)

            load(0)
            with sp.Fori(1, NW2 // U) as i:
                load(i)

        @block.gpsimd
        def _(pool):
            fill_iota(pool, ids).then_inc(init, 1)
            pool.memset(agg[:], 0.0).then_inc(init, 1)

            def gather(i):
                for s in range(U):
                    if s % PU == 0:
                        at(pool, pairs_in[s // PU], (i + 1) * 16 * PU, passed["pool"])
                    if s % 4 == 0 and (s >= RU or not isinstance(i, int)):
                        at(pool, win_summed, i * U + s + 4 - RU, passed["pool"])
                    for r in range(2):
                        pool.indirect_dma_start(rows[:, (2 * (s % RU) + r) * D:(2 * (s % RU) + r + 1) * D], None, xn2_d,
                                                bass.IndirectOffsetOnAxis(ap=pw_in[:, s * 4 + 2 * r:s * 4 + 2 * r + 1].bitcast(U32), axis=0)
                                                ).then_inc(rows_in[s % RU], 16)

            gather(0)
            with pool.Fori(1, NW2 // U) as i:
                gather(i)

        @block.vector
        def _(dve):
            dve.wait_ge(init, 2)

            def add(g, bank, b):
                at(dve, win_summed, g + 1, passed["dve"])
                if not isinstance(g, int) or g:
                    at(dve, acc_done, g, passed["dve"])
                tile = agg[0:P, bass.ds(b * TS, D)]
                dve.tensor_tensor(tile, tile, pg[0:P, bank, 0:D], ALU.add).then_inc(acc_done, 1)

            ch = chain("dve", dve)
            by_head = lambda x: x.rearrange("p (h c) -> p h c", h=HEADS)
            by_group = kv[:].rearrange("p (g d) -> p g d", g=16)

            def norm_kv(t, s):
                if s == 6:
                    at(dve, kv_ready, t + 1, passed["dve"])
                    dve.tensor_tensor(kv[:], pk[0:P, 0, :], bkv[:], ALU.add).then_inc(kv_read, 1)
                if s == 7:
                    at(dve, kv_read, t + 1, passed["dve"])
                    ch.step(dve.tensor_reduce(hm[:], by_group, AX.X, ALU.add))
                    ch.step(dve.tensor_scalar(hm[:], hm[:], 1.0 / HD, None, ALU.mult))
                if s == 8:
                    if not isinstance(t, int):
                        at(dve, ctx_done, t, passed["dve"])
                    dve.tensor_tensor(by_group, by_group, hm[:].unsqueeze(2).to_broadcast([P, 16, HD]), ALU.subtract).then_inc(kv_c, 1)
                if s == 10:
                    at(dve, sq_ready, t + 1, passed["dve"])
                    ch.step(dve.tensor_reduce(hv[:], sq[:].rearrange("p (g d) -> p g d", g=16), AX.X, ALU.add))
                    dve.tensor_scalar(hv[:], hv[:], 1.0 / HD, EPS, ALU.mult, ALU.add).then_inc(var_r, 1)
                if s == 11:
                    at(dve, sd_r, t + 1, passed["dve"])
                    ch.step(dve.reciprocal(hv[:], hv[:]))
                    ch.step(dve.tensor_tensor(by_group, by_group, hv[:].unsqueeze(2).to_broadcast([P, 16, HD]), ALU.mult))
                if s == 12:
                    ch.step(dve.tensor_tensor(by_head(kv[:]), by_head(kv[:]), lng[:].unsqueeze(1).to_broadcast([P, HEADS, 2 * HD]), ALU.mult))
                if s == 13:
                    for j in range(2):
                        dve.tensor_tensor(by_head(kn[:, j * D:(j + 1) * D]), by_head(kv[:])[:, :, j * HD:(j + 1) * HD],
                                          lnb[:, j * HD:(j + 1) * HD].unsqueeze(1).to_broadcast([P, HEADS, HD]), ALU.add).then_inc(kn_ready, 1)

            def windows(i, tile=True):
                early = 0 if isinstance(i, int) else 2
                b = load_values(dve, win2_b, i * U - early, U + early, NT)
                for s in range(U):
                    if s % PU == 0:
                        at(dve, pairs_in[s // PU], (i + 1) * 16 * PU, passed["dve"])
                    keys = pw_in[:, s * 4:(s + 1) * 4].rearrange("p (r c) -> p r c", c=2)[:, :, 1]
                    dve.tensor_tensor(hot[:, (s % 4) * 2 * P:(s % 4 + 1) * 2 * P].rearrange("p (r n) -> p r n", r=2),
                                      ids[:, bass.ds(b[s + early] * P, P)].unsqueeze(1).to_broadcast([128, 2, P]),
                                      keys.unsqueeze(2).to_broadcast([128, 2, P]), ALU.is_equal).then_inc(hot_ready, 1)
                    if early or s >= 2:
                        add(i * U + s - 2, (s - 2) % 4, b[s - 2 + early])
                    if tile:
                        norm_kv(i, s)

            PER = 6
            dve.wait_ge(m_in, M_IN)
            windows(0)
            with dve.Fori(1, NT) as i:
                ch.base -= PER
                ch.enter(i, PER)
                windows(i)
            ch.base += PER
            ch.leave(NT - 1)
            with dve.Fori(NT, NW2 // U) as i:
                windows(i, tile=False)
            b = load_values(dve, win2_b, NW2 - 2, 2, NT)
            for k in range(2):
                add(NW2 - 2 + k, (U - 2 + k) % 4, b[k])
            dve.wait_ge(ctx_done, NT)
            for m in range(2):
                ch.step(dve.tensor_scalar(kvn[:, m * 128:(m + 1) * 128], pc[:, 0, m * 128:(m + 1) * 128], 1.0 / N, None, ALU.mult))
                ch.step(dve.tensor_tensor(kvn[:, m * 128:(m + 1) * 128], kvn[:, m * 128:(m + 1) * 128], blockdiag[:], ALU.mult))

        @block.scalar
        def _(act):
            def parts(t):
                if not isinstance(t, int):
                    at(act, kv_ready, t, passed["act"])
                act.copy(xs[:, 0:2 * P], XT[:, bass.ds(t * TS, 2 * P)]).then_inc(xs_ready, 1)
                at(act, kv_c, t + 1, passed["act"])
                act.activation(sq[:], kv[:], ACT.Square).then_inc(sq_ready, 1)
                at(act, var_r, t + 1, passed["act"])
                act.activation(hv[:], hv[:], ACT.Sqrt).then_inc(sd_r, 1)

            parts(0)
            with act.Fori(1, NT) as i:
                parts(i)

        @block.tensor
        def _(pe):
            def project(t):
                at(pe, xs_ready, t + 1, passed["pe"])
                if not isinstance(t, int):
                    at(pe, kv_read, t, passed["pe"])
                for k in range(2):
                    mm = pe.matmul(pk[0:P, 0, :], xs[:, k * P:(k + 1) * P], wkv[:, k * 2 * D:(k + 1) * 2 * D], start=(k == 0), stop=(k == 1))
                mm.then_inc(kv_ready, 1)

            def context(t):
                at(pe, kn_ready, 2 * t + 2, passed["pe"])
                first = isinstance(t, int)
                for m in range(2):
                    mm = pe.matmul(pc[:, 0, m * 128:(m + 1) * 128], kn[:, m * 128:(m + 1) * 128],
                                   kn[:, D + m * 128:D + (m + 1) * 128], start=first and m == 0, stop=True, skip_group_check=True)
                mm.then_inc(ctx_done, 1)

            def windows(i, tile=True):
                for s in range(U):
                    g = i * U + s
                    if tile and s == 4:
                        project(i)
                    if tile and s == 15:
                        context(i)
                    at(pe, hot_ready, g + 1, passed["pe"])
                    at(pe, rows_in[s % RU], (i * (U // RU) + s // RU + 1) * 32, passed["pe"])
                    if not isinstance(i, int) or s >= 4:
                        at(pe, acc_done, g - 3, passed["pe"])
                    for r in range(2):
                        mm = pe.matmul(pg[0:P, s % 4, 0:D], hot[:, ((s % 4) * 2 + r) * P:((s % 4) * 2 + r + 1) * P],
                                       rows[:, (2 * (s % RU) + r) * D:(2 * (s % RU) + r + 1) * D], start=(r == 0), stop=(r == 1))
                    mm.then_inc(win_summed, 1)

            pe.wait_ge(m_in, M_IN)
            windows(0)
            with pe.Fori(1, NT) as i:
                windows(i)
            with pe.Fori(NT, NW2 // U) as i:
                windows(i, tile=False)

    with mix, ExitStack() as ctx:
        wq = sbuf(ctx, "m_wq", [128, 2 * 768])
        w1 = sbuf(ctx, "m_w1", [128, 2 * D])
        w2 = sbuf(ctx, "m_w2", [128, 2 * D])
        wp = sbuf(ctx, "m_wp", [128, 2 * D])
        b1 = sbuf(ctx, "m_b1", [128, 2])
        bq = sbuf(ctx, "m_bq", [128, 2])
        b2 = sbuf(ctx, "m_b2", [P, D])
        wqT = sbuf(ctx, "m_wqT", [128, 2 * D])
        mT = sbuf(ctx, "m_mT", [128, 2 * D])
        tb = sbuf(ctx, "m_tb", [128, 2])
        bp = sbuf(ctx, "m_bp", [128, 2])
        tmp = sbuf(ctx, "m_tmp", [P, D])
        xn = sbuf(ctx, "m_xn", [P, D])
        m_in, q_compact, fold_pe, fold_dve = sem("m_in2"), sem("q_compact"), sem("m_fold_pe"), sem("m_fold_dve")
        M_IN = 16 * (5 + 8)
        with ExitStack() as c1:
            pf = psum(c1, "m_pf", 4)
            block = c1.enter_context(nc.Block())

            @block.sync
            def _(sp):
                load_rows(sp, wq[:], a["L1_mix_w_qkv"]).then_inc(m_in, 16)
                load_rows(sp, w1[:], a["L1_mix_w1"]).then_inc(m_in, 16)
                load_rows(sp, w2[:], a["L1_mix_w2"]).then_inc(m_in, 16)
                load_cols(sp, b1[:], a["L1_mix_b1"], 2).then_inc(m_in, 16)
                sp.dma_start(b2[:], bcast_rows(a["L1_mix_b2"], P)).then_inc(m_in, 16)
                with nc.allow_non_contiguous_dma(reason="a bias per partition"):
                    for m in range(2):
                        for h in range(4):
                            o = 96 * (4 * m + h)
                            sp.dma_start(bq[32 * h:32 * h + 32, m:m + 1], a["L1_mix_b_qkv"][o:o + 32].rearrange("(p a) -> p a", a=1)).then_inc(m_in, 16)

            @block.vector
            def _(dve):
                ch = chain("dve", dve)
                dve.wait_ge(m_in, M_IN)
                dve.wait_ge(fold_pe, 1)
                for m in range(2):
                    ch.step(dve.tensor_copy(wqT[:, m * D:(m + 1) * D], pf[:, m, 0:D]))
                dve.sem_inc(fold_dve)
                dve.wait_ge(fold_pe, 2)
                for m in range(2):
                    ch.step(dve.tensor_copy(mT[:, m * D:(m + 1) * D], pf[:, 2 + m, 0:D]))
                    d = mT[:, m * D + m * 128:m * D + (m + 1) * 128]
                    ch.step(dve.tensor_tensor(d, d, ident[:], ALU.add))
                    ch.step(dve.tensor_copy(tb[:, m:m + 1], pf[:, 0, m:m + 1]))
                dve.sem_inc(fold_dve)
                dve.wait_ge(fold_pe, 3)
                for m in range(2):
                    ch.step(dve.tensor_copy(wp[:, m * D:(m + 1) * D], pf[:, 2 + m, 0:D]))
                ch.step(dve.tensor_tensor(bp[:], b1[:], pf[:, 1, 0:2], ALU.add))

            @block.scalar
            def _(act):
                act.wait_ge(m_in, M_IN)
                for k in range(2):
                    act.copy(wp[:, k * D:(k + 1) * D].rearrange("p (h c) -> p h c", h=HEADS),
                             wq[:, k * 768:(k + 1) * 768].rearrange("p (h c) -> p h c", h=HEADS)[:, :, 0:32]).then_inc(q_compact, 1)

            @block.tensor
            def _(pe):
                pe.wait_ge(m_in, M_IN)
                pe.wait_ge(q_compact, 2)
                for m in range(2):
                    for k in range(2):
                        mm = pe.matmul(pf[:, m, k * 128:(k + 1) * 128], wp[:, k * D + m * 128:k * D + (m + 1) * 128], ident[:], start=True, stop=True)
                mm.then_inc(fold_pe, 1)
                pe.wait_ge(fold_dve, 1)
                for m in range(2):
                    pe.matmul(pf[:, 2 + m, 0:D], kvn[:, m * 128:(m + 1) * 128], wqT[:, m * D:(m + 1) * D], start=True, stop=True)
                for m in range(2):
                    mm = pe.matmul(pf[:, 0, m:m + 1], kvn[:, m * 128:(m + 1) * 128], bq[:, m:m + 1], start=True, stop=True)
                mm.then_inc(fold_pe, 1)
                pe.wait_ge(fold_dve, 2)
                for k in range(2):
                    for m in range(2):
                        pe.matmul(pf[:, 2 + k, 0:D], mT[:, m * D + k * 128:m * D + (k + 1) * 128], w1[:, m * D:(m + 1) * D], start=(m == 0), stop=(m == 1))
                for c in range(2):
                    for m in range(2):
                        mm = pe.matmul(pf[:, 1, c:c + 1], w1[:, m * D + c * 128:m * D + (c + 1) * 128], tb[:, m:m + 1], start=(m == 0), stop=(m == 1))
                mm.then_inc(fold_pe, 1)

        with ExitStack() as c2:
            ffn = Ffn(c2, "m", 2)
            block = c2.enter_context(nc.Block())

            @block.vector
            def _(dve):
                ch = chain("dve", dve)

                def add_y(t, y):
                    ch.step(dve.tensor_tensor(tmp[:], y, b2[:], ALU.add))
                    ch.step(dve.tensor_scalar(xn[:], Rt(t), mean[:, bass.ds(t, 1)], rstd[:, bass.ds(t, 1)], ALU.subtract, ALU.mult))
                    ch.step(dve.tensor_tensor(tmp[:], tmp[:], xn[:], ALU.add))
                    ch.step(dve.tensor_tensor(Rt(t), Rt(t), tmp[:], ALU.add))

                ffn.dve(dve, ch, 4, add_y)

            @block.scalar
            def _(act):
                ffn.act(act, ACT.Gelu, lambda m: bp[:, m:m + 1])

            @block.tensor
            def _(pe):
                ffn.pe(pe, lambda k, m: wp[:, k * D + m * 128:k * D + (m + 1) * 128], lambda m: w2[:, m * D:(m + 1) * D])

    with s56, ExitStack() as ctx:
        wl = sbuf(ctx, "s_wl", [128, 2 * D])
        wr = sbuf(ctx, "s_wr", [128, 2 * D])
        wn = sbuf(ctx, "s_wn", [128, 4 * D])
        bl = sbuf(ctx, "s_bl", [P, D])
        gm = sbuf(ctx, "s_gm", [P, D])
        bt = sbuf(ctx, "s_bt", [P, D])
        mu = sbuf(ctx, "s_mu", [P, D])
        gv = sbuf(ctx, "s_gv", [P, D])
        xs = sbuf(ctx, "s_xs", [128, 2 * 2 * TS])
        sq = sbuf(ctx, "s_sq", [P, 2 * D])
        rdeg = sbuf(ctx, "s_rdeg", [P, NT])
        ss = sbuf(ctx, "s_ss", [P, NT])
        pa = psum(ctx, "s_pa", 2)
        ptr = psum(ctx, "s_ptr", 2)
        ag = sbuf(ctx, "s_ag", [P, 2 * D])
        pst = psum(ctx, "s_pst", 2)
        pt = psum(ctx, "s_pt", 2)
        s_in, wt_ready, w_stored, xs_ready, ab_ready, o_ready, ss_done, ss_ready, n_ready, sum_ready, c_ready, sq_ready2, var_ready2, sd_ready2, sq_used = (
            sem("s_" + s) for s in ("in", "wt_ready", "w_stored", "xs_ready", "ab_ready", "o_ready", "ss_done", "ss_ready", "n_ready", "sum_ready", "c_ready", "sq_ready2", "var_ready2", "sd_ready2", "sq_used"))
        block = ctx.enter_context(nc.Block())

        sum_steps, ag_ready, ag_transposed = sem("s_sum_steps"), sem("s_ag_ready"), sem("s_ag_transposed")

        def Ot(t):
            return agg[0:P, bass.ds(t * TS, D)]

        @block.sync
        def _(sp):
            load_rows(sp, wn[:, 0:2 * D], a["L1_gnn_W_l"]).then_inc(s_in, 16)
            load_rows(sp, wn[:, 2 * D:4 * D], a["L1_gnn_W_r"]).then_inc(s_in, 16)
            for dst, name in ((bl, "b_l"), (gm, "gamma"), (bt, "beta")):
                sp.dma_start(dst[:], bcast_rows(a["L1_gnn_" + name], P)).then_inc(s_in, 16)

        @block.vector
        def _(dve):
            ch = chain("dve", dve)
            dve.wait_ge(s_in, 80)
            ch.step(dve.tensor_scalar(rdeg[:], deg_in[:], 1.0, None, ALU.max))
            ch.step(dve.reciprocal(rdeg[:], rdeg[:]))

            def combine(t, u):
                at(dve, ab_ready, t + 1, passed["dve"])
                dve.tensor_tensor(Ot(t), pa[0:P, u, 0:D], bl[:], ALU.add).then_inc(o_ready, 1)

            def scale(t, u, i):
                if later(t):
                    at(dve, ag_transposed, t - 1, passed["dve"])
                dve.tensor_scalar(ag[:, u * D:(u + 1) * D], Ot(t), rdeg[:, bass.ds(t, 1)], None, ALU.mult).then_inc(ag_ready, 1)
                if not isinstance(t, int) or t:
                    at(dve, ag_ready, t, passed["dve"])
                    combine(t - 1, 1 - u)

            tiles(dve, scale)
            dve.wait_ge(ag_ready, NT)
            combine(NT - 1, 1)
            dve.wait_ge(o_ready, NT)
            dve.wait_ge(ss_ready, 1)
            ch.step(dve.tensor_scalar(ss[:], ss[:], 1e-12, None, ALU.max))
            ch.step(dve.reciprocal(ss[:], ss[:]))

            def unit(t, u, i):
                dve.tensor_scalar(Ot(t), Ot(t), ss[:, bass.ds(t, 1)], None, ALU.mult).then_inc(n_ready, 1)

            tiles(dve, unit)
            dve.wait_ge(sum_ready, 1)
            dve.wait_ge(n_ready, NT)
            ch.step(dve.tensor_scalar(mu[:], pst[0:P, 0, 0:D], 1.0 / N, None, ALU.mult))

            def center(t, u, i):
                dve.tensor_tensor(Ot(t), Ot(t), mu[:], ALU.subtract).then_inc(c_ready, 1)

            tiles(dve, center)
            dve.wait_ge(sum_ready, 2)
            dve.wait_ge(c_ready, NT)
            dve.tensor_scalar(gv[:], pst[0:P, 1, 0:D], 1.0 / N, EPS, ALU.mult, ALU.add).then_inc(var_ready2, 1)
            dve.wait_ge(sd_ready2, 1)
            ch.step(dve.reciprocal(gv[:], gv[:]))
            ch.step(dve.tensor_tensor(gv[:], gv[:], gm[:], ALU.mult))

            WIDE = 5
            by_tile = lambda x: x.rearrange("p (w d) -> p w d", w=WIDE)
            every_tile = lambda x: x[:].unsqueeze(1).to_broadcast([P, WIDE, D])
            with dve.Fori(0, NT // WIDE) as i:
                ch.enter(i, 3)
                o, r = (by_tile(x[0:P, bass.ds(i * WIDE * TS, WIDE * TS)]) for x in (agg, R))
                ch.step(dve.tensor_tensor(o, o, every_tile(gv), ALU.mult))
                ch.step(dve.tensor_tensor(o, o, every_tile(bt), ALU.add))
                ch.step(dve.scalar_tensor_tensor(out=r, in0=o, scalar=0.0, in1=r, op0=ALU.max, op1=ALU.add))
                ch.leave(NT // WIDE)

        @block.scalar
        def _(act):
            for j in range(2):
                for k in range(2):
                    act.wait_ge(wt_ready, 2 * j + k + 1)
                    act.copy((wl, wr)[j][:, k * D:(k + 1) * D], pt[:, k, 0:D]).then_inc(w_stored, 1)

            def square(t, u):
                at(act, o_ready, t + 1, passed["act"])
                if later(t):
                    at(act, ss_done, t - 1, passed["act"])
                act.activation(sq[:, u * D:(u + 1) * D], Ot(t), ACT.Square, accum_out=ss[:, bass.ds(t, 1)]).then_inc(ss_done, 1)

            def parts(t, u, i):
                if later(t):
                    at(act, ab_ready, t - 1, passed["act"])
                act.copy(xs[:, (2 * u + 1) * TS:(2 * u + 1) * TS + 2 * P], XT[:, bass.ds(t * TS, 2 * P)]).then_inc(xs_ready, 1)
                at(act, ag_transposed, t + 1, passed["act"])
                act.copy(xs[:, 2 * u * TS:2 * u * TS + 2 * P], ptr[:, u, 0:2 * P]).then_inc(xs_ready, 1)
                if not isinstance(t, int) or t:
                    square(t - 1, 1 - u)

            tiles(act, parts)
            square(NT - 1, 1)
            act.wait_ge(ss_done, NT)
            act.activation(ss[:], ss[:], ACT.Sqrt).then_inc(ss_ready, 1)

            def squares(t, u, i):
                at(act, c_ready, t + 1, passed["act"])
                if later(t):
                    at(act, sq_used, t - 1, passed["act"])
                act.activation(sq[:, u * D:(u + 1) * D], Ot(t), ACT.Square).then_inc(sq_ready2, 1)

            tiles(act, squares)
            act.wait_ge(var_ready2, 1)
            act.activation(gv[:], gv[:], ACT.Sqrt).then_inc(sd_ready2, 1)

        @block.tensor
        def _(pe):
            pe.wait_ge(s_in, 80)
            for j in range(2):
                for k in range(2):
                    if j:
                        pe.wait_ge(w_stored, k + 1)
                    for n in range(2):
                        mm = pe.transpose(pt[:, k, n * 128:(n + 1) * 128], wn[:, (2 * j + n) * D + k * 128:(2 * j + n) * D + (k + 1) * 128], ident[:])
                    mm.then_inc(wt_ready, 1)
            pe.wait_ge(w_stored, 4)

            def project(t, u):
                at(pe, xs_ready, 2 * t + 2, passed["pe"])
                if later(t):
                    at(pe, o_ready, t - 1, passed["pe"])
                for j, w in enumerate((wl, wr)):
                    for k in range(2):
                        mm = pe.matmul(pa[0:P, u, 0:D], xs[:, (2 * u + j) * TS + k * P:(2 * u + j) * TS + (k + 1) * P], w[:, k * D:(k + 1) * D],
                                       start=(j == 0 and k == 0), stop=(j == 1 and k == 1))
                mm.then_inc(ab_ready, 1)

            def transpose_ag(t, u, i):
                at(pe, ag_ready, t + 1, passed["pe"])
                if later(t):
                    at(pe, xs_ready, 2 * t - 2, passed["pe"])
                for k in range(2):
                    mm = pe.transpose(ptr[:, u, k * P:(k + 1) * P], ag[:, u * D + k * 128:u * D + (k + 1) * 128], ident[0:P, 0:P])
                mm.then_inc(ag_transposed, 1)
                if not isinstance(t, int) or t:
                    project(t - 1, 1 - u)

            tiles(pe, transpose_ag)
            project(NT - 1, 1)

            def sum_rows(t, u, i):
                at(pe, n_ready, t + 1, passed["pe"])
                mm = pe.matmul(pst[0:P, 0, 0:D], ones[0:P, 0:P], Ot(t), start=(isinstance(t, int) and t == 0), stop=True, skip_group_check=True)
                return mm

            tiles(pe, lambda t, u, i: sum_rows(t, u, i).then_inc(sum_steps, 1))
            pe.wait_ge(sum_steps, NT)
            pe.sem_inc(sum_ready)

            def sum_squares(t, u, i):
                at(pe, sq_ready2, t + 1, passed["pe"])
                pe.matmul(pst[0:P, 1, 0:D], ones[0:P, 0:P], sq[:, u * D:(u + 1) * D], start=(isinstance(t, int) and t == 0), stop=True, skip_group_check=True).then_inc(sq_used, 1)

            tiles(pe, sum_squares)
            pe.wait_ge(sq_used, NT)
            pe.sem_inc(sum_ready)

    end_section()

    def pipelined(eng, body, n):
        for t in range(4):
            body(t, t % 2, t // 2)
        with eng.Fori(2, n // 2) as i:
            body(2 * i, 0, i)
            body(2 * i + 1, 1, i)

    with ExitStack() as ctx:
        KE, NH = EXPERTS, EXP_H // 128
        w1 = sbuf(ctx, "e_w1", [128, KE * 2 * EXP_H])
        w2 = sbuf(ctx, "e_w2", [128, KE * NH * D])
        b1 = sbuf(ctx, "e_b1", [128, KE * NH])
        b2 = sbuf(ctx, "e_b2", [128, KE * D])
        share = sbuf(ctx, "e_share", [P, NT * 2])
        pos_x = sbuf(ctx, "e_pos_x", [P, NT * 2], I32)
        pos_y = sbuf(ctx, "e_pos_y", [P, NT * 2], I32)
        win_e = sbuf(ctx, "e_win_e", [1, NWM], I32)
        win_s = sbuf(ctx, "e_win_s", [1, NWM], I32)
        e_in, w_in = sem("e_in"), sem("e_w_in")

        with ExitStack() as c1:
            wr = sbuf(c1, "e_wr", [128, 2 * KE])
            br = sbuf(c1, "e_br", [P, KE])
            gm = sbuf(c1, "e_gm", [P, D])
            bt = sbuf(c1, "e_bt", [P, D])
            xn = sbuf(c1, "e_xn", [P, 2 * D])
            xs = sbuf(c1, "e_xs", [128, 2 * TS])
            lg = sbuf(c1, "e_lg", [P, NT * KE])
            best = sbuf(c1, "e_best", [P, NT])
            tot = sbuf(c1, "e_tot", [P, NT])
            rank = sbuf(c1, "e_rank", [P, NT * KE])
            prod = sbuf(c1, "e_prod", [P, NT * KE])
            place = sbuf(c1, "e_place", [P, NT * KE])
            cmp = sbuf(c1, "e_cmp", [P, NWM * KE])
            got = sbuf(c1, "e_got", [P, NT])
            e8 = sbuf(c1, "e_e8", [P, 8 * KE])
            e8_i = sbuf(c1, "e_e8_i", [P, KE], I32)
            zero = sbuf(c1, "e_zero", [128, 2 * D])
            xr = sbuf(c1, "e_xr", [P, 2 * D])
            stage = sbuf(c1, "e_stage", [P, 2 * 2], I32)
            ptr = psum(c1, "e_ptr", 2)
            pl = psum(c1, "e_pl", 2)
            pn = psum(c1, "e_pn", 1)
            xn_ready, xn_kept, xt_ready, xs_ready, lg_ready, lg_read, exp_asked, exp_given, n_asked, n_given, zero_set, pad_out, placed, xr_ready = (
                sem("e_" + s) for s in ("xn_ready", "xn_kept", "xt_ready", "xs_ready", "lg_ready", "lg_read", "exp_asked", "exp_given",
                                        "n_asked", "n_given", "zero_set", "pad_out", "placed", "xr_ready"))
            x_scaled = sem("e_x_scaled")
            row_sent = [sem("e_row_sent0"), sem("e_row_sent1")]
            block = c1.enter_context(nc.Block())

            def kept(t):
                return XT[0:P, bass.ds(t * TS, D)]

            @block.sync
            def _(sp):
                for dst, v in ((gm, "gamma"), (bt, "beta"), (br, "br")):
                    sp.dma_start(dst[:], bcast_rows(a["L1_ffn_" + v], P)).then_inc(e_in, 16)
                load_rows(sp, wr[:], a["L1_ffn_Wr"]).then_inc(e_in, 16)
                for e in range(KE):
                    load_rows(sp, w1[:, e * 2 * EXP_H:(e + 1) * 2 * EXP_H], a["L1_ffn_W1"][e]).then_inc(w_in, 16)
                    load_rows(sp, w2[:, e * NH * D:(e + 1) * NH * D], a["L1_ffn_W2"][e]).then_inc(w_in, 16)
                sp.dma_start(b2[:], bcast_rows(a["L1_ffn_b2"].rearrange("e d -> (e d)"), 128)).then_inc(w_in, 16)
                load_cols(sp, b1[:], a["L1_ffn_b1"].rearrange("e h -> (e h)"), KE * NH).then_inc(w_in, 16)
                sp.wait_ge(zero_set, 1)
                sp.dma_start(moe_x_d[2 * N:2 * N + MW, :].rearrange("(p r) c -> p (r c)", p=128), zero[:]).then_inc(pad_out, 16)
                sp.wait_ge(pad_out, 16)
                sp.wait_ge(w_in, 16 * (2 * KE + 2))

            @block.gpsimd
            def _(pool):
                ch = chain("pool", pool)
                pool.memset(zero[:], 0.0).then_inc(zero_set, 1)
                pool.wait_ge(placed, 1)

                def scatter(t, u, i):
                    at(pool, xr_ready, t + 1, passed["pool"])
                    ch.step(pool.tensor_copy(stage[:, 2 * u:2 * u + 2], pos_x[:, bass.ds(t * 2, 2)]))
                    for k in range(2):
                        pool.indirect_dma_start(moe_x_d, bass.IndirectOffsetOnAxis(ap=stage[:, 2 * u + k:2 * u + k + 1].bitcast(U32), axis=0),
                                                xr[:, u * D:(u + 1) * D], None).then_inc(row_sent[u], 16)

                tiles(pool, scatter, ch, 2)
                for u in range(2):
                    pool.wait_ge(row_sent[u], 32 * (NT // 2))

            @block.vector
            def _(dve):
                ch = chain("dve", dve)
                layer_stats(dve, ch, Rt)
                dve.wait_ge(e_in, 64)

                def logits(t, u):
                    at(dve, lg_ready, t + 1, passed["dve"])
                    dve.tensor_tensor(lg[:, bass.ds(t * KE, KE)], pl[0:P, u, 0:KE], br[:], ALU.add).then_inc(lg_read, 1)

                def norm(t, u, i):
                    x_u = xn[:, u * D:(u + 1) * D]
                    if later(t):
                        at(dve, xt_ready, t - 1, passed["dve"])
                        at(dve, xn_kept, t - 1, passed["dve"])
                    dve.tensor_scalar(x_u, Rt(t), mean[:, bass.ds(t, 1)], rstd[:, bass.ds(t, 1)], ALU.subtract, ALU.mult).then_inc(x_scaled, 1)
                    at(dve, x_scaled, t + 1, passed["dve"])
                    ch.step(dve.tensor_tensor(x_u, x_u, gm[:], ALU.mult))
                    dve.tensor_tensor(x_u, x_u, bt[:], ALU.add).then_inc(xn_ready, 1)
                    if later(t):
                        logits(t - 2, u)

                tiles(dve, norm, ch, 2)
                logits(NT - 2, 0)
                logits(NT - 1, 1)
                dve.wait_ge(lg_read, NT)
                l3 = lg[:].rearrange("p (t e) -> p t e", e=KE)
                r3 = rank[:].rearrange("p (t e) -> p t e", e=KE)
                ch.step(dve.memset(rank[:], 0.0))
                for f in range(KE):
                    for lo, hi, op in ((0, f, ALU.is_gt), (f + 1, KE, ALU.is_ge)):
                        if hi > lo:
                            got3 = prod[:].rearrange("p (t e) -> p t e", e=KE)[:, :, lo:hi]
                            ch.step(dve.tensor_tensor(got3, l3[:, :, f:f + 1].to_broadcast([P, NT, hi - lo]), l3[:, :, lo:hi], op))
                            ch.step(dve.tensor_tensor(r3[:, :, lo:hi], r3[:, :, lo:hi], got3, ALU.add))
                p3 = prod[:].rearrange("p (t e) -> p t e", e=KE)
                o3 = place[:].rearrange("p (t e) -> p t e", e=KE)
                cnt, tot8, first8, ends, wins, delta, over = (e8[:, j * KE:(j + 1) * KE] for j in range(7))
                ch.step(dve.tensor_scalar(prod[:], rank[:], 2.0, None, ALU.is_lt))
                ch.step(dve.tensor_reduce(cnt, prod[:].rearrange("p (t e) -> p e t", e=KE), AX.X, ALU.add))
                dve.sem_inc(n_asked)
                ch.step(dve.tensor_reduce(best[:], l3, AX.X, ALU.max))
                ch.step(dve.tensor_tensor(l3, l3, best[:].unsqueeze(2).to_broadcast([P, NT, KE]), ALU.subtract))
                dve.sem_inc(exp_asked)
                dve.wait_ge(exp_given, 1)
                ch.step(dve.tensor_tensor(lg[:], lg[:], prod[:], ALU.mult))
                ch.step(dve.tensor_reduce(tot[:], l3, AX.X, ALU.add))
                ch.step(dve.reciprocal(tot[:], tot[:]))
                ch.step(dve.tensor_tensor(l3, l3, tot[:].unsqueeze(2).to_broadcast([P, NT, KE]), ALU.mult))
                dve.wait_ge(n_given, 1)
                ch.step(dve.tensor_copy(tot8, pn[0:P, 0, 0:KE]))
                ch.step(dve.tensor_tensor_scan(first8, tot8, tot8, 0.0, ALU.add, ALU.bypass))
                ch.step(dve.tensor_tensor(first8, first8, tot8, ALU.subtract))
                ch.step(dve.tensor_scalar(e8_i[:], tot8, float(MW - 1), None, ALU.add))
                ch.step(dve.tensor_scalar(e8_i[:], e8_i[:], MW.bit_length() - 1, None, ALU.arith_shift_right))
                ch.step(dve.tensor_copy(wins, e8_i[:]))
                ch.step(dve.tensor_tensor_scan(ends, wins, wins, 0.0, ALU.add, ALU.bypass))
                ch.step(dve.tensor_tensor(delta, ends, wins, ALU.subtract))
                ch.step(dve.scalar_tensor_tensor(out=delta, in0=delta, scalar=float(MW), in1=first8, op0=ALU.mult, op1=ALU.subtract))
                ch.step(dve.scalar_tensor_tensor(out=over, in0=wins, scalar=-float(MW), in1=tot8, op0=ALU.mult, op1=ALU.add))
                ch.step(dve.scalar_tensor_tensor(out=first8, in0=pn[0:P, 0, 8:8 + KE], scalar=-1.0, in1=first8, op0=ALU.add, op1=ALU.add))
                for e in range(KE):
                    ch.step(dve.tensor_tensor_scan(o3[:, :, e], p3[:, :, e], p3[:, :, e], first8[:, e:e + 1], ALU.add, ALU.bypass))

                def pick(k, values, out):
                    ch.step(dve.tensor_scalar(prod[:], rank[:], float(k), None, ALU.is_equal))
                    ch.step(dve.tensor_tensor(prod[:], prod[:], values, ALU.mult))
                    ch.step(dve.tensor_reduce(got[:], p3, AX.X, ALU.add))
                    ch.step(dve.tensor_copy(out[:].rearrange("p (t k) -> p t k", k=2)[:, :, k], got[:]))

                for k in range(2):
                    pick(k, place[:], pos_x)
                dve.sem_inc(placed)
                for k in range(2):
                    pick(k, lg[:], share)
                ch.step(dve.tensor_tensor(o3, o3, delta.unsqueeze(1).to_broadcast([P, NT, KE]), ALU.add))
                for k in range(2):
                    pick(k, place[:], pos_y)
                c3 = cmp[:].rearrange("p (w e) -> p w e", e=KE)
                ch.step(dve.tensor_tensor(c3, iota_f[0:P, 0:NWM].unsqueeze(2).to_broadcast([P, NWM, KE]),
                                          ends.unsqueeze(1).to_broadcast([P, NWM, KE]), ALU.is_ge))
                ch.step(dve.tensor_reduce(prod[:, 0:NWM], c3, AX.X, ALU.add))
                ch.step(dve.tensor_scalar(win_e[:], prod[0:1, 0:NWM], float(KE - 1), None, ALU.min))
                ch.step(dve.tensor_tensor(c3, c3, over.unsqueeze(1).to_broadcast([P, NWM, KE]), ALU.mult))
                ch.step(dve.tensor_reduce(prod[:, 0:NWM], c3, AX.X, ALU.add))
                ch.step(dve.scalar_tensor_tensor(out=prod[:, 0:NWM], in0=iota_f[0:P, 0:NWM], scalar=float(MW), in1=prod[:, 0:NWM],
                                                 op0=ALU.mult, op1=ALU.add))
                ch.step(dve.tensor_scalar(win_s[:], prod[0:1, 0:NWM], float(2 * N), None, ALU.min))

            @block.scalar
            def _(act):
                finish_stats_act(act)

                def store_xs(t, u, i):
                    at(act, xn_ready, t + 1, passed["act"])
                    act.copy(kept(t), xn[:, u * D:(u + 1) * D]).then_inc(xn_kept, 1)
                    at(act, xt_ready, t + 1, passed["act"])
                    if later(t):
                        at(act, lg_ready, t - 1, passed["act"])
                    act.copy(xs[:, u * TS:u * TS + 2 * P], ptr[:, u, 0:2 * P]).then_inc(xs_ready, 1)

                tiles(act, store_xs)
                act.wait_ge(exp_asked, 1)
                act.activation(lg[:], lg[:], ACT.Exp).then_inc(exp_given, 1)
                act.wait_ge(xn_kept, NT)

                def send(t, u, i):
                    if later(t):
                        at(act, row_sent[u], i * 32, passed["act"])
                    act.copy(xr[:, u * D:(u + 1) * D], kept(t)).then_inc(xr_ready, 1)

                tiles(act, send)

            @block.tensor
            def _(pe):
                pe.wait_ge(e_in, 64)

                def route(t, u):
                    at(pe, xs_ready, t + 1, passed["pe"])
                    if later(t):
                        at(pe, lg_read, t - 1, passed["pe"])
                    for k in range(2):
                        mm = pe.matmul(pl[0:P, u, 0:KE], xs[:, u * TS + k * P:u * TS + (k + 1) * P], wr[:, k * KE:(k + 1) * KE], start=(k == 0), stop=(k == 1))
                    mm.then_inc(lg_ready, 1)

                def transpose_x(t, u, i):
                    at(pe, xn_ready, t + 1, passed["pe"])
                    if later(t):
                        at(pe, xs_ready, t - 1, passed["pe"])
                    for k in range(2):
                        mm = pe.transpose(ptr[:, u, k * P:(k + 1) * P], xn[:, u * D + k * 128:u * D + (k + 1) * 128], ident[0:P, 0:P])
                    mm.then_inc(xt_ready, 1)
                    if not isinstance(t, int) or t:
                        route(t - 1, 1 - u)

                tiles(pe, transpose_x)
                route(NT - 1, 1)
                pe.wait_ge(n_asked, 1)
                pe.matmul(pn[0:P, 0, 0:KE], ones[0:P, 0:P], e8[:, 0:KE], start=True, stop=True)
                pe.matmul(pn[0:P, 0, 8:8 + KE], lower[0:P, 0:P], e8[:, 0:KE], start=True, stop=True).then_inc(n_given, 1)

        with ExitStack() as c2:
            sizes = (2 * 2 * D, 2 * 2 * MW, 2 * 2 * EXP_H, 2 * NH * MW, 2 * 2 * D)
            xw, xT, w1s, hT, yw = (XT[:, sum(sizes[:j]):sum(sizes[:j + 1])] for j in range(5))
            ph = psum(c2, "e_ph", 4)
            py = psum(c2, "e_py", 2)
            pt = psum(c2, "e_pt", 2)
            xw_in = [sem("e_xw_in0"), sem("e_xw_in1")]
            y_out = [sem("e_y_out0"), sem("e_y_out1")]
            transposed, xT_copied, w1_staged, h_ready, h_stored, y_ready, y_added = (
                sem("e_" + s) for s in ("transposed", "xT_copied", "w1_staged", "h_ready", "h_stored", "y_ready", "y_added"))
            block = c2.enter_context(nc.Block())

            @block.sync
            def _(sp):
                def load(t, u, i):
                    start = load_values(sp, win_s, t, 1, 2 * N)[0]
                    if later(t):
                        at(sp, transposed, t - 1, passed["sp"])
                    sp.dma_start(xw[:, u * 2 * D:(u + 1) * 2 * D],
                                 moe_x_d[bass.ds(start, MW), :].rearrange("(p r) c -> p (r c)", p=128)).then_inc(xw_in[u], 16)

                tiles(sp, load, n=NWM)

            @block.gpsimd
            def _(pool):
                def store(t, u, i):
                    at(pool, y_added, 2 * t + 2, passed["pool"])
                    pool.dma_start(moe_y_d[bass.ds(t * MW, MW), :].rearrange("(p r) c -> p (r c)", p=128),
                                   yw[:, u * 2 * D:(u + 1) * 2 * D]).then_inc(y_out[u], 16)

                tiles(pool, store, n=NWM)
                for u in range(2):
                    pool.wait_ge(y_out[u], 16 * (NWM // 2))

            @block.vector
            def _(dve):
                def add(t, u, i):
                    e = load_values(dve, win_e, t, 1, KE - 1)[0]
                    if later(t):
                        at(dve, y_out[u], i * 16, passed["dve"])
                    for v in range(2):
                        at(dve, y_ready, 2 * t + v + 1, passed["dve"])
                        dve.tensor_tensor(yw[:, (2 * u + v) * D:(2 * u + v + 1) * D], py[:, v, 0:D], b2[:, bass.ds(e * D, D)], ALU.add).then_inc(y_added, 1)

                def body(t, u, i):
                    e = load_values(dve, win_e, t, 1, KE - 1)[0]
                    if later(t):
                        at(dve, h_ready, NH * (t - 1), passed["dve"])
                    dve.tensor_copy(w1s[:, u * 2 * EXP_H:(u + 1) * 2 * EXP_H], w1[:, bass.ds(e * 2 * EXP_H, 2 * EXP_H)]).then_inc(w1_staged, 1)
                    if not isinstance(t, int) or t:
                        add(t - 1, 1 - u, i - 1 + u)

                pipelined(dve, body, NWM)
                add(NWM - 1, 1, NWM // 2 - 1)

            @block.scalar
            def _(act):
                def body(t, u, i):
                    e = load_values(act, win_e, t, 1, KE - 1)[0]
                    at(act, transposed, t + 1, passed["act"])
                    act.copy(xT[:, u * 2 * MW:(u + 1) * 2 * MW], pt[:, u, :]).then_inc(xT_copied, 1)
                    if later(t):
                        at(act, y_ready, 2 * t - 2, passed["act"])
                    for m in range(NH):
                        at(act, h_ready, NH * t + m + 1, passed["act"])
                        act.activation(hT[:, (u * NH + m) * MW:(u * NH + m + 1) * MW], ph[:, m, 0:MW], ACT.Gelu,
                                       bias=b1[:, bass.ds(e * NH + m, 1)]).then_inc(h_stored, 1)

                tiles(act, body, n=NWM)

            @block.tensor
            def _(pe):
                def second(t, u):
                    e = load_values(pe, win_e, t, 1, KE - 1)[0]
                    at(pe, h_stored, NH * (t + 1), passed["pe"])
                    for v in range(2):
                        if not isinstance(t, int) or t:
                            at(pe, y_added, 2 * t + v - 1, passed["pe"])
                        for m in range(NH):
                            mm = pe.matmul(py[:, v, 0:D], hT[:, (u * NH + m) * MW + v * 128:(u * NH + m) * MW + (v + 1) * 128],
                                           w2[:, bass.ds((e * NH + m) * D, D)], start=(m == 0), stop=(m == NH - 1))
                        mm.then_inc(y_ready, 1)

                def body(t, u, i):
                    at(pe, xw_in[u], i * 16 + 16, passed["pe"])
                    if later(t):
                        at(pe, xT_copied, t - 1, passed["pe"])
                    for k in range(2):
                        for v in range(2):
                            mm = pe.transpose(pt[:, u, k * MW + v * 128:k * MW + (v + 1) * 128],
                                              xw[:, (2 * u + v) * D + k * 128:(2 * u + v) * D + (k + 1) * 128], ident[:])
                    mm.then_inc(transposed, 1)
                    if not isinstance(t, int) or t:
                        second(t - 1, 1 - u)
                    at(pe, w1_staged, t + 1, passed["pe"])
                    at(pe, xT_copied, t + 1, passed["pe"])
                    for m in range(NH):
                        for k in range(2):
                            mm = pe.matmul(ph[:, m, 0:MW], w1s[:, (2 * u + k) * EXP_H + m * 128:(2 * u + k) * EXP_H + (m + 1) * 128],
                                           xT[:, (2 * u + k) * MW:(2 * u + k + 1) * MW], start=(k == 0), stop=(k == 1))
                        mm.then_inc(h_ready, 1)

                tiles(pe, body, n=NWM)
                second(NWM - 1, 1)

        with ExitStack() as c3:
            yg = sbuf(c3, "e_yg", [P, 4 * 2 * D])
            stage = sbuf(c3, "e_stage2", [P, 4 * 2], I32)
            yg_in = [sem(f"e_yg_in{u}") for u in range(4)]
            written = [sem("written0"), sem("written1")]
            yg_used = sem("e_yg_used")
            block = c3.enter_context(nc.Block())

            def fours(eng, body, ch=None, per=0):
                for t in range(4):
                    body(t, t, 0)
                with eng.Fori(1, NT // 4) as i:
                    if ch:
                        ch.base -= 4 * per
                        ch.enter(i, 4 * per)
                    for u in range(4):
                        body(4 * i + u, u, i)
                if ch:
                    ch.base += 4 * per
                    ch.leave(NT // 4 - 1)
                for t in range(NT // 4 * 4, NT):
                    body(t, t % 4, t // 4)

            @block.gpsimd
            def _(pool):
                ch = chain("pool", pool)

                def gather(t, u, i):
                    if not isinstance(t, int) or t >= 4:
                        at(pool, yg_used, t - 3, passed["pool"])
                    ch.step(pool.tensor_copy(stage[:, 2 * u:2 * u + 2], pos_y[:, bass.ds(t * 2, 2)]))
                    for k in range(2):
                        pool.indirect_dma_start(yg[:, (2 * u + k) * D:(2 * u + k + 1) * D], None, moe_y_d,
                                                bass.IndirectOffsetOnAxis(ap=stage[:, 2 * u + k:2 * u + k + 1].bitcast(U32), axis=0)
                                                ).then_inc(yg_in[u], 16)

                fours(pool, gather, ch, 1)

            @block.vector
            def _(dve):
                ch = chain("dve", dve)

                def add(t, u, i):
                    at(dve, yg_in[u], i * 32 + 32, passed["dve"])
                    for k in range(2):
                        ch.step(dve.scalar_tensor_tensor(out=Rt(t), in0=yg[:, (2 * u + k) * D:(2 * u + k + 1) * D],
                                                         scalar=share[:, bass.ds(t * 2 + k, 1)], in1=Rt(t), op0=ALU.mult, op1=ALU.add))
                    dve.sem_inc(yg_used)

                fours(dve, add, ch, 2)

            @block.sync
            def _(sp):
                def store(t, u, i):
                    at(sp, yg_used, t + 1, passed["sp"])
                    sp.dma_start(out[bass.ds(t * P, P), :], Rt(t)).then_inc(written[u], 16)

                tiles(sp, store)
                for u in range(2):
                    sp.wait_ge(written[u], 16 * (NT // 2))
    top.close()


def kernel(**inputs):
    import numpy as np
    import concourse.bacc as bacc
    from concourse.bass_utils import run_bass_kernel_spmd

    nc = bacc.Bacc("TRN2", target_bir_lowering=False, num_devices=1)
    arrays, args = {}, {}
    for name, value in inputs.items():
        value = np.ascontiguousarray(value)
        arrays[f"in_{name}"] = value
        args[name] = nc.dram_tensor(f"in_{name}", value.shape, mybir.dt.from_np(value.dtype), kind="ExternalInput").ap()
    out = nc.dram_tensor("out_nodes", (N, D), F32, kind="ExternalOutput").ap()
    program(nc, args, out)
    result = run_bass_kernel_spmd(nc, [arrays], core_ids=[0])
    return result.results[0]["out_nodes"]
```
